# Optimizing a Trainium2 kernel written in Bass

```python
import numpy as np
import jax
import jax.numpy as jnp

def _softmax(x, axis=-1):
    return jax.nn.softmax(x, axis=axis)

def _gelu(x):
    return jax.nn.gelu(x, approximate=True)

def _silu(x):
    return jax.nn.silu(x)

def _sigmoid(x):
    return jax.nn.sigmoid(x)

def _layernorm(x, axis=-1, eps=1e-05):
    m = jnp.mean(x, axis=axis, keepdims=True)
    v = jnp.var(x, axis=axis, keepdims=True)
    return (x - m) / jnp.sqrt(v + eps)

def _scatter_add(tgt, idx, src, axis=0):
    return tgt.at[idx].add(src)

def _segment_sum(src, seg, n):
    return jax.ops.segment_sum(src, seg, n)
kernel_name = 'mk_prb_d1_jaxref_r4_77c3dc'

def setup_inputs(seed: int=0):
    np.random.seed(seed)
    _w = jnp.asarray

    def _L0_attn_setup():
        import jax, jax.numpy as jnp
        import numpy as np
        B, S, DIN, DIM = (1, 1024, 256, 256)
        NH, NKV = (16, 4)
        HD = DIM // NH
        GS = NH // NKV
        key = jax.random.key(seed)
        ks = jax.random.split(key, 5)

        def w(k, shape, fan_in):
            return jax.random.normal(k, shape, jnp.float32) * fan_in ** (-0.5)
        return {'x': jax.random.normal(ks[0], (B, S, DIN), jnp.float32), 'wq': w(ks[1], (DIM, DIN), DIN), 'wk': w(ks[2], (NKV * HD, DIN), DIN), 'wv': w(ks[3], (NKV * HD, DIN), DIN), 'wo': w(ks[4], (DIM, DIM), DIM)}
    _L0_attn_in = _L0_attn_setup()

    def _L0_ffn_setup():
        import jax, jax.numpy as jnp
        import numpy as np
        B, N, D = (4, 1024, 256)
        E, S, F = (16, 64, 512)
        DO = 256
        EPS = 1e-05

        def _layernorm(x, g, b):
            mu = jnp.mean(x, axis=-1, keepdims=True)
            var = jnp.mean(jnp.square(x - mu), axis=-1, keepdims=True)
            return (x - mu) * jax.lax.rsqrt(var + EPS) * g + b
        key = jax.random.key(seed)
        ks = jax.random.split(key, 8)
        d = {'x': jax.random.normal(ks[0], (B, N, D), dtype=jnp.float32), 'norm_g': jnp.ones((D,), jnp.float32), 'norm_b': jnp.zeros((D,), jnp.float32), 'slot_g': jnp.ones((D,), jnp.float32), 'slot_b': jnp.zeros((D,), jnp.float32), 'scale': jnp.ones((1,), jnp.float32), 'slot_embeds': jax.random.normal(ks[1], (E, S, D), jnp.float32) / np.sqrt(D), 'Wg': jax.random.normal(ks[2], (E, D, F), jnp.float32) * np.sqrt(2.0 / (D + F)), 'bg': jnp.zeros((E, F), jnp.float32), 'Wu': jax.random.normal(ks[3], (E, D, F), jnp.float32) * np.sqrt(2.0 / (D + F)), 'bu': jnp.zeros((E, F), jnp.float32), 'Wd': jax.random.normal(ks[4], (E, F, DO), jnp.float32) * np.sqrt(2.0 / (F + DO)), 'bd': jnp.zeros((E, DO), jnp.float32)}
        return d
    _L0_ffn_in = _L0_ffn_setup()
    _d = {'L0_attn_x': _L0_attn_in['x'], 'L0_attn_wq': _L0_attn_in['wq'], 'L0_attn_wk': _L0_attn_in['wk'], 'L0_attn_wv': _L0_attn_in['wv'], 'L0_attn_wo': _L0_attn_in['wo'], 'L0_ffn_norm_g': _L0_ffn_in['norm_g'], 'L0_ffn_norm_b': _L0_ffn_in['norm_b'], 'L0_ffn_slot_g': _L0_ffn_in['slot_g'], 'L0_ffn_slot_b': _L0_ffn_in['slot_b'], 'L0_ffn_scale': _L0_ffn_in['scale'], 'L0_ffn_slot_embeds': _L0_ffn_in['slot_embeds'], 'L0_ffn_Wg': _L0_ffn_in['Wg'], 'L0_ffn_bg': _L0_ffn_in['bg'], 'L0_ffn_Wu': _L0_ffn_in['Wu'], 'L0_ffn_bu': _L0_ffn_in['bu'], 'L0_ffn_Wd': _L0_ffn_in['Wd'], 'L0_ffn_bd': _L0_ffn_in['bd']}
    _x0 = _d['L0_attn_x']
    _d['L0_attn_x'] = jax.random.normal(jax.random.fold_in(jax.random.key(seed), 1), (4, 2048, 256), dtype=_x0.dtype)
    del _x0
    return _d

def reference(L0_attn_x, L0_attn_wq, L0_attn_wk, L0_attn_wv, L0_attn_wo, L0_ffn_norm_g, L0_ffn_norm_b, L0_ffn_slot_g, L0_ffn_slot_b, L0_ffn_scale, L0_ffn_slot_embeds, L0_ffn_Wg, L0_ffn_bg, L0_ffn_Wu, L0_ffn_bu, L0_ffn_Wd, L0_ffn_bd):

    def _L0_attn_ref(x, wq, wk, wv, wo):
        import jax, jax.numpy as jnp
        import numpy as np
        B, S, DIN, DIM = (1, 1024, 256, 256)
        NH, NKV = (16, 4)
        HD = DIM // NH
        GS = NH // NKV
        b, s, _ = x.shape
        q = (x @ wq.T).reshape(b, s, NKV, GS, HD)
        k = (x @ wk.T).reshape(b, s, NKV, HD)
        v = (x @ wv.T).reshape(b, s, NKV, HD)
        scale = jnp.asarray(HD ** 0.5, x.dtype)
        att = jnp.einsum('bsgmd,btgd->bgmst', q, k) / scale
        causal = jnp.triu(jnp.ones((s, s), bool), 1)
        att = jnp.where(causal, -jnp.inf, att)
        att = jax.nn.softmax(att, axis=-1)
        ctx = jnp.einsum('bgmst,btgd->bsgmd', att, v).reshape(b, s, DIM)
        return ctx @ wo.T

    def _L0_ffn_ref(x, norm_g, norm_b, slot_g, slot_b, scale, slot_embeds, Wg, bg, Wu, bu, Wd, bd):
        import jax, jax.numpy as jnp
        import numpy as np
        B, N, D = (4, 1024, 256)
        E, S, F = (16, 64, 512)
        DO = 256
        EPS = 1e-05

        def _layernorm(x, g, b):
            mu = jnp.mean(x, axis=-1, keepdims=True)
            var = jnp.mean(jnp.square(x - mu), axis=-1, keepdims=True)
            return (x - mu) * jax.lax.rsqrt(var + EPS) * g + b
        x = _layernorm(x, norm_g, norm_b)
        se = _layernorm(slot_embeds, slot_g, slot_b) * scale
        logits = jnp.einsum('bnd,esd->bnes', x, se)
        dispatch = jax.nn.softmax(logits, axis=1)
        combine = jax.nn.softmax(logits.reshape(x.shape[0], x.shape[1], -1), axis=-1)
        slots = jnp.einsum('bnd,bnes->besd', x, dispatch)
        gate = jax.nn.gelu(jnp.einsum('besd,edf->besf', slots, Wg) + bg[None, :, None, :], approximate=False)
        up = jnp.einsum('besd,edf->besf', slots, Wu) + bu[None, :, None, :]
        eout = jnp.einsum('besf,efo->beso', gate * up, Wd) + bd[None, :, None, :]
        eout = eout.reshape(eout.shape[0], -1, eout.shape[-1])
        return jnp.einsum('bns,bso->bno', combine, eout)
    x = L0_attn_x
    xn = _layernorm(x, axis=-1)
    x = x + _L0_attn_ref(xn, L0_attn_wq, L0_attn_wk, L0_attn_wv, L0_attn_wo) + _L0_ffn_ref(xn, L0_ffn_norm_g, L0_ffn_norm_b, L0_ffn_slot_g, L0_ffn_slot_b, L0_ffn_scale, L0_ffn_slot_embeds, L0_ffn_Wg, L0_ffn_bg, L0_ffn_Wu, L0_ffn_bu, L0_ffn_Wd, L0_ffn_bd)
    return x

_drawn_inputs = setup_inputs


def setup_inputs(seed=0):
    import zlib

    import numpy as np

    out = dict(_drawn_inputs(seed))
    spreads = {'L0_ffn_norm_g': (1.0, 0.2),
     'L0_ffn_norm_b': (0.0, 0.1),
     'L0_ffn_slot_g': (1.0, 0.2),
     'L0_ffn_slot_b': (0.0, 0.1),
     'L0_ffn_bg': (0.0, 0.1),
     'L0_ffn_bu': (0.0, 0.1),
     'L0_ffn_bd': (0.0, 0.1)}
    factors = {}
    for name, (base, spread) in spreads.items():
        noise = np.random.default_rng([zlib.crc32(name.encode()), seed]).standard_normal(out[name].shape)
        drawn = base * np.exp(spread * noise) if base else spread * noise
        out[name] = jnp.asarray(drawn.astype(out[name].dtype))
    for name, factor in factors.items():
        out[name] = (out[name] * factor).astype(out[name].dtype)
    return out
```

```python
from contextlib import ExitStack

import concourse.bass as bass
from concourse import mybir

ALU = mybir.AluOpType
ACT = mybir.ActivationFunctionType
AX = mybir.AxisListType
F32 = mybir.dt.float32
BF16 = mybir.dt.bfloat16
RMAX = bass.bass_isa.ReduceOp.max

P = 128
B, S, D = 4, 2048, 256
NH, NKV, HD = 16, 4, 16
GS = NH // NKV
E, SL, F = 16, 64, 512
NS = E * SL
DK = D // P
EPS = 1e-5
LOW = -3.0e38
TOK = B * S
CH = 512
TPC = CH // P
CPB = S // CH
NCH = TOK // CH
TPB = S // P
SB = NS // P
Q_PART = (0, 0, 1, 1, 0, 2)
K_PART = (0, 1, 0, 1, 2, 0)
KR = HD * len(Q_PART)
VW = 32


class Alloc:

    def __init__(self, nc, ctx, tag):
        self.nc, self.ctx, self.tag = nc, ctx, tag

    def sb(self, name, shape, dt=F32):
        return self.ctx.enter_context(self.nc.sbuf_tensor(f"{self.tag}_{name}", shape, dt))

    def ps(self, name, shape, dt=F32):
        return self.ctx.enter_context(self.nc.psum_tensor(f"{self.tag}_{name}", shape, dt))

    def sem(self, name):
        return self.ctx.enter_context(self.nc.semaphore(f"{self.tag}_{name}"))


def wait_apart(eng, sem, value, passed):
    eng.wait_ge(sem, value)
    eng.sem_inc(passed, 1)


def prepare(nc, w, io):
    with ExitStack() as ctx:
        a = Alloc(nc, ctx, "prep")
        wq, wo = a.sb("wq", [P, DK, D]), a.sb("wo", [P, DK, D])
        wkv = a.sb("wkv", [P, D])
        se = a.sb("se", [P, SB, D])
        sg, sbb, sc = a.sb("sg", [P, D]), a.sb("sbb", [P, D]), a.sb("sc", [P, 1])
        bgr, bur = a.sb("bgr", [E, F]), a.sb("bur", [E, F])
        st, mv, rs = a.sb("st", [P, SB, 6]), a.sb("mv", [P, SB, 2]), a.sb("rs", [P, SB])
        bank = a.ps("bank", [P, 8, 512])
        loaded, zeroed, made = a.sem("loaded"), a.sem("zeroed"), a.sem("made")
        rooted = a.sem("rooted")
        step, scaled, turned, kept = a.sem("step"), a.sem("scaled"), a.sem("turned"), a.sem("kept")
        ident, identb = w["ident"], w["identb"]
        NLOAD = 15

        jobs = []
        jobs.append(([(wq[:, m, k * P:(k + 1) * P], P, (k * DK + m) * P) for k in range(DK) for m in range(DK)],
                     w["wqT"][:, :, :].rearrange("p k n -> p (k n)"), P))
        jobs.append(([(wkv[:, k * P:(k + 1) * P], P, k * P) for k in range(DK)],
                     w["wkvT"][:, :, :].rearrange("p k n -> p (k n)"), P))
        jobs.append(([(wo[:, m, k * P:(k + 1) * P], P, (k * DK + m) * P) for k in range(DK) for m in range(DK)],
                     w["woT"][:, :, :].rearrange("p k n -> p (k n)"), P))
        jobs.append(([(bgr[:, f * P:(f + 1) * P], E, f * E) for f in range(F // P)],
                     w["bgT"][:, :, :].rearrange("p f e -> p (f e)"), P))
        jobs.append(([(bur[:, f * P:(f + 1) * P], E, f * E) for f in range(F // P)],
                     w["buT"][:, :, :].rearrange("p f e -> p (f e)"), P))
        for k in range(DK):
            for h in range(SB // 4):
                jobs.append(([(se[:, 4 * h + j, k * P:(k + 1) * P], P, j * P) for j in range(4)],
                             w["seT"][:, k, h * 512:(h + 1) * 512], P))

        with nc.Block() as block:
            @block.sync
            def _(sp):
                pm = lambda t: t.rearrange("(m p) d -> p m d", p=P)
                sp.dma_start(wq[:], pm(io["wq"])).then_inc(loaded, 16)
                sp.dma_start(wkv[0:64, :], io["wv"]).then_inc(loaded, 16)
                sp.dma_start(wkv[64:128, :], io["wk"]).then_inc(loaded, 16)
                sp.dma_start(wo[:], pm(io["wo"])).then_inc(loaded, 16)
                sp.dma_start(se[:], pm(io["slot_embeds"].rearrange("e s d -> (e s) d"))).then_inc(loaded, 16)
                sp.dma_start(bgr[:], io["bg"]).then_inc(loaded, 16)
                sp.dma_start(bur[:], io["bu"]).then_inc(loaded, 16)
                for t, v in ((sg, "slot_g"), (sbb, "slot_b"), (w["ng"], "norm_g"), (w["nb"], "norm_b")):
                    for h in range(2):
                        sp.dma_start(t[:, h * P:(h + 1) * P],
                                     io[v][h * P:(h + 1) * P].partition_broadcast(P)).then_inc(loaded, 16)
                sp.dma_start(sc[:], io["scale"].partition_broadcast(P)).then_inc(loaded, 16)

            @block.gpsimd
            def _(pool):
                nc.gpsimd.memset(w["power"][:], -0.5).then_inc(zeroed, 1)
                nc.gpsimd.memset(ident[:], 0.0).then_inc(zeroed, 1)
                pool.wait_ge(zeroed, 2)
                nc.gpsimd.affine_select(out=ident[:], in_=ident[:], compare_op=ALU.not_equal, fill=1.0, base=0,
                                        pattern=[[-1, P]], channel_multiplier=1).then_inc(made, 1)
                nc.gpsimd.memset(w["causal"][:], 0.0).then_inc(zeroed, 1)
                pool.wait_ge(zeroed, 3)
                tri = w["causal"][:, CH - P:CH]
                nc.gpsimd.affine_select(out=tri, in_=tri, compare_op=ALU.is_ge, fill=LOW, base=0,
                                        pattern=[[-1, P]], channel_multiplier=1).then_inc(made, 1)
                pool.wait_ge(made, 1)
                nc.gpsimd.tensor_copy(identb[:], ident[:]).then_inc(made, 1)
                pool.wait_ge(step, 2 * SB)
                nc.gpsimd.tensor_scalar(rs[:], mv[:, :, 1], EPS, None, ALU.add).then_inc(made, 1)
                pool.wait_ge(made, 4)
                nc.gpsimd.tensor_tensor(rs[:], rs[:], w["power"][:], ALU.pow).then_inc(rooted, 1)

            @block.vector
            def _(dve):
                n = 0

                def after(ins):
                    nonlocal n
                    ins.then_inc(step, 1)
                    n += 1

                dve.wait_ge(loaded, 16 * (NLOAD + 1))
                for t in range(SB):
                    after(nc.vector.bn_stats(st[:, t, :], se[:, t, :]))
                dve.wait_ge(step, n)
                for t in range(SB):
                    after(nc.vector.bn_aggr(mv[:, t, :], st[:, t, :]))
                dve.wait_ge(step, n)
                dve.wait_ge(rooted, 1)
                for t in range(SB):
                    after(nc.vector.tensor_scalar(se[:, t, :], se[:, t, :], mv[:, t, 0:1], rs[:, t:t + 1],
                                                  ALU.subtract, ALU.mult))
                dve.wait_ge(step, n)
                for t in range(SB):
                    after(nc.vector.tensor_tensor(se[:, t, :], se[:, t, :], sg[:], ALU.mult))
                dve.wait_ge(step, n)
                for t in range(SB):
                    after(nc.vector.tensor_tensor(se[:, t, :], se[:, t, :], sbb[:], ALU.add))
                dve.wait_ge(step, n)
                for t in range(SB):
                    nc.vector.tensor_scalar(se[:, t, :], se[:, t, :], sc[:, 0:1], None, ALU.mult).then_inc(scaled, 1)
                for i, (parts, dest, _) in enumerate(jobs):
                    dve.wait_ge(turned, i + 1)
                    src = bank[:, i % 8, 0:dest.shape[1]]
                    if i == 0:
                        for k in range(DK):
                            ins = nc.vector.tensor_copy(
                                w["wqT"][:, k, :].rearrange("p (g d h) -> p g h d", g=NKV, h=GS),
                                bank[:, 0, k * D:(k + 1) * D].rearrange("p (g h d) -> p g h d", g=NKV, h=GS))
                        ins.then_inc(kept, 1)
                    else:
                        nc.vector.tensor_copy(dest, src).then_inc(kept, 1)

            @block.tensor
            def _(pe):
                pe.wait_ge(made, 3)
                pe.wait_ge(loaded, 16 * (NLOAD + 1))
                for i, (parts, dest, _) in enumerate(jobs):
                    if i == 5:
                        pe.wait_ge(scaled, SB)
                    if i >= 8:
                        pe.wait_ge(kept, i - 7)
                    for src, rows, col in parts:
                        last = nc.tensor.transpose(bank[:, i % 8, col:col + rows], src, ident[0:rows, 0:rows])
                    last.then_inc(turned, 1)


def project(nc, w, io, scr):
    with ExitStack() as ctx:
        a = Alloc(nc, ctx, "proj")
        passed = a.sem("passed")
        x = a.sb("x", [P, 2, TPC, D])
        xn = a.sb("xn", [P, 2, TPC, D])
        y = a.sb("y", [P, 2, TPC, D])
        st, mv, rs = a.sb("st", [P, TPC, 6]), a.sb("mv", [P, 2, TPC, 2]), a.sb("rs", [P, 2, TPC])
        xT = a.sb("xT", [P, DK, CH])
        yT = a.sb("yT", [P, 2, DK, CH])
        part = a.sb("part", [P, 2, 3, 3, CH], BF16)
        rest = a.sb("rest", [P, 3, CH])
        vT = a.sb("vT", [64, CH])
        v = a.sb("v", [P, 2, NKV, TPC, VW])
        xTp = a.ps("xTp", [P, DK, CH])
        yTp = a.ps("yTp", [P, DK, CH])
        pj = a.ps("pj", [P, 3, CH])
        vp = a.ps("vp", [P, TPC, 2 * 64])
        sem = a.sem
        x_in = [sem(f"x_in{q}") for q in range(2)]
        out = [sem(f"out{q}") for q in range(2)]
        rs_ready, eps_added = sem("rs_ready"), sem("eps_added")
        ln_step, xn_ready, y0_ready, y_step, y_ready = (sem(n) for n in
                                                        ("ln_step", "xn_ready", "y0_ready", "y_step", "y_ready"))
        xT_ready, xT_kept, yT_ready, yT_kept = (sem(n) for n in ("xT_ready", "xT_kept", "yT_ready", "yT_kept"))
        pj_ready, p1_ready, rest_ready, p2_ready, p3_ready = (
            sem(n) for n in ("pj_ready", "p1_ready", "rest_ready", "p2_ready", "p3_ready"))
        vT_ready, vp_ready, v_ready, v_ones, v_init = (sem(n) for n in ("vT_ready", "vp_ready", "v_ready", "v_ones", "v_init"))
        NOUT = 6
        LN_STEPS = 2 * 2 * TPC
        credits = [(xn_ready, 2 * TPC), (xT_kept, DK), (yT_kept, DK), (rest_ready, 3),
                   (p3_ready, 3), (v_ready, 1), (vp_ready, 1), (out[0], 16 * NOUT), (out[1], 16 * NOUT),
                   (yT_ready, 2 * DK)]
        idn = w["ident"]
        rows = lambda s: slice(64, 128) if s == 2 else slice(0, 128)

        with nc.Block() as block:
            @block.sync
            def _(sp):
                for s, n in credits:
                    sp.sem_inc(s, n)
                load = lambda i, j, q: sp.dma_start(x[:, q], io["x"][i]).then_inc(x_in[q], 16)
                load(0, 0, 0)
                load(1, 0, 1)

                def chunk(i, j, q, more):
                    sp.wait_ge(y_ready, i * TPC + TPC)
                    sp.dma_start(scr["y"][i], y[:, q]).then_inc(out[q], 16)
                    if more:
                        sp.wait_ge(xn_ready, (i + 2) * TPC + TPC)
                        load(i + 2, j + 1, q)
                    wait_apart(sp, p3_ready, 3 * i + 6, passed)
                    for m in range(2):
                        sp.dma_start(scr["q_out"][i, m], part[:, q, m]).then_inc(out[q], 16)
                    sp.dma_start(scr["k_out"][i], part[64:128, q, 2]).then_inc(out[q], 16)
                    sp.wait_ge(v_ready, i + 2)
                    sp.dma_start(scr["v_out"][i], v[:, q].rearrange("p g t c -> p (g t c)")).then_inc(out[q], 16)
                    sp.wait_ge(yT_kept, DK * i + 2 * DK)
                    sp.dma_start(scr["yT_out"][i], yT[:, q]).then_inc(out[q], 16)

                with sp.Fori(0, NCH // 2 - 1) as j:
                    for q in range(2):
                        chunk(2 * j + q, j, q, True)
                for q in range(2):
                    chunk(NCH - 2 + q, NCH // 2 - 1, q, False)
                for q in range(2):
                    sp.wait_ge(out[q], 16 * NOUT * (NCH // 2 + 1))

            @block.vector
            def _(dve):
                nc.vector.memset(v[:], 0.0).then_inc(v_init, 1)
                dve.wait_ge(v_init, 1)
                nc.vector.memset(v[:, :, :, :, HD:HD + 1], 1.0).then_inc(v_ones, 1)

                def norms(i, j, q):
                    base = i * LN_STEPS
                    n = 0
                    dve.wait_ge(x_in[q], 16 * j + 16)
                    for r, src in enumerate((x, xn)):
                        if r:
                            dve.wait_ge(xn_ready, i * TPC + 3 * TPC)
                        for t in range(TPC):
                            nc.vector.bn_stats(st[:, t, :], src[:, q, t]).then_inc(ln_step, 1)
                        n += TPC
                        wait_apart(dve, ln_step, base + n, passed)
                        for t in range(TPC):
                            nc.vector.bn_aggr(mv[:, r, t, :], st[:, t, :]).then_inc(ln_step, 1)
                        n += TPC
                        dve.wait_ge(ln_step, base + n)
                        dve.wait_ge(rs_ready, 2 * i + r + 1)
                        if r == 0:
                            dve.wait_ge(xT_ready, DK * (i - 2) + DK) if not isinstance(i, int) or i >= 2 else None
                        else:
                            dve.wait_ge(out[q], 16 * NOUT * j + 16 * NOUT)
                        dst, ready = ((xn, xn_ready), (y, y0_ready))[r]
                        for t in range(TPC):
                            nc.vector.tensor_scalar(dst[:, q, t], src[:, q, t], mv[:, r, t, 0:1], rs[:, r, t:t + 1],
                                                    ALU.subtract, ALU.mult).then_inc(ready, 1)

                def splits(i, q):
                    for s in range(3):
                        dve.wait_ge(p1_ready, 3 * i + s + 1)
                        dve.wait_ge(p3_ready, 3 * i + s + 1)
                        r = rows(s)
                        nc.vector.tensor_tensor(rest[r, s, :], pj[r, s, :], part[r, q, s, 0, :],
                                                ALU.subtract).then_inc(rest_ready, 1)

                norms(0, 0, 0)
                norms(1, 0, 1)
                splits(0, 0)
                with dve.Fori(1, NCH // 2) as j:
                    norms(2 * j, j, 0)
                    splits(2 * j - 1, 1)
                    norms(2 * j + 1, j, 1)
                    splits(2 * j, 0)
                splits(NCH - 1, 1)

            @block.gpsimd
            def _(pool):
                def gains(i, q):
                    for r in range(2):
                        wait_apart(pool, ln_step, i * LN_STEPS + (r + 1) * 2 * TPC, passed)
                        nc.gpsimd.tensor_scalar(rs[:, r], mv[:, r, :, 1], EPS, None, ALU.add).then_inc(eps_added, 1)
                        pool.wait_ge(eps_added, 2 * i + r + 1)
                        nc.gpsimd.tensor_tensor(rs[:, r], rs[:, r], w["power"][:, 0:TPC],
                                                ALU.pow).then_inc(rs_ready, 1)
                    for t in range(TPC):
                        pool.wait_ge(y0_ready, i * TPC + t + 1)
                        nc.gpsimd.tensor_tensor(y[:, q, t], y[:, q, t], w["ng"][:], ALU.mult).then_inc(y_step, 1)
                    for t in range(TPC):
                        pool.wait_ge(y_step, i * TPC + t + 1)
                        nc.gpsimd.tensor_tensor(y[:, q, t], y[:, q, t], w["nb"][:], ALU.add).then_inc(y_ready, 1)

                def thirds(i, q):
                    for s in range(3):
                        pool.wait_ge(p2_ready, 3 * i + s + 1)
                        pool.wait_ge(p3_ready, 3 * i + s + 3)
                        r = rows(s)
                        nc.gpsimd.tensor_tensor(part[r, q, s, 2, :], rest[r, s, :], part[r, q, s, 1, :],
                                                ALU.subtract).then_inc(p3_ready, 1)
                    pool.wait_ge(p3_ready, 3 * i + 6)

                gains(0, 0)
                gains(1, 1)
                thirds(0, 0)
                with pool.Fori(1, NCH // 2) as j:
                    gains(2 * j, 0)
                    thirds(2 * j - 1, 1)
                    gains(2 * j + 1, 1)
                    thirds(2 * j, 0)
                thirds(NCH - 1, 1)

            @block.scalar
            def _(act):
                act.wait_ge(v_ones, 1)

                def chunk(i, j, q):
                    act.wait_ge(pj_ready, 3 * i) if not isinstance(i, int) or i > 0 else None
                    for k in range(DK):
                        act.wait_ge(xT_ready, DK * i + k + 1)
                        nc.scalar.copy(xT[:, k, :], xTp[:, k, :]).then_inc(xT_kept, 1)
                    act.wait_ge(out[q], 16 * NOUT * j + 16 * NOUT)
                    for s in range(3):
                        r = rows(s)
                        act.wait_ge(pj_ready, 3 * i + s + 1)
                        if s == 2:
                            act.wait_ge(vp_ready, i + 1)
                            nc.scalar.copy(vT[:, :], pj[0:64, 2, :]).then_inc(vT_ready, 1)
                        nc.scalar.copy(part[r, q, s, 0, :], pj[r, s, :]).then_inc(p1_ready, 1)
                    for k in range(DK):
                        act.wait_ge(yT_ready, DK * (i + 2) + k + 1)
                        nc.scalar.copy(yT[:, q, k, :], yTp[:, k, :]).then_inc(yT_kept, 1)
                    for s in range(3):
                        r = rows(s)
                        act.wait_ge(rest_ready, 3 * i + 3 + s + 1)
                        nc.scalar.copy(part[r, q, s, 1, :], rest[r, s, :]).then_inc(p2_ready, 1)
                    act.wait_ge(vp_ready, i + 2)
                    nc.scalar.copy(v[:, q, :, :, 0:HD],
                                   vp[:, :, 0:64].rearrange("p t (g d) -> p g t d", g=NKV)).then_inc(v_ready, 1)

                chunk(0, 0, 0)
                chunk(1, 0, 1)
                with act.Fori(1, NCH // 2) as j:
                    for q in range(2):
                        chunk(2 * j + q, j, q)

            @block.tensor
            def _(pe):
                def chunk(i, q):
                    pe.wait_ge(xn_ready, i * TPC + 3 * TPC)
                    for k in range(DK):
                        pe.wait_ge(xT_kept, DK * i + k + 1)
                        for t in range(TPC):
                            last = nc.tensor.transpose(xTp[:, k, t * P:(t + 1) * P], xn[:, q, t, k * P:(k + 1) * P],
                                                       idn[:])
                        last.then_inc(xT_ready, 1)
                    pe.wait_ge(y_ready, i * TPC + TPC)
                    for k in range(DK):
                        pe.wait_ge(yT_kept, DK * i + k + 1)
                        for t in range(TPC):
                            last = nc.tensor.transpose(yTp[:, k, t * P:(t + 1) * P], y[:, q, t, k * P:(k + 1) * P],
                                                       idn[:])
                        last.then_inc(yT_ready, 1)
                    pe.wait_ge(xT_kept, DK * i + 2 * DK)
                    for s in range(3):
                        pe.wait_ge(rest_ready, 3 * i + s + 1)
                        for k in range(DK):
                            lhsT = w["wqT"][:, k, s * P:(s + 1) * P] if s < 2 else w["wkvT"][:, k, :]
                            last = nc.tensor.matmul(pj[:, s, :], lhsT, xT[:, k, :], start=(k == 0), stop=(k == DK - 1))
                        last.then_inc(pj_ready, 1)
                    pe.wait_ge(v_ready, i + 1)
                    wait_apart(pe, vT_ready, i + 1, passed)
                    for t in range(TPC):
                        last = nc.tensor.transpose(vp[:, t, 0:64], vT[:, t * P:(t + 1) * P], idn[0:64, 0:64])
                    last.then_inc(vp_ready, 1)

                with pe.Fori(0, NCH // 2) as j:
                    for q in range(2):
                        chunk(2 * j + q, q)


def attend(nc, w, scr):
    UNITS = [(c, kb) for c in range(CPB) for kb in range(TPC * (c + 1))]
    NU = len(UNITS)
    MAXES = [(c, h, t, j) for c in range(CPB) for h in range(GS) for t in range(TPC) for j in range(c + 1)]
    NM = len(MAXES)
    MPS = NM // NU
    LEAD = 20
    STEPS = NU * NKV
    ROWS = GS * TPC
    last_max = {}
    for n, (c, h, t, j) in enumerate(MAXES):
        last_max[c] = n + 1
    diag = [u for u, (c, kb) in enumerate(UNITS) if kb >= TPC * c]
    ends = [u for u, (c, kb) in enumerate(UNITS) if kb == TPC * (c + 1) - 1]

    with ExitStack() as ctx:
        a = Alloc(nc, ctx, "att")
        passed = a.sem("passed")
        qs = a.sb("qs", [KR + 2, NKV, CPB, GS * CH], BF16)
        ks = a.sb("ks", [KR + 2, NKV, S], BF16)
        v = a.sb("v", [P, NKV, TPB, VW])
        pr = a.sb("pr", [P, 4, GS, CH])
        junk = a.sb("junk", [P, 2, CH], BF16)
        mx = a.sb("mx", [P, 2, ROWS, CPB])
        nm = a.sb("nm", [P, ROWS])
        nml = a.sb("nml", [P, 2, ROWS], BF16)
        mrow = a.sb("mrow", [2 * ROWS, CPB, P], BF16)
        cT = a.sb("cT", [P, 2, CH])
        rz = a.sb("rz", [P, TPC, GS])
        cn = a.sb("cn", [P, CPB, TPC, GS * HD])
        sT = a.ps("sT", [P, GS, CH])
        mb = a.ps("mb", [P, 2, CH])
        acc = a.ps("acc", [P, CH])
        misc = a.ps("misc", [P, CH])
        miscb = misc[:, 0:P // 2].bitcast(BF16)
        sem = a.sem
        loaded = [sem(f"loaded{g}") for g in range(NKV)]
        m_rows = [sem(f"m_rows{c}") for c in range(CPB)]
        c_out = [sem(f"c_out{c}") for c in range(CPB)]
        (ones_set, sT_ready, exp_done, mask_done, pv_done, mb_ready, mb_used, m_step, nm_ready, mT_ready,
         mrow_ready, cT_ready, c_turned, rz_ready, cn_ready) = (
            sem(n) for n in ("ones_set", "sT_ready", "exp_done", "mask_done", "pv_done", "mb_ready",
                             "mb_used", "m_step", "nm_ready", "mT_ready", "mrow_ready", "cT_ready",
                             "c_turned", "rz_ready", "cn_ready"))
        NLD = 2 * len(Q_PART) + 1
        credits = [(exp_done, 2), (pv_done, 4), (mb_used, 2), (cT_ready, 1), (c_turned, 2), (mrow_ready, 1), (cn_ready, 1)] + \
                  [(s, 32) for s in m_rows] + [(s, 16) for s in c_out]

        def m_events(s, limit):
            lo, hi = MPS * (s + LEAD), MPS * (s + LEAD + 1) if s < STEPS else 0
            return [(g, c) for g in range(limit) for c in range(CPB) if lo < g * NM + last_max[c] <= hi]

        def c_events(s, lag):
            return [((s - lag) // NU, UNITS[(s - lag) % NU][0])] if 0 <= s - lag < STEPS and (s - lag) % NU in ends else []

        C_LAG = 3
        TAIL = STEPS + C_LAG + 1
        NMC = NKV * CPB

        def run(step_fn, eng):
            for s in range(-LEAD, 0):
                step_fn(0, s, False, NKV)
            with eng.Fori(0, B - 1) as b:
                for s in range(TAIL):
                    step_fn(b, s, True, NKV + 1)
            for s in range(TAIL):
                step_fn(B - 1, s, True, NKV)

        def maxes_of(s, limit):
            lo = MPS * (s + LEAD)
            return [k for k in range(lo, lo + MPS) if k < limit * NM] if s < STEPS else []
        def m_before(b, g, c):
            return b * NMC + g * CPB + c

        def m_by(s, limit):
            return sum(1 for g in range(NKV + 1) for c in range(CPB) if g * NM + last_max[c] <= MPS * (min(s, STEPS) + LEAD)
                       and g < limit)

        def c_by(s):
            return sum(1 for r in range(s) if c_events(r, C_LAG))

        with nc.Block() as block:
            @block.sync
            def _(sp):
                for s, n in credits:
                    sp.sem_inc(s, n)

                def load(b, g):
                    for j in range(len(Q_PART)):
                        r = slice(HD * j, HD * (j + 1))
                        sp.dma_start(qs[r, g], scr["q_in"][b, Q_PART[j], g]).then_inc(loaded[g], 16)
                        sp.dma_start(ks[r, g], scr["k_in"][b, K_PART[j], g]).then_inc(loaded[g], 16)
                    sp.dma_start(v[:, g].rearrange("p (c t) w -> p c (t w)", c=CPB),
                                 scr["v_in"][b, :, g]).then_inc(loaded[g], 16)

                for g in range(NKV):
                    load(0, g)

                def step(b, s, main, limit):
                    for g, c in m_events(s - 1, limit):
                        n = b * NMC + g * CPB + c
                        sp.wait_ge(mrow_ready, n + 2)
                        for hl in range(2):
                            sp.dma_start(qs[KR + hl:KR + hl + 1, g % NKV, c, :],
                                         mrow[hl * ROWS:(hl + 1) * ROWS, c, :]).then_inc(m_rows[c], 16)
                    for g, c in c_events(s, C_LAG):
                        sp.wait_ge(cn_ready, b * NMC + g * CPB + c + 2)
                        sp.dma_start(scr["ctx_out"][b, c, :, :, g * GS * HD:(g + 1) * GS * HD],
                                     cn[:, c]).then_inc(c_out[c], 16)
                    if main and limit > NKV and s > 0 and s % NU == 0 and s <= STEPS:
                        g = s // NU - 1
                        sp.wait_ge(pv_done, b * STEPS + s + 4)
                        load(b + 1, g)

                run(step, sp)
                for c in range(CPB):
                    sp.wait_ge(c_out[c], 16 * (B * NKV + 1))

            @block.gpsimd
            def _(pool):
                def step(b, s, main, limit):
                    if main and s < STEPS and s % NU in diag:
                        u = s % NU
                        c, kb = UNITS[u]
                        off = (kb - TPC * c) * P
                        wait_apart(pool, exp_done, 2 * (b * STEPS + s) + 4, passed)
                        blk = pr[:, s % 4, :, off:off + P]
                        nc.gpsimd.affine_select(out=blk, in_=blk, compare_op=ALU.is_ge, fill=0.0, base=0,
                                                pattern=[[0, GS], [1, P]],
                                                channel_multiplier=-1).then_inc(mask_done, 1)

                with pool.Fori(0, B) as b:
                    for s in range(STEPS):
                        step(b, s, True, NKV)

            @block.scalar
            def _(act):
                def step(b, s, main, limit):
                    n = b * STEPS + s
                    if main and s < STEPS:
                        c, kb = UNITS[s % NU]
                        off = max(0, kb - TPC * c) * P
                        act.wait_ge(pv_done, n + 1)
                        for hf in range(2):
                            act.wait_ge(sT_ready, 2 * n + hf + 1)
                            nc.scalar.activation(pr[:, s % 4, 2 * hf:2 * hf + 2, off:CH],
                                                 sT[:, 2 * hf:2 * hf + 2, off:CH], ACT.Exp,
                                                 scale=float(HD) ** -0.5).then_inc(exp_done, 1)
                    if main:
                        for g, c in c_events(s, 1):
                            m = b * NMC + g * CPB + c
                            act.wait_ge(pv_done, b * STEPS + s - 1 + 5)
                            act.wait_ge(c_turned, m + 1)
                            nc.scalar.copy(cT[:, c % 2, :], acc[:, :]).then_inc(cT_ready, 1)

                with act.Fori(0, B) as b:
                    for s in range(STEPS + 2):
                        step(b, s, True, NKV)

            @block.vector
            def _(dve):
                nc.vector.memset(ks[KR:KR + 2, :, :], 1.0).then_inc(ones_set, 1)

                def step(b, s, main, limit):
                    for k in maxes_of(s, limit):
                        g, (c, h, t, j) = k // NM, MAXES[k % NM]
                        n = b * NKV * NM + k
                        r = h * TPC + t
                        if j < c:
                            dve.wait_ge(mb_ready, n + 1)
                            nc.vector.tensor_reduce(mx[:, c % 2, r, j:j + 1], mb[:, k % 2, :], AX.X,
                                                    ALU.max).then_inc(mb_used, 1)
                        else:
                            wd = (t + 1) * P
                            dve.wait_ge(mb_used, n + 2)
                            wait_apart(dve, mb_ready, n + 1, passed)
                            nc.vector.tensor_tensor_reduce(junk[:, t % 2, 0:wd], mb[:, k % 2, 0:wd],
                                                           w["causal"][:, CH - wd:CH], 1.0, LOW, ALU.add, ALU.max,
                                                           mx[:, c % 2, r, j:j + 1]).then_inc(mb_used, 1)
                    for g, c in m_events(s - 1, limit):
                        n = b * NMC + g * CPB + c
                        dve.wait_ge(mT_ready, n + 1)
                        dve.wait_ge(m_rows[c], 32 * (b * NKV + g) + 32)
                        nc.vector.tensor_copy(mrow[:, c, :], miscb[0:2 * ROWS, :]).then_inc(mrow_ready, 1)
                    for g, c in m_events(s, limit):
                        n = b * NMC + g * CPB + c
                        dve.wait_ge(mb_used, b * NKV * NM + g * NM + last_max[c] + 2)
                        nc.vector.tensor_reduce(nm[:], mx[:, c % 2, :, 0:c + 1], AX.X, ALU.max,
                                                negate=True).then_inc(m_step, 1)
                        dve.wait_ge(m_step, 2 * n + 1)
                        nc.vector.tensor_copy(nml[:, 0, :], nm[:]).then_inc(m_step, 1)
                        dve.wait_ge(m_step, 2 * n + 2)
                        nc.vector.tensor_tensor(nml[:, 1, :], nm[:], nml[:, 0, :], ALU.subtract).then_inc(nm_ready, 1)
                    if main:
                        for g, c in c_events(s, C_LAG):
                            n = b * NMC + g * CPB + c
                            ct = misc[:, :].rearrange("p (t h w) -> p t h w", t=TPC, h=GS)
                            dve.wait_ge(c_turned, n + 3)
                            nc.vector.reciprocal(rz[:, :, :], ct[:, :, :, HD]).then_inc(rz_ready, 1)
                            dve.wait_ge(rz_ready, n + 1)
                            dve.wait_ge(c_out[c], 16 * (b * NKV + g) + 16)
                            nc.vector.tensor_tensor(cn[:, c].rearrange("p t (h d) -> p t h d", h=GS),
                                                    ct[:, :, :, 0:HD], rz[:, :, :].unsqueeze(3).to_broadcast([P, TPC, GS, HD]),
                                                    ALU.mult).then_inc(cn_ready, 1)

                run(step, dve)

            @block.tensor
            def _(pe):
                pe.wait_ge(ones_set, 1)

                def maxima(b, ks_list):
                    for k in ks_list:
                        g, (c, h, t, j) = k // NM, MAXES[k % NM]
                        g4 = g % NKV
                        n = b * NKV * NM + k
                        if k % NM == 0:
                            pe.wait_ge(loaded[g4], 16 * NLD * (b + g // NKV) + 16 * NLD)
                        pe.wait_ge(mb_used, n + 1)
                        q0 = h * CH + t * P
                        wd = CH if j < c else (t + 1) * P
                        nc.tensor.matmul(mb[:, k % 2, 0:wd], qs[0:KR, g4, c, q0:q0 + P],
                                         ks[0:KR, g4, j * CH:j * CH + wd], start=True, stop=True).then_inc(mb_ready, 1)

                def values(b, s):
                    c, kb = UNITS[s % NU]
                    g, n = s // NU, b * STEPS + s
                    off = max(0, kb - TPC * c) * P
                    pe.wait_ge(exp_done, 2 * n + 4)
                    if s % NU in diag:
                        pe.wait_ge(mask_done, b * len(diag) * NKV + g * len(diag) + diag.index(s % NU) + 1)
                    if kb == 0:
                        pe.wait_ge(cT_ready, b * NMC + g * CPB + c + 1)
                    for h in range(GS):
                        last = nc.tensor.matmul(acc[VW * h:VW * (h + 1), off:CH], v[:, g, kb, :],
                                                pr[:, s % 4, h, off:CH], start=(kb == 0),
                                                stop=(kb == TPC * (c + 1) - 1), skip_group_check=True)
                    last.then_inc(pv_done, 1)

                def step(b, s, main, limit):
                    todo = maxes_of(s, limit)
                    if main and s < STEPS:
                        c, kb = UNITS[s % NU]
                        g, n = s // NU, b * STEPS + s
                        off = max(0, kb - TPC * c) * P
                        if kb == 0:
                            pe.wait_ge(m_rows[c], 32 * (b * NKV + g) + 64)
                        for hf in range(2):
                            pe.wait_ge(exp_done, 2 * n + hf + 1)
                            for h in (2 * hf, 2 * hf + 1):
                                last = nc.tensor.matmul(sT[:, h, off:CH], ks[:, g, kb * P:(kb + 1) * P],
                                                        qs[:, g, c, h * CH + off:(h + 1) * CH], start=True, stop=True)
                            last.then_inc(sT_ready, 1)
                            maxima(b, todo[MPS // 2 * hf:MPS // 2 * (hf + 1)])
                    else:
                        maxima(b, todo)
                    for g, c in m_events(s - 1, limit):
                        pe.wait_ge(nm_ready, b * NMC + g * CPB + c + 1)
                        pe.wait_ge(mrow_ready, m_before(b, g, c) + 1)
                        pe.wait_ge(cn_ready, b * NMC + c_by(s) + 1)
                        nc.tensor.transpose(miscb[0:2 * ROWS, :], nml[:, :, :].rearrange("p a r -> p (a r)"),
                                            w["identb"][:]).then_inc(mT_ready, 1)
                    if main:
                        for g, c in c_events(s, C_LAG):
                            pe.wait_ge(cT_ready, b * NMC + g * CPB + c + 2)
                            pe.wait_ge(mrow_ready, b * NMC + m_by(s, limit) + 1)
                            pe.wait_ge(cn_ready, b * NMC + g * CPB + c + 1)
                            for t in range(TPC):
                                last = nc.tensor.transpose(misc[:, t * P:(t + 1) * P], cT[:, c % 2, t * P:(t + 1) * P],
                                                           w["ident"][:])
                            last.then_inc(c_turned, 1)
                        if 1 <= s <= STEPS:
                            values(b, s - 1)

                run(step, pe)


def dispatch(nc, w, scr):
    HB = SB // 2
    with ExitStack() as ctx:
        a = Alloc(nc, ctx, "dis")
        passed = a.sem("passed")
        yT = a.sb("yT", [P, CPB, DK, CH])
        y = a.sb("y", [P, TPB, D + 1])
        lg = a.sb("lg", [P, TPB, NS])
        e1 = a.sb("e1", [P, 2, NS])
        nr = a.sb("nr", [P, TPB])
        zr = a.sb("zr", [P, TPB])
        cm = a.sb("cm", [P, NS])
        ca = a.sb("ca", [P, NS])
        rz = a.sb("rz", [P, SB])
        sl = a.sb("sl", [P, SB, D])
        slT = a.sb("slT", [P, SB, DK, P])
        lp = a.ps("lp", [P, 4, 512])
        dp = a.ps("dp", [P, 4, 512])
        sem = a.sem
        yT_in = [sem(f"yT_in{c}") for c in range(CPB)]
        y_in, e_out0, e_out1, z_out, s_out = (sem(n) for n in ("y_in", "e_out0", "e_out1", "z_out", "s_out"))
        e_out = [e_out0, e_out1]
        (ones_set, lp_ready, lg_ready, nr_ready, cm_done, ca_ready, e1_ready, sub_done, d_ready, d_used,
         half_done, rz_ready, sl_ready, slT_ready, slT_kept) = (
            sem(n) for n in ("ones_set", "lp_ready", "lg_ready", "nr_ready", "cm_done", "ca_ready", "e1_ready",
                             "sub_done", "d_ready", "d_used", "half_done", "rz_ready", "sl_ready", "slT_ready",
                             "slT_kept"))
        sub_v = sem("sub_v")
        sub_p = sem("sub_p")
        credits = [(d_used, TPB), (slT_kept, SB), (ca_ready, 1), (e_out0, 16), (e_out1, 16),
                   (z_out, 16), (s_out, 16 * 2 * SB), (lg_ready, 2), (sub_p, TPB // 2), (sub_v, TPB // 2)]
        bank = lambda s: (lp if s < HB else dp)[:, s % HB, :]

        with nc.Block() as block:
            @block.sync
            def _(sp):
                for s, n in credits:
                    sp.sem_inc(s, n)
                with sp.Fori(0, B) as b:
                    for c in range(CPB):
                        sp.wait_ge(d_used, b * TPB + TPB)
                        sp.dma_start(yT[:, c], scr["yT_in"][b, c]).then_inc(yT_in[c], 16)
                    for c in range(CPB):
                        sp.dma_start(y[:, c * TPC:(c + 1) * TPC, 0:D], scr["y_in"][b, c]).then_inc(y_in, 16)
                    for t in range(TPB):
                        sp.wait_ge(e1_ready, b * TPB + t + 1)
                        sp.dma_start(scr["e1"][b, t], e1[:, t % 2]).then_inc(e_out[t % 2], 16)
                    sp.dma_start(scr["zr"][b], zr[:, :]).then_inc(z_out, 16)
                    for s in range(SB):
                        sp.wait_ge(slT_kept, b * SB + SB + s + 1)
                        for k in range(DK):
                            sp.dma_start(scr["slot_out"][b, s, k],
                                         slT[:, s, k, :].rearrange("p (e j) -> p e j", e=2)).then_inc(s_out, 16)
                sp.wait_ge(e_out0, 16 * (B * TPB // 2 + 1))
                sp.wait_ge(e_out1, 16 * (B * TPB // 2 + 1))
                sp.wait_ge(z_out, 16 * (B + 1))
                sp.wait_ge(s_out, 16 * 2 * SB * (B + 1))

            @block.scalar
            def _(act):
                with act.Fori(0, B) as b:
                    for t in range(TPB + 1):
                        if t < TPB:
                            act.wait_ge(lp_ready, b * TPB + t + 1)
                            act.wait_ge(d_used, b * TPB + t + 1)
                            nc.scalar.copy(lg[:, t, :], lp[:, 2 * (t % 2):2 * (t % 2) + 2, :]
                                           .rearrange("p a n -> p (a n)")).then_inc(lg_ready, 1)
                        if t > 0:
                            u = t - 1
                            act.wait_ge(nr_ready, b * TPB + u + 1)
                            if u == 0:
                                act.wait_ge(z_out, 16 * b + 16)
                            act.wait_ge(e_out[u % 2], 16 * (b * TPB // 2 + u // 2) + 16)
                            nc.scalar.activation(e1[:, u % 2], lg[:, u, :], ACT.Exp, bias=nr[:, u:u + 1],
                                                 accum_out=zr[:, u:u + 1]).then_inc(e1_ready, 1)
                    for t in range(TPB):
                        if t % 2:
                            act.wait_ge(sub_v, b * (TPB // 2) + TPB // 2 + t // 2 + 1)
                        else:
                            act.wait_ge(sub_p, b * (TPB // 2) + TPB // 2 + t // 2 + 1)
                        nc.scalar.activation(lg[:, t, :], lg[:, t, :], ACT.Exp).then_inc(d_ready, 1)
                    for s in range(SB):
                        act.wait_ge(slT_ready, b * SB + s + 1)
                        if s == 0:
                            act.wait_ge(s_out, 16 * 2 * SB * b + 16 * 2 * SB)
                        nc.scalar.copy(slT[:, s].rearrange("p k n -> p (k n)"), bank(s)[:, 0:D]).then_inc(slT_kept, 1)

            @block.vector
            def _(dve):
                nc.vector.memset(y[:, :, D:D + 1], 1.0).then_inc(ones_set, 1)
                with dve.Fori(0, B) as b:
                    for t in range(TPB):
                        dve.wait_ge(lg_ready, b * TPB + t + 3)
                        if t == 0:
                            dve.wait_ge(ca_ready, b + 1)
                        nc.vector.tensor_reduce(nr[:, t:t + 1], lg[:, t, :], AX.X, ALU.max,
                                                negate=True).then_inc(nr_ready, 1)
                        if t == 0:
                            nc.vector.tensor_copy(cm[:], lg[:, t, :]).then_inc(cm_done, 1)
                        else:
                            dve.wait_ge(cm_done, b * TPB + t)
                            nc.vector.tensor_tensor(cm[:], cm[:], lg[:, t, :], ALU.max).then_inc(cm_done, 1)
                    dve.wait_ge(ca_ready, b + 2)
                    for t in range(1, TPB, 2):
                        dve.wait_ge(e1_ready, b * TPB + t + 1)
                        nc.vector.tensor_tensor(lg[:, t, :], lg[:, t, :], ca[:], ALU.subtract).then_inc(sub_v, 1)
                    for s in range(SB):
                        if s < HB:
                            dve.wait_ge(half_done, b + 1)
                        else:
                            dve.wait_ge(d_used, b * TPB + 2 * TPB)
                        nc.vector.reciprocal(rz[:, s:s + 1], bank(s)[:, D:D + 1]).then_inc(rz_ready, 1)
                        dve.wait_ge(rz_ready, b * SB + s + 1)
                        nc.vector.tensor_scalar(sl[:, s, :], bank(s)[:, 0:D], rz[:, s:s + 1], None,
                                                ALU.mult).then_inc(sl_ready, 1)

            @block.gpsimd
            def _(pool):
                with pool.Fori(0, B) as b:
                    pool.wait_ge(sub_v, b * (TPB // 2) + TPB // 2)
                    wait_apart(pool, cm_done, b * TPB + TPB, passed)
                    nc.gpsimd.partition_all_reduce(ca[:], cm[:], P, RMAX).then_inc(ca_ready, 1)
                    pool.wait_ge(ca_ready, b + 2)
                    for t in range(0, TPB, 2):
                        pool.wait_ge(e1_ready, b * TPB + t + 1)
                        nc.gpsimd.tensor_tensor(lg[:, t, :], lg[:, t, :], ca[:], ALU.subtract).then_inc(sub_p, 1)

            @block.tensor
            def _(pe):
                pe.wait_ge(ones_set, 1)
                with pe.Fori(0, B) as b:
                    pe.wait_ge(slT_kept, b * SB + SB)
                    for t in range(TPB):
                        if t % TPC == 0:
                            pe.wait_ge(yT_in[t // TPC], 16 * b + 16)
                        pe.wait_ge(lg_ready, b * TPB + t + 1)
                        for h in range(2):
                            for k in range(DK):
                                last = nc.tensor.matmul(lp[:, 2 * (t % 2) + h, :],
                                                        yT[:, t // TPC, k, (t % TPC) * P:(t % TPC + 1) * P],
                                                        w["seT"][:, k, h * 512:(h + 1) * 512], start=(k == 0),
                                                        stop=(k == DK - 1))
                        last.then_inc(lp_ready, 1)
                    pe.wait_ge(lg_ready, b * TPB + TPB + 2)
                    pe.wait_ge(y_in, 16 * CPB * b + 16 * CPB)

                    def turn(hf):
                        for s in range(hf * HB, (hf + 1) * HB):
                            pe.wait_ge(sl_ready, b * SB + s + 1)
                            for k in range(DK):
                                last = nc.tensor.transpose(bank(s)[:, k * P:(k + 1) * P], sl[:, s, k * P:(k + 1) * P],
                                                           w["ident"][:])
                            last.then_inc(slT_ready, 1)

                    for hf in range(2):
                        for t in range(TPB):
                            pe.wait_ge(d_ready, b * TPB + t + 1)
                            if hf and t == 3:
                                turn(0)
                            for s in range(hf * HB, (hf + 1) * HB):
                                last = nc.tensor.matmul(bank(s)[:, 0:D + 1], lg[:, t, s * P:(s + 1) * P], y[:, t, :],
                                                        start=(t == 0), stop=(t == TPB - 1))
                            if hf:
                                last.then_inc(d_used, 1)
                        if hf == 0:
                            last.then_inc(half_done, 1)
                    turn(1)


def experts(nc, w, io, scr):
    FB = F // P
    RB = B * SL // P
    with ExitStack() as ctx:
        a = Alloc(nc, ctx, "exp")
        wg, wu = a.sb("wg", [P, 2, DK, F]), a.sb("wu", [P, 2, DK, F])
        wd = a.sb("wd", [P, 2, FB, D])
        sl = a.sb("sl", [P, 2, DK, B * SL])
        bd = a.sb("bd", [P, 2, D])
        bg, bu = a.sb("bg", [P, 2, FB]), a.sb("bu", [P, 2, FB])
        gate = a.sb("gate", [P, 2, FB, B * SL])
        h = a.sb("h", [P, 2, FB, B * SL])
        eo = a.sb("eo", [P, 2, RB, D])
        gp = a.ps("gp", [P, FB, B * SL])
        up = a.ps("up", [P, FB, B * SL])
        op = a.ps("op", [P, 2, RB, D])
        sem = a.sem
        gu_in = [sem(f"gu_in{q}") for q in range(2)]
        down_in = [sem(f"down_in{q}") for q in range(2)]
        out = [sem(f"out{q}") for q in range(2)]
        bias_ready, gu_ready, gate_ready, h_ready, o_ready, eo_ready = (
            sem(n) for n in ("bias_ready", "gu_ready", "gate_ready", "h_ready", "o_ready", "eo_ready"))
        NGU, NDN = 3, 2
        credits = [(gu_ready, 2), (gate_ready, FB), (h_ready, FB), (o_ready, 2), (eo_ready, 2 * RB),
                   (out[0], 16 * B), (out[1], 16 * B)]

        with nc.Block() as block:
            @block.sync
            def _(sp):
                for s, n in credits:
                    sp.sem_inc(s, n)

                def load_gu(e, q):
                    sp.wait_ge(gu_ready, 2 * e)
                    for dst, src in ((sl[:, q], scr["slot_in"][e]), (wg[:, q], io["Wg"][e]), (wu[:, q], io["Wu"][e])):
                        sp.dma_start(dst, src).then_inc(gu_in[q], 16)

                def load_down(e, q):
                    sp.wait_ge(o_ready, e + 1)
                    sp.wait_ge(eo_ready, RB * (e + 1))
                    for dst, src in ((wd[:, q], io["Wd"][e]), (bd[:, q], io["bd"][e].partition_broadcast(P))):
                        sp.dma_start(dst, src).then_inc(down_in[q], 16)

                def store(e, q):
                    sp.wait_ge(eo_ready, RB * (e + 3))
                    for b in range(B):
                        r = slice(SL * (b % 2), SL * (b % 2) + SL)
                        sp.dma_start(scr["eo_out"][e, b], eo[r, q, b // 2, :]).then_inc(out[q], 16)

                sp_first = ((sl[:, 0], scr["slot_in"][0]), (wg[:, 0], io["Wg"][0]), (wu[:, 0], io["Wu"][0]))
                for dst, src in sp_first:
                    sp.dma_start(dst, src).then_inc(gu_in[0], 16)
                load_gu(1, 1)
                load_down(0, 0)
                load_gu(2, 0)
                load_down(1, 1)
                with sp.Fori(1, E // 2 - 1) as j:
                    for q in range(2):
                        e = 2 * j + q
                        load_gu(e + 1, 1 - q)
                        store(e - 2, q)
                        load_down(e, q)
                load_gu(E - 1, 1)
                store(E - 4, 0)
                load_down(E - 2, 0)
                store(E - 3, 1)
                load_down(E - 1, 1)
                store(E - 2, 0)
                store(E - 1, 1)
                for q in range(2):
                    sp.wait_ge(out[q], 16 * B * (E // 2 + 1))

            @block.scalar
            def _(act):
                with act.Fori(0, E // 2) as j:
                    for q in range(2):
                        e = 2 * j + q
                        act.wait_ge(bias_ready, 2 * e + 1)
                        for f in range(FB):
                            act.wait_ge(gu_ready, 2 * e + f // 2 + 3)
                            nc.scalar.activation(gate[:, q, f, :], gp[:, f, :], ACT.Gelu,
                                                 bias=bg[:, q, f:f + 1]).then_inc(gate_ready, 1)

            @block.vector
            def _(dve):
                def hidden(e, q):
                    nc.vector.tensor_copy(bg[:, q, :], w["bgT"][:, :, bass.ds(e, 1)].rearrange("p f o -> p (f o)")
                                          ).then_inc(bias_ready, 1)
                    nc.vector.tensor_copy(bu[:, q, :], w["buT"][:, :, bass.ds(e, 1)].rearrange("p f o -> p (f o)")
                                          ).then_inc(bias_ready, 1)
                    dve.wait_ge(bias_ready, 2 * e + 2)
                    dve.wait_ge(o_ready, e + 1)
                    for f in range(FB):
                        dve.wait_ge(gate_ready, FB * e + FB + f + 1)
                        dve.wait_ge(gu_ready, 2 * e + f // 2 + 3)
                        nc.vector.scalar_tensor_tensor(out=h[:, q, f, :], in0=up[:, f, :], scalar=bu[:, q, f:f + 1],
                                                       in1=gate[:, q, f, :], op0=ALU.add,
                                                       op1=ALU.mult).then_inc(h_ready, 1)

                def output(e, j, q):
                    dve.wait_ge(o_ready, e + 3)
                    dve.wait_ge(down_in[q], 16 * NDN * j + 16 * NDN)
                    dve.wait_ge(out[q], 16 * B * j + 16 * B)
                    for r in range(RB):
                        nc.vector.tensor_tensor(eo[:, q, r, :], op[:, q, r, :], bd[:, q, :],
                                                ALU.add).then_inc(eo_ready, 1)

                hidden(0, 0)
                with dve.Fori(0, E // 2 - 1) as j:
                    hidden(2 * j + 1, 1)
                    output(2 * j, j, 0)
                    hidden(2 * j + 2, 0)
                    output(2 * j + 1, j, 1)
                hidden(E - 1, 1)
                output(E - 2, E // 2 - 1, 0)
                output(E - 1, E // 2 - 1, 1)

            @block.tensor
            def _(pe):
                def gate_up(e, j, q):
                    pe.wait_ge(gu_in[q], 16 * NGU * j + 16 * NGU)
                    for half in range(FB // 2):
                        pe.wait_ge(gate_ready, FB * e + 2 * half + 2)
                        pe.wait_ge(h_ready, FB * e + 2 * half + 2)
                        for f in (2 * half, 2 * half + 1):
                            for dst, wt in ((gp, wg), (up, wu)):
                                for k in range(DK):
                                    last = nc.tensor.matmul(dst[:, f, :], wt[:, q, k, f * P:(f + 1) * P],
                                                            sl[:, q, k, :], start=(k == 0), stop=(k == DK - 1))
                        last.then_inc(gu_ready, 1)

                def down(e, j, q):
                    pe.wait_ge(down_in[q], 16 * NDN * j + 16 * NDN)
                    pe.wait_ge(h_ready, FB * e + 2 * FB)
                    pe.wait_ge(eo_ready, RB * (e + 1))
                    for r in range(RB):
                        for f in range(FB):
                            last = nc.tensor.matmul(op[:, q, r, :], h[:, q, f, r * P:(r + 1) * P], wd[:, q, f, :],
                                                    start=(f == 0), stop=(f == FB - 1))
                    last.then_inc(o_ready, 1)

                gate_up(0, 0, 0)
                with pe.Fori(0, E // 2 - 1) as j:
                    gate_up(2 * j + 1, j, 1)
                    down(2 * j, j, 0)
                    gate_up(2 * j + 2, j + 1, 0)
                    down(2 * j + 1, j, 1)
                gate_up(E - 1, E // 2 - 1, 1)
                down(E - 2, E // 2 - 1, 0)
                down(E - 1, E // 2 - 1, 1)


def combine(nc, w, io, scr):
    with ExitStack() as ctx:
        a = Alloc(nc, ctx, "com")
        eo = a.sb("eo", [P, SB, D])
        e1 = a.sb("e1", [P, 2, NS])
        c = a.sb("c", [P, 2, D])
        x = a.sb("x", [P, 2, D])
        e1T = a.sb("e1T", [P, 2, SB, P])
        cT = a.sb("cT", [P, 2, DK, P])
        zr, rz = a.sb("zr", [P, TPB]), a.sb("rz", [P, TPB])
        part = a.sb("part", [P, 2, D])
        o = a.sb("o", [P, 2, D])
        tp = a.ps("tp", [P, 2, 3, 512])
        mp = a.ps("mp", [P, 2, 512])
        sem = a.sem
        in_ = [sem(f"in{q}") for q in range(2)]
        x_in = [sem(f"x_in{q}") for q in range(2)]
        out = [sem(f"out{q}") for q in range(2)]
        eo_in, z_in, turned, e1T_kept, cT_kept, m_ready, rz_ready, part_ready, o_ready = (
            sem(n) for n in ("eo_in", "z_in", "turned", "e1T_kept", "cT_kept", "m_ready", "rz_ready", "part_ready",
                             "o_ready"))
        credits = [(turned, 2), (e1T_kept, 2), (cT_kept, 2), (m_ready, 2), (o_ready, 2), (rz_ready, 1),
                   (out[0], 16), (out[1], 16)]
        H2 = TPB // 2
        with nc.Block() as block:
            @block.sync
            def _(sp):
                for s, n in credits:
                    sp.sem_inc(s, n)
                with sp.Fori(0, B) as b:
                    for t in range(TPB):
                        q = t % 2
                        n = b * TPB + t
                        sp.wait_ge(turned, n + 1)
                        sp.dma_start(e1[:, q], scr["e1"][b, t]).then_inc(in_[q], 16)
                        sp.dma_start(c[:, q], scr["ctx_in"][b, t]).then_inc(in_[q], 16)
                        sp.wait_ge(o_ready, n + 1)
                        sp.dma_start(x[:, q], io["x_tile"][b, t]).then_inc(x_in[q], 16)
                        if t == 0:
                            sp.wait_ge(m_ready, b * TPB + 2)
                            sp.dma_start(eo[:], scr["eo_in"][b]).then_inc(eo_in, 16)
                            sp.wait_ge(rz_ready, b + 1)
                            sp.dma_start(zr[:], scr["zr"][b]).then_inc(z_in, 16)

            @block.scalar
            def _(act):
                def store(b, t):
                    act.wait_ge(o_ready, b * TPB + t + 3)
                    act.dma_start(io["out_tile"][b, t], o[:, t % 2]).then_inc(out[t % 2], 16)

                with act.Fori(0, B) as b:
                    for t in range(TPB):
                        q = t % 2
                        n = b * TPB + t
                        act.wait_ge(turned, n + 3)
                        act.wait_ge(m_ready, n + 1)
                        nc.scalar.copy(e1T[:, q].rearrange("p s n -> p (s n)"),
                                       tp[:, q, 0:2, :].rearrange("p a n -> p (a n)")).then_inc(e1T_kept, 1)
                        if t > 1:
                            store(b, t - 2)
                    for t in (TPB - 2, TPB - 1):
                        store(b, t)
                for q in range(2):
                    act.wait_ge(out[q], 16 * (B * H2 + 1))

            @block.vector
            def _(dve):
                with dve.Fori(0, B) as b:
                    for t in range(TPB + 1):
                        n = b * TPB + t
                        if t < TPB:
                            q = t % 2
                            dve.wait_ge(turned, n + 3)
                            dve.wait_ge(m_ready, n + 1)
                            nc.vector.tensor_copy(cT[:, q].rearrange("p k n -> p (k n)"),
                                                  tp[:, q, 2, 0:D]).then_inc(cT_kept, 1)
                        if t == 0:
                            dve.wait_ge(z_in, 16 * b + 16)
                            nc.vector.reciprocal(rz[:], zr[:]).then_inc(rz_ready, 1)
                            dve.wait_ge(rz_ready, b + 2)
                        if t > 0:
                            u, q = t - 1, (t - 1) % 2
                            n = b * TPB + u
                            dve.wait_ge(m_ready, n + 3)
                            dve.wait_ge(x_in[q], 16 * (b * H2 + u // 2) + 16)
                            nc.vector.scalar_tensor_tensor(out=part[:, q, :], in0=mp[:, q, 0:D],
                                                           scalar=rz[:, u:u + 1], in1=x[:, q, :], op0=ALU.mult,
                                                           op1=ALU.add).then_inc(part_ready, 1)
                            dve.wait_ge(part_ready, n + 1)
                            dve.wait_ge(out[q], 16 * (b * H2 + u // 2) + 16)
                            nc.vector.tensor_tensor(o[:, q, :], part[:, q, :], mp[:, q, D:2 * D],
                                                    ALU.add).then_inc(o_ready, 1)

            @block.tensor
            def _(pe):
                with pe.Fori(0, B) as b:
                    for t in range(TPB + 1):
                        if t < TPB:
                            q = t % 2
                            n = b * TPB + t
                            pe.wait_ge(in_[q], 32 * (b * H2 + t // 2) + 32)
                            pe.wait_ge(e1T_kept, n + 1)
                            pe.wait_ge(cT_kept, n + 1)
                            for s in range(SB):
                                nc.tensor.transpose(tp[:, q, s // 4, (s % 4) * P:(s % 4 + 1) * P],
                                                    e1[:, q, s * P:(s + 1) * P], w["ident"][:])
                            for k in range(DK):
                                last = nc.tensor.transpose(tp[:, q, 2, k * P:(k + 1) * P], c[:, q, k * P:(k + 1) * P],
                                                           w["ident"][:])
                            last.then_inc(turned, 1)
                        if t > 0:
                            u, q = t - 1, (t - 1) % 2
                            n = b * TPB + u
                            if u == 0:
                                pe.wait_ge(eo_in, 16 * b + 16)
                            pe.wait_ge(o_ready, n + 1)
                            pe.wait_ge(cT_kept, n + 3)
                            for k in range(DK):
                                nc.tensor.matmul(mp[:, q, D:2 * D], cT[:, q, k, :], w["woT"][:, k, :],
                                                 start=(k == 0), stop=(k == DK - 1))
                            pe.wait_ge(e1T_kept, n + 3)
                            for s in range(SB):
                                last = nc.tensor.matmul(mp[:, q, 0:D], e1T[:, q, s, :], eo[:, s, :],
                                                        start=(s == 0), stop=(s == SB - 1))
                            last.then_inc(m_ready, 1)


def block_kernel(nc, x, wq, wk, wv, wo, norm_g, norm_b, slot_g, slot_b, scale, slot_embeds,
                 Wg, bg, Wu, bu, Wd, bd, out):
    def dram(name, shape, dt=F32):
        return nc.dram_tensor(name, shape, dt, kind="Internal").ap()

    q_d = dram("q_parts", [3, NCH, D, CH], BF16)
    k_d = dram("k_parts", [3, NKV * HD, TOK], BF16)
    v_d = dram("v_rows", [NCH, P, NKV, TPC * VW])
    y_d = dram("y_rows", [NCH, P, TPC, D])
    yT_d = dram("y_cols", [NCH, P, DK, CH])
    c_d = dram("context", [B, S, D])
    e_d = dram("slot_exps", [B, TPB, P, NS])
    z_d = dram("slot_sums", [B, P, TPB])
    s_d = dram("slots", [E, P, DK, B * SL])
    o_d = dram("expert_out", [B, NS, D])
    io = {
        "x": x.rearrange("b (c t p) d -> (b c) p t d", p=P, t=TPC),
        "x_tile": x.rearrange("b (n p) d -> b n p d", p=P),
        "out_tile": out.rearrange("b (n p) d -> b n p d", p=P),
        "wq": wq, "wk": wk, "wv": wv, "wo": wo, "norm_g": norm_g, "norm_b": norm_b, "slot_g": slot_g,
        "slot_b": slot_b, "scale": scale, "slot_embeds": slot_embeds, "bg": bg, "bu": bu, "bd": bd,
        "Wg": Wg.rearrange("e (k p) f -> e p k f", p=P), "Wu": Wu.rearrange("e (k p) f -> e p k f", p=P),
        "Wd": Wd.rearrange("e (k p) o -> e p k o", p=P),
    }
    scr = {
        "q_out": q_d.rearrange("a i (m p) t -> i m p a t", p=P),
        "q_in": q_d.rearrange("a (b c) (g d h) t -> b a g d c (h t)", g=NKV, h=GS, b=B),
        "k_out": k_d.rearrange("a p (i t) -> i p a t", t=CH),
        "k_in": k_d.rearrange("a (g d) (b s) -> b a g d s", g=NKV, b=B),
        "v_out": v_d.rearrange("i p g x -> i p (g x)"),
        "v_in": v_d.rearrange("(b c) p g x -> b p g c x", b=B),
        "y": y_d, "y_in": y_d.rearrange("(b c) p t d -> b c p t d", b=B),
        "yT_out": yT_d, "yT_in": yT_d.rearrange("(b c) p k t -> b c p k t", b=B),
        "ctx_out": c_d.rearrange("b (c t p) d -> b c p t d", p=P, t=TPC),
        "ctx_in": c_d.rearrange("b (n p) d -> b n p d", p=P),
        "e1": e_d, "zr": z_d,
        "slot_out": s_d.rearrange("(s e) p k (b j) -> b s k p e j", e=2, b=B),
        "slot_in": s_d,
        "eo_out": o_d.rearrange("b (e j) d -> e b j d", e=E),
        "eo_in": o_d.rearrange("b (s p) d -> b p s d", p=P),
    }
    with ExitStack() as ctx:
        a = Alloc(nc, ctx, "w")
        w = {
            "ident": a.sb("ident", [P, P]), "identb": a.sb("identb", [P, P], BF16), "causal": a.sb("causal", [P, CH]),
            "wqT": a.sb("wqT", [P, DK, D]), "wkvT": a.sb("wkvT", [P, DK, P]), "woT": a.sb("woT", [P, DK, D]),
            "seT": a.sb("seT", [P, DK, NS]), "bgT": a.sb("bgT", [P, F // P, E]), "buT": a.sb("buT", [P, F // P, E]),
            "power": a.sb("power", [P, SB]), "ng": a.sb("ng", [P, D]), "nb": a.sb("nb", [P, D]),
        }
        prepare(nc, w, io)
        project(nc, w, io, scr)
        attend(nc, w, scr)
        dispatch(nc, w, scr)
        experts(nc, w, io, scr)
        combine(nc, w, io, scr)


_INS = ['L0_attn_x', 'L0_attn_wq', 'L0_attn_wk', 'L0_attn_wv', 'L0_attn_wo', 'L0_ffn_norm_g', 'L0_ffn_norm_b',
        'L0_ffn_slot_g', 'L0_ffn_slot_b', 'L0_ffn_scale', 'L0_ffn_slot_embeds', 'L0_ffn_Wg', 'L0_ffn_bg',
        'L0_ffn_Wu', 'L0_ffn_bu', 'L0_ffn_Wd', 'L0_ffn_bd']
_OUTS = [((B, S, D), 'float32')]


def kernel(**inputs):
    import numpy as _np
    import concourse.bacc as _bacc
    from concourse import mybir as _mybir
    from concourse.bass_utils import run_bass_kernel_spmd as _run

    nc = _bacc.Bacc("TRN2", target_bir_lowering=False, num_devices=1)
    arrays, args = {}, []
    for name in _INS:
        a = _np.ascontiguousarray(inputs[name])
        arrays[f"in_{name}_dram"] = a
        args.append(nc.dram_tensor(f"in_{name}_dram", a.shape, _mybir.dt.from_np(a.dtype), kind="ExternalInput").ap())
    for i, (shape, dtype) in enumerate(_OUTS):
        dt = _mybir.dt.from_np(_np.dtype(dtype))
        args.append(nc.dram_tensor(f"out_{i}_dram", shape, dt, kind="ExternalOutput").ap())
    block_kernel(nc, *args)
    r = _run(nc, [arrays], core_ids=[0])
    got = tuple(r.results[0][f"out_{i}_dram"] for i in range(len(_OUTS)))
    return got[0]
```

```python
from contextlib import ExitStack

import concourse.bass as bass
from concourse import mybir

ALU = mybir.AluOpType
ACT = mybir.ActivationFunctionType
AX = mybir.AxisListType
F32 = mybir.dt.float32
BF16 = mybir.dt.bfloat16
F32R = mybir.dt.float32r
RMAX = bass.bass_isa.ReduceOp.max

P = 128
B, S, D = 4, 2048, 256
NH, NKV, HD = 16, 4, 16
GS = NH // NKV
E, SL, F = 16, 64, 512
NS = E * SL
DK = D // P
EPS = 1e-5
LOW = -3.0e38
TOK = B * S
CH = 512
TPC = CH // P
CPB = S // CH
NCH = TOK // CH
TPB = S // P
SB = NS // P
Q_PART = (0, 0, 1, 1, 0, 2)
K_PART = (0, 1, 0, 1, 2, 0)
KR = HD * len(Q_PART)
VW = 32


class Alloc:

    def __init__(self, nc, ctx, tag):
        self.nc, self.ctx, self.tag = nc, ctx, tag

    def sb(self, name, shape, dt=F32):
        return self.ctx.enter_context(self.nc.sbuf_tensor(f"{self.tag}_{name}", shape, dt))

    def ps(self, name, shape, dt=F32):
        return self.ctx.enter_context(self.nc.psum_tensor(f"{self.tag}_{name}", shape, dt))

    def sem(self, name):
        return self.ctx.enter_context(self.nc.semaphore(f"{self.tag}_{name}"))


def wait_apart(eng, sem, value, passed):
    eng.wait_ge(sem, value)
    eng.sem_inc(passed, 1)


def prepare(nc, w, io):
    with ExitStack() as ctx:
        a = Alloc(nc, ctx, "prep")
        wq, wo = a.sb("wq", [P, DK, D]), a.sb("wo", [P, DK, D])
        wkv = a.sb("wkv", [P, D])
        se = a.sb("se", [P, SB, D])
        sg, sbb, sc = a.sb("sg", [P, D]), a.sb("sbb", [P, D]), a.sb("sc", [P, 1])
        bgr, bur = a.sb("bgr", [E, F]), a.sb("bur", [E, F])
        gb = a.sb("gb", [2 * DK, P])
        st, mv, rs = a.sb("st", [P, SB, 6]), a.sb("mv", [P, SB, 2]), a.sb("rs", [P, SB])
        bank = a.ps("bank", [P, 8, 512])
        loaded, zeroed, made = a.sem("loaded"), a.sem("zeroed"), a.sem("made")
        rooted, high = a.sem("rooted"), a.sem("high")
        step, scaled, turned, kept = a.sem("step"), a.sem("scaled"), a.sem("turned"), a.sem("kept")
        ident, identb = w["ident"], w["identb"]
        NLOAD = 13

        jobs = []
        jobs.append(([(wq[:, m, k * P:(k + 1) * P], P, (k * DK + m) * P) for k in range(DK) for m in range(DK)],
                     w["wqT"][:, :, :].rearrange("p k n -> p (k n)"), P))
        jobs.append(([(wkv[:, k * P:(k + 1) * P], P, k * P) for k in range(DK)],
                     w["wkvT"][:, :, :].rearrange("p k n -> p (k n)"), P))
        jobs.append(([(wo[:, m, k * P:(k + 1) * P], P, (k * DK + m) * P) for k in range(DK) for m in range(DK)],
                     w["woT"][:, :, :].rearrange("p k n -> p (k n)"), P))
        jobs.append(([(bgr[:, f * P:(f + 1) * P], E, f * E) for f in range(F // P)],
                     w["bgT"][:, :, :].rearrange("p f e -> p (f e)"), P))
        jobs.append(([(bur[:, f * P:(f + 1) * P], E, f * E) for f in range(F // P)],
                     w["buT"][:, :, :].rearrange("p f e -> p (f e)"), P))
        jobs.append(([(gb[:, :], 2 * DK, 0)], w["gbT"][:, :], P))
        for k in range(DK):
            for h in range(SB // 4):
                jobs.append(([(se[:, 4 * h + j, k * P:(k + 1) * P], P, j * P) for j in range(4)],
                             w["seTh"][:, k, h * 512:(h + 1) * 512], P))

        with nc.Block() as block:
            @block.sync
            def _(sp):
                pm = lambda t: t.rearrange("(m p) d -> p m d", p=P)
                sp.dma_start(wq[:], pm(io["wq"])).then_inc(loaded, 16)
                sp.dma_start(wkv[0:64, :], io["wv"]).then_inc(loaded, 16)
                sp.dma_start(wkv[64:128, :], io["wk"]).then_inc(loaded, 16)
                sp.dma_start(wo[:], pm(io["wo"])).then_inc(loaded, 16)
                sp.dma_start(se[:], pm(io["slot_embeds"].rearrange("e s d -> (e s) d"))).then_inc(loaded, 16)
                sp.dma_start(bgr[:], io["bg"]).then_inc(loaded, 16)
                sp.dma_start(bur[:], io["bu"]).then_inc(loaded, 16)
                for t, v in ((sg, "slot_g"), (sbb, "slot_b")):
                    for h in range(2):
                        sp.dma_start(t[:, h * P:(h + 1) * P],
                                     io[v][h * P:(h + 1) * P].partition_broadcast(P)).then_inc(loaded, 16)
                for i, v in enumerate(("norm_g", "norm_b")):
                    sp.dma_start(gb[i * DK:(i + 1) * DK, :],
                                 io[v].rearrange("(k p) -> k p", p=P)).then_inc(loaded, 16)
                sp.dma_start(sc[:], io["scale"].partition_broadcast(P)).then_inc(loaded, 16)

            @block.gpsimd
            def _(pool):
                nc.gpsimd.memset(w["power"][:], -0.5).then_inc(zeroed, 1)
                nc.gpsimd.memset(ident[:], 0.0).then_inc(zeroed, 1)
                pool.wait_ge(zeroed, 2)
                nc.gpsimd.affine_select(out=ident[:], in_=ident[:], compare_op=ALU.not_equal, fill=1.0, base=0,
                                        pattern=[[-1, P]], channel_multiplier=1).then_inc(made, 1)
                nc.gpsimd.memset(w["causal"][:], 0.0).then_inc(zeroed, 1)
                pool.wait_ge(zeroed, 3)
                tri = w["causal"][:, CH - P:CH]
                nc.gpsimd.affine_select(out=tri, in_=tri, compare_op=ALU.is_ge, fill=LOW, base=0,
                                        pattern=[[-1, P]], channel_multiplier=1).then_inc(made, 1)
                pool.wait_ge(made, 1)
                nc.gpsimd.tensor_copy(identb[:], ident[:]).then_inc(made, 1)
                pool.wait_ge(step, 2 * SB)
                nc.gpsimd.tensor_scalar(rs[:], mv[:, :, 1], EPS, None, ALU.add).then_inc(made, 1)
                pool.wait_ge(made, 4)
                nc.gpsimd.tensor_tensor(rs[:], rs[:], w["power"][:], ALU.pow).then_inc(rooted, 1)

            @block.vector
            def _(dve):
                n = 0

                def after(ins):
                    nonlocal n
                    ins.then_inc(step, 1)
                    n += 1

                dve.wait_ge(loaded, 16 * (NLOAD + 1))
                for t in range(SB):
                    after(nc.vector.bn_stats(st[:, t, :], se[:, t, :]))
                dve.wait_ge(step, n)
                for t in range(SB):
                    after(nc.vector.bn_aggr(mv[:, t, :], st[:, t, :]))
                dve.wait_ge(step, n)
                dve.wait_ge(rooted, 1)
                for t in range(SB):
                    after(nc.vector.tensor_scalar(se[:, t, :], se[:, t, :], mv[:, t, 0:1], rs[:, t:t + 1],
                                                  ALU.subtract, ALU.mult))
                dve.wait_ge(step, n)
                for t in range(SB):
                    after(nc.vector.tensor_tensor(se[:, t, :], se[:, t, :], sg[:], ALU.mult))
                dve.wait_ge(step, n)
                for t in range(SB):
                    after(nc.vector.tensor_tensor(se[:, t, :], se[:, t, :], sbb[:], ALU.add))
                dve.wait_ge(step, n)
                for t in range(SB):
                    nc.vector.tensor_scalar(se[:, t, :], se[:, t, :], sc[:, 0:1], None, ALU.mult).then_inc(scaled, 1)
                for i, (parts, dest, _) in enumerate(jobs):
                    dve.wait_ge(turned, i + 1)
                    src = bank[:, i % 8, 0:dest.shape[1]]
                    if i == 0:
                        for k in range(DK):
                            ins = nc.vector.tensor_copy(
                                w["wqT"][:, k, :].rearrange("p (g d h) -> p g h d", g=NKV, h=GS),
                                bank[:, 0, k * D:(k + 1) * D].rearrange("p (g h d) -> p g h d", g=NKV, h=GS))
                        ins.then_inc(kept, 1)
                    elif i >= 6:
                        nc.vector.tensor_copy(dest, src).then_inc(high, 1)
                        dve.wait_ge(high, i - 5)
                        k, h = divmod(i - 6, 2)
                        nc.vector.tensor_tensor(w["seTl"][:, k, h * 512:(h + 1) * 512], src, dest.bitcast(F32),
                                                ALU.subtract).then_inc(kept, 1)
                    else:
                        nc.vector.tensor_copy(dest, src).then_inc(kept, 1)

            @block.tensor
            def _(pe):
                pe.wait_ge(made, 3)
                pe.wait_ge(loaded, 16 * (NLOAD + 1))
                for i, (parts, dest, _) in enumerate(jobs):
                    if i == 6:
                        pe.wait_ge(scaled, SB)
                    if i >= 8:
                        pe.wait_ge(kept, i - 7)
                    for src, rows, col in parts:
                        last = nc.tensor.transpose(bank[:, i % 8, col:col + rows], src, ident[0:rows, 0:rows])
                    last.then_inc(turned, 1)


def project(nc, w, io, scr):
    with ExitStack() as ctx:
        a = Alloc(nc, ctx, "proj")
        passed = a.sem("passed")
        x = a.sb("x", [P, 2, TPC, D])
        xn = a.sb("xn", [P, 2, TPC, D])
        y = a.sb("y", [P, 2, TPC, D])
        st, mv, rs = a.sb("st", [P, TPC, 6]), a.sb("mv", [P, 2, TPC, 2]), a.sb("rs", [P, 2, TPC])
        xT = a.sb("xT", [P, DK, CH])
        yT = a.sb("yT", [P, 2, DK, CH])
        part = a.sb("part", [P, 2, 3, 3, CH], BF16)
        rest = a.sb("rest", [P, 3, CH])
        vT = a.sb("vT", [64, CH])
        v = a.sb("v", [P, 2, NKV, TPC, VW])
        xTp = a.ps("xTp", [P, DK, CH])
        yTp = a.ps("yTp", [P, DK, CH])
        pj = a.ps("pj", [P, 3, CH])
        vp = a.ps("vp", [P, TPC, 2 * 64])
        sem = a.sem
        x_in = [sem(f"x_in{q}") for q in range(2)]
        out = [sem(f"out{q}") for q in range(2)]
        rs_ready, eps_added = sem("rs_ready"), sem("eps_added")
        ln_step, xn_ready, y_ready = (sem(n) for n in ("ln_step", "xn_ready", "y_ready"))
        xT_ready, xT_kept, yT_ready, yT_kept = (sem(n) for n in ("xT_ready", "xT_kept", "yT_ready", "yT_kept"))
        pj_ready, p1_ready, rest_ready, p2_ready, p3_ready = (
            sem(n) for n in ("pj_ready", "p1_ready", "rest_ready", "p2_ready", "p3_ready"))
        vT_ready, vp_ready, v_ready, v_ones, v_init = (sem(n) for n in ("vT_ready", "vp_ready", "v_ready", "v_ones", "v_init"))
        NOUT = 6
        LN_STEPS = 2 * 2 * TPC
        credits = [(xn_ready, 2 * TPC), (xT_kept, DK), (yT_kept, DK), (rest_ready, 3),
                   (p3_ready, 3), (v_ready, 1), (vp_ready, 1), (out[0], 16 * NOUT), (out[1], 16 * NOUT),
                   (yT_ready, 2 * DK)]
        idn = w["ident"]
        rows = lambda s: slice(64, 128) if s == 2 else slice(0, 128)

        with nc.Block() as block:
            @block.sync
            def _(sp):
                for s, n in credits:
                    sp.sem_inc(s, n)
                load = lambda i, j, q: sp.dma_start(x[:, q], io["x"][i]).then_inc(x_in[q], 16)
                load(0, 0, 0)
                load(1, 0, 1)

                def chunk(i, j, q, more):
                    sp.wait_ge(y_ready, i * TPC + TPC)
                    sp.dma_start(scr["y"][i], y[:, q]).then_inc(out[q], 16)
                    if more:
                        sp.wait_ge(xn_ready, (i + 2) * TPC + TPC)
                        load(i + 2, j + 1, q)
                    wait_apart(sp, p3_ready, 3 * i + 6, passed)
                    for m in range(2):
                        sp.dma_start(scr["q_out"][i, m], part[:, q, m]).then_inc(out[q], 16)
                    sp.dma_start(scr["k_out"][i], part[64:128, q, 2]).then_inc(out[q], 16)
                    sp.wait_ge(v_ready, i + 2)
                    sp.dma_start(scr["v_out"][i], v[:, q].rearrange("p g t c -> p (g t c)")).then_inc(out[q], 16)
                    sp.wait_ge(yT_kept, DK * i + 2 * DK)
                    sp.dma_start(scr["yT_out"][i], yT[:, q]).then_inc(out[q], 16)

                with sp.Fori(0, NCH // 2 - 1) as j:
                    for q in range(2):
                        chunk(2 * j + q, j, q, True)
                for q in range(2):
                    chunk(NCH - 2 + q, NCH // 2 - 1, q, False)
                for q in range(2):
                    sp.wait_ge(out[q], 16 * NOUT * (NCH // 2 + 1))

            @block.vector
            def _(dve):
                nc.vector.memset(v[:], 0.0).then_inc(v_init, 1)
                dve.wait_ge(v_init, 1)
                nc.vector.memset(v[:, :, :, :, HD:HD + 1], 1.0).then_inc(v_ones, 1)

                def norms(i, j, q):
                    base = i * LN_STEPS
                    n = 0
                    dve.wait_ge(x_in[q], 16 * j + 16)
                    for r, src in enumerate((x, xn)):
                        if r:
                            dve.wait_ge(xn_ready, i * TPC + 3 * TPC)
                        for t in range(TPC):
                            nc.vector.bn_stats(st[:, t, :], src[:, q, t]).then_inc(ln_step, 1)
                        n += TPC
                        wait_apart(dve, ln_step, base + n, passed)
                        for t in range(TPC):
                            nc.vector.bn_aggr(mv[:, r, t, :], st[:, t, :]).then_inc(ln_step, 1)
                        n += TPC
                        dve.wait_ge(ln_step, base + n)
                        dve.wait_ge(rs_ready, 2 * i + r + 1)
                        if r == 0:
                            dve.wait_ge(xT_ready, DK * (i - 2) + DK) if not isinstance(i, int) or i >= 2 else None
                        else:
                            dve.wait_ge(out[q], 16 * NOUT * j + 16 * NOUT)
                        dst, ready = ((xn, xn_ready), (y, y_ready))[r]
                        for t in range(TPC):
                            nc.vector.tensor_scalar(dst[:, q, t], src[:, q, t], mv[:, r, t, 0:1], rs[:, r, t:t + 1],
                                                    ALU.subtract, ALU.mult).then_inc(ready, 1)

                def splits(i, q):
                    for s in range(3):
                        dve.wait_ge(p1_ready, 3 * i + s + 1)
                        dve.wait_ge(p3_ready, 3 * i + s + 1)
                        r = rows(s)
                        nc.vector.tensor_tensor(rest[r, s, :], pj[r, s, :], part[r, q, s, 0, :],
                                                ALU.subtract).then_inc(rest_ready, 1)

                norms(0, 0, 0)
                norms(1, 0, 1)
                splits(0, 0)
                with dve.Fori(1, NCH // 2) as j:
                    norms(2 * j, j, 0)
                    splits(2 * j - 1, 1)
                    norms(2 * j + 1, j, 1)
                    splits(2 * j, 0)
                splits(NCH - 1, 1)

            @block.gpsimd
            def _(pool):
                def roots(i, q):
                    for r in range(2):
                        wait_apart(pool, ln_step, i * LN_STEPS + (r + 1) * 2 * TPC, passed)
                        nc.gpsimd.tensor_scalar(rs[:, r], mv[:, r, :, 1], EPS, None, ALU.add).then_inc(eps_added, 1)
                        pool.wait_ge(eps_added, 2 * i + r + 1)
                        nc.gpsimd.tensor_tensor(rs[:, r], rs[:, r], w["power"][:, 0:TPC],
                                                ALU.pow).then_inc(rs_ready, 1)

                def thirds(i, q):
                    for s in range(3):
                        pool.wait_ge(p2_ready, 3 * i + s + 1)
                        pool.wait_ge(p3_ready, 3 * i + s + 3)
                        r = rows(s)
                        nc.gpsimd.tensor_tensor(part[r, q, s, 2, :], rest[r, s, :], part[r, q, s, 1, :],
                                                ALU.subtract).then_inc(p3_ready, 1)
                    pool.wait_ge(p3_ready, 3 * i + 6)

                roots(0, 0)
                roots(1, 1)
                thirds(0, 0)
                with pool.Fori(1, NCH // 2) as j:
                    roots(2 * j, 0)
                    thirds(2 * j - 1, 1)
                    roots(2 * j + 1, 1)
                    thirds(2 * j, 0)
                thirds(NCH - 1, 1)

            @block.scalar
            def _(act):
                act.wait_ge(v_ones, 1)

                def chunk(i, j, q):
                    act.wait_ge(pj_ready, 3 * i) if not isinstance(i, int) or i > 0 else None
                    for k in range(DK):
                        act.wait_ge(xT_ready, DK * i + k + 1)
                        nc.scalar.copy(xT[:, k, :], xTp[:, k, :]).then_inc(xT_kept, 1)
                    act.wait_ge(out[q], 16 * NOUT * j + 16 * NOUT)
                    for s in range(3):
                        r = rows(s)
                        act.wait_ge(pj_ready, 3 * i + s + 1)
                        if s == 2:
                            act.wait_ge(vp_ready, i + 1)
                            nc.scalar.copy(vT[:, :], pj[0:64, 2, :]).then_inc(vT_ready, 1)
                        nc.scalar.copy(part[r, q, s, 0, :], pj[r, s, :]).then_inc(p1_ready, 1)
                    for k in range(DK):
                        act.wait_ge(yT_ready, DK * (i + 2) + k + 1)
                        nc.scalar.activation(yT[:, q, k, :], yTp[:, k, :], ACT.Identity,
                                             scale=w["gbT"][:, k:k + 1],
                                             bias=w["gbT"][:, DK + k:DK + k + 1]).then_inc(yT_kept, 1)
                    for s in range(3):
                        r = rows(s)
                        act.wait_ge(rest_ready, 3 * i + 3 + s + 1)
                        nc.scalar.copy(part[r, q, s, 1, :], rest[r, s, :]).then_inc(p2_ready, 1)
                    act.wait_ge(vp_ready, i + 2)
                    nc.scalar.copy(v[:, q, :, :, 0:HD],
                                   vp[:, :, 0:64].rearrange("p t (g d) -> p g t d", g=NKV)).then_inc(v_ready, 1)

                chunk(0, 0, 0)
                chunk(1, 0, 1)
                with act.Fori(1, NCH // 2) as j:
                    for q in range(2):
                        chunk(2 * j + q, j, q)

            @block.tensor
            def _(pe):
                def chunk(i, q):
                    pe.wait_ge(xn_ready, i * TPC + 3 * TPC)
                    for k in range(DK):
                        pe.wait_ge(xT_kept, DK * i + k + 1)
                        for t in range(TPC):
                            last = nc.tensor.transpose(xTp[:, k, t * P:(t + 1) * P], xn[:, q, t, k * P:(k + 1) * P],
                                                       idn[:])
                        last.then_inc(xT_ready, 1)
                    pe.wait_ge(y_ready, i * TPC + TPC)
                    for k in range(DK):
                        pe.wait_ge(yT_kept, DK * i + k + 1)
                        for t in range(TPC):
                            last = nc.tensor.transpose(yTp[:, k, t * P:(t + 1) * P], y[:, q, t, k * P:(k + 1) * P],
                                                       idn[:])
                        last.then_inc(yT_ready, 1)
                    pe.wait_ge(xT_kept, DK * i + 2 * DK)
                    for s in range(3):
                        pe.wait_ge(rest_ready, 3 * i + s + 1)
                        for k in range(DK):
                            lhsT = w["wqT"][:, k, s * P:(s + 1) * P] if s < 2 else w["wkvT"][:, k, :]
                            last = nc.tensor.matmul(pj[:, s, :], lhsT, xT[:, k, :], start=(k == 0), stop=(k == DK - 1))
                        last.then_inc(pj_ready, 1)
                    pe.wait_ge(v_ready, i + 1)
                    wait_apart(pe, vT_ready, i + 1, passed)
                    for t in range(TPC):
                        last = nc.tensor.transpose(vp[:, t, 0:64], vT[:, t * P:(t + 1) * P], idn[0:64, 0:64])
                    last.then_inc(vp_ready, 1)

                with pe.Fori(0, NCH // 2) as j:
                    for q in range(2):
                        chunk(2 * j + q, q)


def attend(nc, w, scr):
    UNITS = [(c, kb) for c in range(CPB) for kb in range(TPC * (c + 1))]
    NU = len(UNITS)
    MAXES = [(c, h, t, j) for c in range(CPB) for h in range(GS) for t in range(TPC) for j in range(c + 1)]
    NM = len(MAXES)
    MPS = NM // NU
    NBANK = 3
    LEAD = 20
    STEPS = NU * NKV
    ROWS = GS * TPC
    last_max = {}
    for n, (c, h, t, j) in enumerate(MAXES):
        last_max[c] = n + 1
    diag = [u for u, (c, kb) in enumerate(UNITS) if kb >= TPC * c]
    ends = [u for u, (c, kb) in enumerate(UNITS) if kb == TPC * (c + 1) - 1]

    with ExitStack() as ctx:
        a = Alloc(nc, ctx, "att")
        passed = a.sem("passed")
        qs = a.sb("qs", [KR + 2, NKV, CPB, GS * CH], BF16)
        ks = a.sb("ks", [KR + 2, NKV, S], BF16)
        v = a.sb("v", [P, NKV, TPB, VW])
        pr = a.sb("pr", [P, 4, GS, CH])
        junk = a.sb("junk", [P, 2, CH], BF16)
        mx = a.sb("mx", [P, 2, ROWS, CPB])
        nm = a.sb("nm", [P, ROWS])
        nml = a.sb("nml", [P, 2, ROWS], BF16)
        mrow = a.sb("mrow", [2 * ROWS, CPB, P], BF16)
        cT = a.sb("cT", [P, 2, CH])
        rz = a.sb("rz", [P, TPC, GS])
        cn = a.sb("cn", [P, CPB, TPC, GS * HD])
        sT = a.ps("sT", [P, GS, CH])
        mb = a.ps("mb", [P, NBANK, CH])
        acc = a.ps("acc", [P, CH])
        sem = a.sem
        loaded = [sem(f"loaded{g}") for g in range(NKV)]
        m_rows = [sem(f"m_rows{c}") for c in range(CPB)]
        c_out = [sem(f"c_out{c}") for c in range(CPB)]
        (ones_set, sT_ready, exp_done, mask_done, pv_done, mb_ready, mb_used, m_step, nm_ready,
         cT_ready, rz_ready) = (
            sem(n) for n in ("ones_set", "sT_ready", "exp_done", "mask_done", "pv_done", "mb_ready",
                             "mb_used", "m_step", "nm_ready", "cT_ready",
                             "rz_ready"))
        NLD = 2 * len(Q_PART) + 1
        credits = [(exp_done, 2), (pv_done, 4), (mb_used, NBANK), (cT_ready, 1), (rz_ready, 2)] + \
                  [(s, 32) for s in m_rows] + [(s, 16) for s in c_out]

        def m_events(s, limit):
            lo, hi = MPS * (s + LEAD), MPS * (s + LEAD + 1) if s < STEPS else 0
            return [(g, c) for g in range(limit) for c in range(CPB) if lo < g * NM + last_max[c] <= hi]

        def c_events(s, lag):
            return [((s - lag) // NU, UNITS[(s - lag) % NU][0])] if 0 <= s - lag < STEPS and (s - lag) % NU in ends else []

        C_LAG = 3
        TAIL = STEPS + C_LAG + 1
        NMC = NKV * CPB

        def run(step_fn, eng):
            for s in range(-LEAD, 0):
                step_fn(0, s, False, NKV)
            with eng.Fori(0, B - 1) as b:
                for s in range(TAIL):
                    step_fn(b, s, True, NKV + 1)
            for s in range(TAIL):
                step_fn(B - 1, s, True, NKV)

        def maxes_of(s, limit):
            lo = MPS * (s + LEAD)
            return [k for k in range(lo, lo + MPS) if k < limit * NM] if s < STEPS else []
        def entries(s, main, limit):
            xs = [("x", k) for k in maxes_of(s, limit)]
            ms = [("m", g, c) for g, c in m_events(s - 1, limit)]
            cs = [("c", g, c) for g, c in c_events(s, C_LAG)] if main else []
            return xs[:MPS - 1] + ms + cs + xs[MPS - 1:]

        def numbered(steps, main, limit):
            return {e: n for n, e in enumerate(e for s in steps for e in entries(s, main, limit))}

        ahead_no = numbered(range(-LEAD, 0), False, NKV)
        batch_no = {limit: numbered(range(TAIL), True, limit) for limit in (NKV, NKV + 1)}
        PER_BATCH = len(batch_no[NKV + 1])
        assert PER_BATCH % NBANK == 0

        def place(b, s, limit, e):
            if s < 0:
                return ahead_no[e], ahead_no[e] % NBANK
            n = len(ahead_no) + batch_no[limit][e]
            return b * PER_BATCH + n, n % NBANK

        with nc.Block() as block:
            @block.sync
            def _(sp):
                for s, n in credits:
                    sp.sem_inc(s, n)

                def load(b, g):
                    for j in range(len(Q_PART)):
                        r = slice(HD * j, HD * (j + 1))
                        sp.dma_start(qs[r, g], scr["q_in"][b, Q_PART[j], g]).then_inc(loaded[g], 16)
                        sp.dma_start(ks[r, g], scr["k_in"][b, K_PART[j], g]).then_inc(loaded[g], 16)
                    sp.dma_start(v[:, g].rearrange("p (c t) w -> p c (t w)", c=CPB),
                                 scr["v_in"][b, :, g]).then_inc(loaded[g], 16)

                for g in range(NKV):
                    load(0, g)

                def step(b, s, main, limit):
                    for e in entries(s, main, limit):
                        if e[0] == "x":
                            continue
                        kind, g, c = e
                        sp.wait_ge(mb_used, place(b, s, limit, e)[0] + 1 + NBANK)
                        if kind == "m":
                            for hl in range(2):
                                sp.dma_start(qs[KR + hl:KR + hl + 1, g % NKV, c, :],
                                             mrow[hl * ROWS:(hl + 1) * ROWS, c, :]).then_inc(m_rows[c], 16)
                        else:
                            sp.dma_start(scr["ctx_out"][b, c, :, :, g * GS * HD:(g + 1) * GS * HD],
                                         cn[:, c]).then_inc(c_out[c], 16)
                    if main and limit > NKV and s > 0 and s % NU == 0 and s <= STEPS:
                        g = s // NU - 1
                        sp.wait_ge(pv_done, b * STEPS + s + 4)
                        load(b + 1, g)

                run(step, sp)
                for c in range(CPB):
                    sp.wait_ge(c_out[c], 16 * (B * NKV + 1))

            @block.gpsimd
            def _(pool):
                def step(b, s, main, limit):
                    if main and s < STEPS and s % NU in diag:
                        u = s % NU
                        c, kb = UNITS[u]
                        off = (kb - TPC * c) * P
                        wait_apart(pool, exp_done, 2 * (b * STEPS + s) + 4, passed)
                        blk = pr[:, s % 4, :, off:off + P]
                        nc.gpsimd.affine_select(out=blk, in_=blk, compare_op=ALU.is_ge, fill=0.0, base=0,
                                                pattern=[[0, GS], [1, P]],
                                                channel_multiplier=-1).then_inc(mask_done, 1)

                with pool.Fori(0, B) as b:
                    for s in range(STEPS):
                        step(b, s, True, NKV)

            @block.scalar
            def _(act):
                def step(b, s, main, limit):
                    n = b * STEPS + s
                    if main and s < STEPS:
                        c, kb = UNITS[s % NU]
                        off = max(0, kb - TPC * c) * P
                        act.wait_ge(pv_done, n + 1)
                        for hf in range(2):
                            act.wait_ge(sT_ready, 2 * n + hf + 1)
                            nc.scalar.activation(pr[:, s % 4, 2 * hf:2 * hf + 2, off:CH],
                                                 sT[:, 2 * hf:2 * hf + 2, off:CH], ACT.Exp,
                                                 scale=float(HD) ** -0.5).then_inc(exp_done, 1)
                    if main:
                        for g, c in c_events(s, 1):
                            m = b * NMC + g * CPB + c
                            act.wait_ge(pv_done, b * STEPS + s - 1 + 5)
                            act.wait_ge(rz_ready, m + 1)
                            nc.scalar.copy(cT[:, c % 2, :], acc[:, :]).then_inc(cT_ready, 1)

                with act.Fori(0, B) as b:
                    for s in range(STEPS + 2):
                        step(b, s, True, NKV)

            @block.vector
            def _(dve):
                nc.vector.memset(ks[KR:KR + 2, :, :], 1.0).then_inc(ones_set, 1)

                def take_max(k, n, bank):
                    c, h, t, j = MAXES[k % NM]
                    r = h * TPC + t
                    dst = mx[:, c % 2, r, j:j + 1]
                    if j < c:
                        dve.wait_ge(mb_ready, n + 1)
                        nc.vector.tensor_reduce(dst, mb[:, bank, :], AX.X, ALU.max).then_inc(mb_used, 1)
                    else:
                        wd = (t + 1) * P
                        dve.wait_ge(mb_used, n + NBANK - 1)
                        wait_apart(dve, mb_ready, n + 1, passed)
                        nc.vector.tensor_tensor_reduce(junk[:, t % 2, 0:wd], mb[:, bank, 0:wd],
                                                       w["causal"][:, CH - wd:CH], 1.0, LOW, ALU.add, ALU.max,
                                                       dst).then_inc(mb_used, 1)

                def step(b, s, main, limit):
                    for e in entries(s, main, limit):
                        n, bank = place(b, s, limit, e)
                        if e[0] == "x":
                            take_max(e[1], n, bank)
                            continue
                        kind, g, c = e
                        dve.wait_ge(mb_ready, n + 1)
                        if kind == "m":
                            dve.wait_ge(m_rows[c], 32 * (b * NKV + g) + 32)
                            nc.vector.tensor_copy(mrow[:, c, :],
                                                  mb[0:2 * ROWS, bank, 0:P // 2].bitcast(BF16)).then_inc(mb_used, 1)
                        else:
                            ct = mb[:, bank, :].rearrange("p (t h w) -> p t h w", t=TPC, h=GS)
                            dve.wait_ge(mb_used, n + NBANK)
                            nc.vector.reciprocal(rz[:, :, :], ct[:, :, :, HD]).then_inc(rz_ready, 1)
                            dve.wait_ge(rz_ready, b * NMC + g * CPB + c + 3)
                            dve.wait_ge(c_out[c], 16 * (b * NKV + g) + 16)
                            nc.vector.tensor_tensor(cn[:, c].rearrange("p t (h d) -> p t h d", h=GS),
                                                    ct[:, :, :, 0:HD],
                                                    rz[:, :, :].unsqueeze(3).to_broadcast([P, TPC, GS, HD]),
                                                    ALU.mult).then_inc(mb_used, 1)
                    for g, c in m_events(s, limit):
                        n = b * NMC + g * CPB + c
                        last = entries(s, main, limit)[-1]
                        dve.wait_ge(mb_used, place(b, s, limit, last)[0] + 1 + NBANK)
                        nc.vector.tensor_reduce(nm[:], mx[:, c % 2, :, 0:c + 1], AX.X, ALU.max,
                                                negate=True).then_inc(m_step, 1)
                        dve.wait_ge(m_step, 2 * n + 1)
                        nc.vector.tensor_copy(nml[:, 0, :], nm[:]).then_inc(m_step, 1)
                        dve.wait_ge(m_step, 2 * n + 2)
                        nc.vector.tensor_tensor(nml[:, 1, :], nm[:], nml[:, 0, :], ALU.subtract).then_inc(nm_ready, 1)

                run(step, dve)

            @block.tensor
            def _(pe):
                pe.wait_ge(ones_set, 1)

                def fill(b, s, limit, todo):
                    for e in todo:
                        n, bank = place(b, s, limit, e)
                        pe.wait_ge(mb_used, n + 1)
                        if e[0] == "x":
                            k = e[1]
                            g, (c, h, t, j) = k // NM, MAXES[k % NM]
                            if k % NM == 0:
                                pe.wait_ge(loaded[g % NKV], 16 * NLD * (b + g // NKV) + 16 * NLD)
                            q0 = h * CH + t * P
                            wd = CH if j < c else (t + 1) * P
                            last = nc.tensor.matmul(mb[:, bank, 0:wd], qs[0:KR, g % NKV, c, q0:q0 + P],
                                                    ks[0:KR, g % NKV, j * CH:j * CH + wd], start=True, stop=True)
                        elif e[0] == "m":
                            _, g, c = e
                            pe.wait_ge(nm_ready, b * NMC + g * CPB + c + 1)
                            last = nc.tensor.transpose(mb[0:2 * ROWS, bank, 0:P // 2].bitcast(BF16),
                                                       nml[:, :, :].rearrange("p a r -> p (a r)"), w["identb"][:])
                        else:
                            _, g, c = e
                            pe.wait_ge(cT_ready, b * NMC + g * CPB + c + 2)
                            for t in range(TPC):
                                last = nc.tensor.transpose(mb[:, bank, t * P:(t + 1) * P],
                                                           cT[:, c % 2, t * P:(t + 1) * P], w["ident"][:])
                        last.then_inc(mb_ready, 1)

                def values(b, s):
                    c, kb = UNITS[s % NU]
                    g, n = s // NU, b * STEPS + s
                    off = max(0, kb - TPC * c) * P
                    pe.wait_ge(exp_done, 2 * n + 4)
                    if s % NU in diag:
                        pe.wait_ge(mask_done, b * len(diag) * NKV + g * len(diag) + diag.index(s % NU) + 1)
                    if kb == 0:
                        pe.wait_ge(cT_ready, b * NMC + g * CPB + c + 1)
                    for h in range(GS):
                        last = nc.tensor.matmul(acc[VW * h:VW * (h + 1), off:CH], v[:, g, kb, :],
                                                pr[:, s % 4, h, off:CH], start=(kb == 0),
                                                stop=(kb == TPC * (c + 1) - 1), skip_group_check=True)
                    last.then_inc(pv_done, 1)

                def step(b, s, main, limit):
                    todo = entries(s, main, limit)
                    tail = min(1, sum(e[0] == "x" for e in todo))
                    if main and s < STEPS:
                        c, kb = UNITS[s % NU]
                        g, n = s // NU, b * STEPS + s
                        off = max(0, kb - TPC * c) * P
                        if kb == 0:
                            pe.wait_ge(m_rows[c], 32 * (b * NKV + g) + 64)
                        for hf in range(2):
                            pe.wait_ge(exp_done, 2 * n + hf + 1)
                            for h in (2 * hf, 2 * hf + 1):
                                last = nc.tensor.matmul(sT[:, h, off:CH], ks[:, g, kb * P:(kb + 1) * P],
                                                        qs[:, g, c, h * CH + off:(h + 1) * CH], start=True, stop=True)
                            last.then_inc(sT_ready, 1)
                            fill(b, s, limit, todo[hf:hf + 1])
                        fill(b, s, limit, todo[2:len(todo) - tail])
                    else:
                        fill(b, s, limit, todo[:len(todo) - tail])
                    if main and 1 <= s <= STEPS:
                        values(b, s - 1)
                    fill(b, s, limit, todo[len(todo) - tail:])

                run(step, pe)


def dispatch(nc, w, scr):
    HB = SB // 2
    with ExitStack() as ctx:
        a = Alloc(nc, ctx, "dis")
        passed = a.sem("passed")
        yT = a.sb("yT", [P, CPB, DK, CH])
        yTh, yTl = a.sb("yTh", [P, CPB, DK, CH], F32R), a.sb("yTl", [P, CPB, DK, CH], F32R)
        y = a.sb("y", [P, TPB, D + 1])
        lg = a.sb("lg", [P, TPB, NS])
        e1 = a.sb("e1", [P, 2, NS])
        nr = a.sb("nr", [P, TPB])
        zr = a.sb("zr", [P, TPB])
        cm = a.sb("cm", [P, NS])
        ca = a.sb("ca", [P, NS])
        rz = a.sb("rz", [P, SB])
        sl = a.sb("sl", [P, SB, D])
        slT = a.sb("slT", [P, SB, DK, P])
        lp = a.ps("lp", [P, 4, 512])
        dp = a.ps("dp", [P, 4, 512])
        sem = a.sem
        yT_in = [sem(f"yT_in{c}") for c in range(CPB)]
        y_in, e_out0, e_out1, z_out, s_out = (sem(n) for n in ("y_in", "e_out0", "e_out1", "z_out", "s_out"))
        e_out = [e_out0, e_out1]
        (ones_set, lp_ready, lg_ready, nr_ready, cm_done, ca_ready, e1_ready, sub_done, d_ready, d_used,
         half_done, rz_ready, sl_ready, slT_ready, slT_kept) = (
            sem(n) for n in ("ones_set", "lp_ready", "lg_ready", "nr_ready", "cm_done", "ca_ready", "e1_ready",
                             "sub_done", "d_ready", "d_used", "half_done", "rz_ready", "sl_ready", "slT_ready",
                             "slT_kept"))
        sub_v, sub_p = sem("sub_v"), sem("sub_p")
        yT_high, yT_split = sem("yT_high"), sem("yT_split")
        credits = [(d_used, TPB), (slT_kept, DK * SB), (ca_ready, 2), (e_out0, 16), (e_out1, 16),
                   (z_out, 16), (s_out, 16 * 2 * SB), (lg_ready, 2), (sub_p, TPB), (sub_v, TPB)]
        bank = lambda s: (lp if s < HB else dp)[:, s % HB, :]

        with nc.Block() as block:
            @block.sync
            def _(sp):
                for s, n in credits:
                    sp.sem_inc(s, n)

                def slots_out(b):
                    for s in range(SB):
                        sp.wait_ge(slT_kept, DK * (b * SB + SB + s + 1))
                        for k in range(DK):
                            sp.dma_start(scr["slot_out"][b, s, k],
                                         slT[:, s, k, :].rearrange("p (e j) -> p e j", e=2)).then_inc(s_out, 16)

                def batch(b, first):
                    for c in range(CPB):
                        if not first:
                            sp.wait_ge(yT_split, b * CPB)
                        sp.dma_start(yT[:, c], scr["yT_in"][b, c]).then_inc(yT_in[c], 16)
                    if not first:
                        slots_out(b - 1)
                        sp.wait_ge(d_used, b * TPB + TPB)
                    for c in range(CPB):
                        sp.dma_start(y[:, c * TPC:(c + 1) * TPC, 0:D], scr["y_in"][b, c]).then_inc(y_in, 16)
                    for t in range(TPB):
                        sp.wait_ge(e1_ready, b * TPB + t + 1)
                        sp.dma_start(scr["e1"][b, t], e1[:, t % 2]).then_inc(e_out[t % 2], 16)
                    sp.dma_start(scr["zr"][b], zr[:, :]).then_inc(z_out, 16)

                batch(0, True)
                with sp.Fori(1, B) as b:
                    batch(b, False)
                slots_out(B - 1)
                sp.wait_ge(e_out0, 16 * (B * TPB // 2 + 1))
                sp.wait_ge(e_out1, 16 * (B * TPB // 2 + 1))
                sp.wait_ge(z_out, 16 * (B + 1))
                sp.wait_ge(s_out, 16 * 2 * SB * (B + 1))

            @block.scalar
            def _(act):
                with act.Fori(0, B) as b:
                    for t in range(TPB + 1):
                        if t < TPB:
                            act.wait_ge(lp_ready, b * TPB + t + 1)
                            act.wait_ge(d_used, b * TPB + t + 1)
                            nc.scalar.copy(lg[:, t, :], lp[:, 2 * (t % 2):2 * (t % 2) + 2, :]
                                           .rearrange("p a n -> p (a n)")).then_inc(lg_ready, 1)
                        if t > 0:
                            u = t - 1
                            act.wait_ge(nr_ready, b * TPB + u + 1)
                            if u == 0:
                                act.wait_ge(z_out, 16 * b + 16)
                            act.wait_ge(e_out[u % 2], 16 * (b * TPB // 2 + u // 2) + 16)
                            nc.scalar.activation(e1[:, u % 2], lg[:, u, :], ACT.Exp, bias=nr[:, u:u + 1],
                                                 accum_out=zr[:, u:u + 1]).then_inc(e1_ready, 1)
                    for hf in range(2):
                        for t in range(TPB):
                            act.wait_ge(sub_v if t % 2 else sub_p, (b + 1) * TPB + hf * (TPB // 2) + t // 2 + 1)
                            cols = lg[:, t, hf * 512:(hf + 1) * 512]
                            nc.scalar.activation(cols, cols, ACT.Exp).then_inc(d_ready, 1)
                    for s in range(SB):
                        act.wait_ge(slT_ready, b * SB + s + 1)
                        if s == 0:
                            act.wait_ge(s_out, 16 * 2 * SB * b + 16 * 2 * SB)
                        for k in range(DK):
                            nc.scalar.activation(slT[:, s, k, :], bank(s)[:, k * P:(k + 1) * P], ACT.Identity,
                                                 scale=w["gbT"][:, k:k + 1],
                                                 bias=w["gbT"][:, DK + k:DK + k + 1]).then_inc(slT_kept, 1)

            @block.vector
            def _(dve):
                nc.vector.memset(y[:, :, D:D + 1], 1.0).then_inc(ones_set, 1)
                with dve.Fori(0, B) as b:
                    for t in range(TPB):
                        dve.wait_ge(lg_ready, b * TPB + t + 3)
                        if t == 0:
                            dve.wait_ge(ca_ready, 2 * b + 2)
                        nc.vector.tensor_reduce(nr[:, t:t + 1], lg[:, t, :], AX.X, ALU.max,
                                                negate=True).then_inc(nr_ready, 1)
                        if t == 0:
                            nc.vector.tensor_copy(cm[:], lg[:, t, :]).then_inc(cm_done, 1)
                        else:
                            dve.wait_ge(cm_done, b * TPB + t)
                            nc.vector.tensor_tensor(cm[:], cm[:], lg[:, t, :], ALU.max).then_inc(cm_done, 1)
                    for hf in range(2):
                        h = slice(hf * 512, (hf + 1) * 512)
                        dve.wait_ge(ca_ready, 2 * b + hf + 3)
                        for t in range(1, TPB, 2):
                            dve.wait_ge(e1_ready, b * TPB + t + 1)
                            nc.vector.tensor_tensor(lg[:, t, h], lg[:, t, h], ca[:, h],
                                                    ALU.subtract).then_inc(sub_v, 1)
                    for s in range(SB):
                        if s < HB:
                            dve.wait_ge(half_done, b + 1)
                        else:
                            dve.wait_ge(d_used, b * TPB + 2 * TPB)
                        nc.vector.reciprocal(rz[:, s:s + 1], bank(s)[:, D:D + 1]).then_inc(rz_ready, 1)
                        dve.wait_ge(rz_ready, b * SB + s + 1)
                        nc.vector.tensor_scalar(sl[:, s, :], bank(s)[:, 0:D], rz[:, s:s + 1], None,
                                                ALU.mult).then_inc(sl_ready, 1)

            @block.gpsimd
            def _(pool):
                with pool.Fori(0, B) as b:
                    pool.wait_ge(lg_ready, b * TPB + 2)
                    for c in range(CPB):
                        wait_apart(pool, yT_in[c], 16 * b + 16, passed)
                        nc.gpsimd.tensor_copy(yTh[:, c], yT[:, c]).then_inc(yT_high, 1)
                        pool.wait_ge(yT_high, b * CPB + c + 1)
                        nc.gpsimd.tensor_tensor(yTl[:, c], yT[:, c], yTh[:, c].bitcast(F32),
                                                ALU.subtract).then_inc(yT_split, 1)
                    pool.wait_ge(sub_v, (b + 1) * TPB)
                    for hf in range(2):
                        h = slice(hf * 512, (hf + 1) * 512)
                        pool.wait_ge(sub_p, (b + 1) * TPB + hf * (TPB // 2))
                        wait_apart(pool, cm_done, b * TPB + TPB, passed)
                        nc.gpsimd.partition_all_reduce(ca[:, h], cm[:, h], P, RMAX).then_inc(ca_ready, 1)
                        pool.wait_ge(ca_ready, 2 * b + hf + 3)
                        for t in range(0, TPB, 2):
                            pool.wait_ge(e1_ready, b * TPB + t + 1)
                            nc.gpsimd.tensor_tensor(lg[:, t, h], lg[:, t, h], ca[:, h],
                                                    ALU.subtract).then_inc(sub_p, 1)

            @block.tensor
            def _(pe):
                pe.wait_ge(ones_set, 1)
                with pe.Fori(0, B) as b:
                    pe.wait_ge(slT_kept, DK * (b * SB + HB))
                    for t in range(TPB):
                        if t % TPC == 0:
                            pe.wait_ge(yT_split, b * CPB + t // TPC + 1)
                        pe.wait_ge(lg_ready, b * TPB + t + 1)
                        for h in range(2):
                            for k in range(DK):
                                for lhs, rhs in ((yTh, "seTh"), (yTh, "seTl"), (yTl, "seTh")):
                                    last = nc.tensor.matmul(lp[:, 2 * (t % 2) + h, :],
                                                            lhs[:, t // TPC, k, (t % TPC) * P:(t % TPC + 1) * P],
                                                            w[rhs][:, k, h * 512:(h + 1) * 512],
                                                            start=(k == 0 and lhs is yTh and rhs == "seTh"),
                                                            stop=(k == DK - 1 and lhs is yTl))
                        last.then_inc(lp_ready, 1)
                    pe.wait_ge(lg_ready, b * TPB + TPB + 2)
                    pe.wait_ge(slT_kept, DK * (b * SB + SB))
                    pe.wait_ge(y_in, 16 * CPB * b + 16 * CPB)

                    def turn(hf):
                        for s in range(hf * HB, (hf + 1) * HB):
                            pe.wait_ge(sl_ready, b * SB + s + 1)
                            for k in range(DK):
                                last = nc.tensor.transpose(bank(s)[:, k * P:(k + 1) * P], sl[:, s, k * P:(k + 1) * P],
                                                           w["ident"][:])
                            last.then_inc(slT_ready, 1)

                    for hf in range(2):
                        for t in range(TPB):
                            pe.wait_ge(d_ready, (2 * b + hf) * TPB + t + 1)
                            if hf and t == 3:
                                turn(0)
                            for s in range(hf * HB, (hf + 1) * HB):
                                last = nc.tensor.matmul(bank(s)[:, 0:D + 1], lg[:, t, s * P:(s + 1) * P], y[:, t, :],
                                                        start=(t == 0), stop=(t == TPB - 1))
                            if hf:
                                last.then_inc(d_used, 1)
                        if hf == 0:
                            last.then_inc(half_done, 1)
                    turn(1)


def experts(nc, w, io, scr):
    FB = F // P
    RB = B * SL // P
    with ExitStack() as ctx:
        a = Alloc(nc, ctx, "exp")
        wg, wu = a.sb("wg", [P, 2, DK, F]), a.sb("wu", [P, 2, DK, F])
        wd = a.sb("wd", [P, 2, FB, D])
        sl = a.sb("sl", [P, 2, DK, B * SL])
        bd = a.sb("bd", [P, 2, D])
        bg, bu = a.sb("bg", [P, 2, FB]), a.sb("bu", [P, 2, FB])
        gate = a.sb("gate", [P, 2, FB, B * SL])
        h = a.sb("h", [P, 2, FB, B * SL])
        eo = a.sb("eo", [P, 2, RB, D])
        gp = a.ps("gp", [P, FB, B * SL])
        up = a.ps("up", [P, FB, B * SL])
        op = a.ps("op", [P, 2, RB, D])
        sem = a.sem
        gu_in = [sem(f"gu_in{q}") for q in range(2)]
        down_in = [sem(f"down_in{q}") for q in range(2)]
        out = [sem(f"out{q}") for q in range(2)]
        bias_ready, gu_ready, gate_ready, h_ready, o_ready, eo_ready = (
            sem(n) for n in ("bias_ready", "gu_ready", "gate_ready", "h_ready", "o_ready", "eo_ready"))
        NGU, NDN = 3, 2
        credits = [(gu_ready, 2), (gate_ready, FB), (h_ready, FB), (o_ready, 2), (eo_ready, 2 * RB),
                   (out[0], 16 * B), (out[1], 16 * B)]

        with nc.Block() as block:
            @block.sync
            def _(sp):
                for s, n in credits:
                    sp.sem_inc(s, n)

                def load_gu(e, q):
                    sp.wait_ge(gu_ready, 2 * e)
                    for dst, src in ((sl[:, q], scr["slot_in"][e]), (wg[:, q], io["Wg"][e]), (wu[:, q], io["Wu"][e])):
                        sp.dma_start(dst, src).then_inc(gu_in[q], 16)

                def load_down(e, q):
                    sp.wait_ge(o_ready, e + 1)
                    sp.wait_ge(eo_ready, RB * (e + 1))
                    for dst, src in ((wd[:, q], io["Wd"][e]), (bd[:, q], io["bd"][e].partition_broadcast(P))):
                        sp.dma_start(dst, src).then_inc(down_in[q], 16)

                def store(e, q):
                    sp.wait_ge(eo_ready, RB * (e + 3))
                    for b in range(B):
                        r = slice(SL * (b % 2), SL * (b % 2) + SL)
                        sp.dma_start(scr["eo_out"][e, b], eo[r, q, b // 2, :]).then_inc(out[q], 16)

                sp_first = ((sl[:, 0], scr["slot_in"][0]), (wg[:, 0], io["Wg"][0]), (wu[:, 0], io["Wu"][0]))
                for dst, src in sp_first:
                    sp.dma_start(dst, src).then_inc(gu_in[0], 16)
                load_gu(1, 1)
                load_down(0, 0)
                load_gu(2, 0)
                load_down(1, 1)
                with sp.Fori(1, E // 2 - 1) as j:
                    for q in range(2):
                        e = 2 * j + q
                        load_gu(e + 1, 1 - q)
                        store(e - 2, q)
                        load_down(e, q)
                load_gu(E - 1, 1)
                store(E - 4, 0)
                load_down(E - 2, 0)
                store(E - 3, 1)
                load_down(E - 1, 1)
                store(E - 2, 0)
                store(E - 1, 1)
                for q in range(2):
                    sp.wait_ge(out[q], 16 * B * (E // 2 + 1))

            @block.scalar
            def _(act):
                with act.Fori(0, E // 2) as j:
                    for q in range(2):
                        e = 2 * j + q
                        act.wait_ge(bias_ready, 2 * e + 1)
                        for f in range(FB):
                            act.wait_ge(gu_ready, 2 * e + f // 2 + 3)
                            nc.scalar.activation(gate[:, q, f, :], gp[:, f, :], ACT.Gelu,
                                                 bias=bg[:, q, f:f + 1]).then_inc(gate_ready, 1)

            @block.vector
            def _(dve):
                def hidden(e, q):
                    nc.vector.tensor_copy(bg[:, q, :], w["bgT"][:, :, bass.ds(e, 1)].rearrange("p f o -> p (f o)")
                                          ).then_inc(bias_ready, 1)
                    nc.vector.tensor_copy(bu[:, q, :], w["buT"][:, :, bass.ds(e, 1)].rearrange("p f o -> p (f o)")
                                          ).then_inc(bias_ready, 1)
                    dve.wait_ge(bias_ready, 2 * e + 2)
                    dve.wait_ge(o_ready, e + 1)
                    for f in range(FB):
                        dve.wait_ge(gate_ready, FB * e + FB + f + 1)
                        dve.wait_ge(gu_ready, 2 * e + f // 2 + 3)
                        nc.vector.scalar_tensor_tensor(out=h[:, q, f, :], in0=up[:, f, :], scalar=bu[:, q, f:f + 1],
                                                       in1=gate[:, q, f, :], op0=ALU.add,
                                                       op1=ALU.mult).then_inc(h_ready, 1)

                def output(e, j, q):
                    dve.wait_ge(o_ready, e + 3)
                    dve.wait_ge(down_in[q], 16 * NDN * j + 16 * NDN)
                    dve.wait_ge(out[q], 16 * B * j + 16 * B)
                    for r in range(RB):
                        nc.vector.tensor_tensor(eo[:, q, r, :], op[:, q, r, :], bd[:, q, :],
                                                ALU.add).then_inc(eo_ready, 1)

                hidden(0, 0)
                with dve.Fori(0, E // 2 - 1) as j:
                    hidden(2 * j + 1, 1)
                    output(2 * j, j, 0)
                    hidden(2 * j + 2, 0)
                    output(2 * j + 1, j, 1)
                hidden(E - 1, 1)
                output(E - 2, E // 2 - 1, 0)
                output(E - 1, E // 2 - 1, 1)

            @block.tensor
            def _(pe):
                def gate_up(e, j, q):
                    pe.wait_ge(gu_in[q], 16 * NGU * j + 16 * NGU)
                    for half in range(FB // 2):
                        pe.wait_ge(gate_ready, FB * e + 2 * half + 2)
                        pe.wait_ge(h_ready, FB * e + 2 * half + 2)
                        for f in (2 * half, 2 * half + 1):
                            for dst, wt in ((gp, wg), (up, wu)):
                                for k in range(DK):
                                    last = nc.tensor.matmul(dst[:, f, :], wt[:, q, k, f * P:(f + 1) * P],
                                                            sl[:, q, k, :], start=(k == 0), stop=(k == DK - 1))
                        last.then_inc(gu_ready, 1)

                def down(e, j, q):
                    pe.wait_ge(down_in[q], 16 * NDN * j + 16 * NDN)
                    pe.wait_ge(h_ready, FB * e + 2 * FB)
                    pe.wait_ge(eo_ready, RB * (e + 1))
                    for r in range(RB):
                        for f in range(FB):
                            last = nc.tensor.matmul(op[:, q, r, :], h[:, q, f, r * P:(r + 1) * P], wd[:, q, f, :],
                                                    start=(f == 0), stop=(f == FB - 1))
                    last.then_inc(o_ready, 1)

                gate_up(0, 0, 0)
                with pe.Fori(0, E // 2 - 1) as j:
                    gate_up(2 * j + 1, j, 1)
                    down(2 * j, j, 0)
                    gate_up(2 * j + 2, j + 1, 0)
                    down(2 * j + 1, j, 1)
                gate_up(E - 1, E // 2 - 1, 1)
                down(E - 2, E // 2 - 1, 0)
                down(E - 1, E // 2 - 1, 1)


def combine(nc, w, io, scr):
    NB = 4
    with ExitStack() as ctx:
        a = Alloc(nc, ctx, "com")
        eo = a.sb("eo", [P, B, SB, D])
        eoh, eol = a.sb("eoh", [P, B, SB, D], F32R), a.sb("eol", [P, B, SB, D], F32R)
        woh, wol = a.sb("woh", [P, DK, D], F32R), a.sb("wol", [P, DK, D], F32R)
        e1 = a.sb("e1", [P, NB, NS])
        c = a.sb("c", [P, NB, D])
        x = a.sb("x", [P, NB, D])
        e1h, e1l = a.sb("e1h", [P, 2, SB, P], F32R), a.sb("e1l", [P, 2, SB, P], F32R)
        ch, cl = a.sb("ch", [P, 2, DK, P], F32R), a.sb("cl", [P, 2, DK, P], F32R)
        zr, rz = a.sb("zr", [P, TPB]), a.sb("rz", [P, TPB])
        part = a.sb("part", [P, 2, D])
        o = a.sb("o", [P, 2, D])
        tp = a.ps("tp", [P, 2, 3, 512])
        mp = a.ps("mp", [P, 2, 512])
        sem = a.sem
        in_ = [sem(f"in{q}") for q in range(NB)]
        x_in = [sem(f"x_in{q}") for q in range(NB)]
        out = [sem(f"out{q}") for q in range(2)]
        (z_in, turned, e1h_kept, e1l_kept, ch_kept, cl_kept, m_ready, rz_ready, part_ready, o_ready,
         wo_high, wo_split, eo_high, eo_split) = (
            sem(n) for n in ("z_in", "turned", "e1h_kept", "e1l_kept", "ch_kept", "cl_kept", "m_ready", "rz_ready",
                             "part_ready", "o_ready", "wo_high", "wo_split", "eo_high", "eo_split"))
        eo_in = [sem(f"eo_in{b}") for b in range(B)]
        credits = [(turned, NB), (e1l_kept, 2), (cl_kept, 2), (m_ready, 2), (o_ready, NB), (rz_ready, 1),
                   (out[0], 16), (out[1], 16)]
        H2 = TPB // 2
        with nc.Block() as block:
            @block.sync
            def _(sp):
                for s, n in credits:
                    sp.sem_inc(s, n)
                with sp.Fori(0, B) as b:
                    for t in range(TPB):
                        q = t % NB
                        n = b * TPB + t
                        sp.wait_ge(turned, n + 1)
                        sp.dma_start(e1[:, q], scr["e1"][b, t]).then_inc(in_[q], 16)
                        sp.dma_start(c[:, q], scr["ctx_in"][b, t]).then_inc(in_[q], 16)
                        sp.wait_ge(o_ready, n + 1)
                        sp.dma_start(x[:, q], io["x_tile"][b, t]).then_inc(x_in[q], 16)
                        if t == 0:
                            sp.wait_ge(rz_ready, b + 1)
                            sp.dma_start(zr[:], scr["zr"][b]).then_inc(z_in, 16)

            @block.scalar
            def _(act):
                def store(b, t):
                    act.wait_ge(o_ready, b * TPB + t + 1 + NB)
                    act.dma_start(io["out_tile"][b, t], o[:, t % 2]).then_inc(out[t % 2], 16)

                act.dma_start(eo[:, 0], scr["eo_in"][0]).then_inc(eo_in[0], 16)
                act.wait_ge(turned, NB + 1)
                for b in range(1, B):
                    act.dma_start(eo[:, b], scr["eo_in"][b]).then_inc(eo_in[b], 16)
                with act.Fori(0, B) as b:
                    for t in range(TPB):
                        q = t % 2
                        n = b * TPB + t
                        act.wait_ge(turned, n + 1 + NB)
                        act.wait_ge(m_ready, n + 1)
                        nc.scalar.copy(e1h[:, q].rearrange("p s n -> p (s n)"),
                                       tp[:, q, 0:2, :].rearrange("p a n -> p (a n)")).then_inc(e1h_kept, 1)
                        if t > 1:
                            store(b, t - 2)
                    for t in (TPB - 2, TPB - 1):
                        store(b, t)
                for q in range(2):
                    act.wait_ge(out[q], 16 * (B * H2 + 1))

            @block.vector
            def _(dve):
                with dve.Fori(0, B) as b:
                    for t in range(TPB + 1):
                        n = b * TPB + t
                        if t < TPB:
                            q = t % 2
                            dve.wait_ge(turned, n + 1 + NB)
                            dve.wait_ge(m_ready, n + 1)
                            nc.vector.tensor_copy(ch[:, q].rearrange("p k n -> p (k n)"),
                                                  tp[:, q, 2, 0:D]).then_inc(ch_kept, 1)
                            dve.wait_ge(ch_kept, n + 1)
                            nc.vector.tensor_tensor(cl[:, q].rearrange("p k n -> p (k n)"), tp[:, q, 2, 0:D],
                                                    ch[:, q].rearrange("p k n -> p (k n)").bitcast(F32),
                                                    ALU.subtract).then_inc(cl_kept, 1)
                            dve.wait_ge(e1h_kept, n + 1)
                            nc.vector.tensor_tensor(e1l[:, q].rearrange("p s n -> p (s n)"),
                                                    tp[:, q, 0:2, :].rearrange("p a n -> p (a n)"),
                                                    e1h[:, q].rearrange("p s n -> p (s n)").bitcast(F32),
                                                    ALU.subtract).then_inc(e1l_kept, 1)
                        if t == 0:
                            dve.wait_ge(z_in, 16 * b + 16)
                            nc.vector.reciprocal(rz[:], zr[:]).then_inc(rz_ready, 1)
                            dve.wait_ge(rz_ready, b + 2)
                        if t > 0:
                            u, q = t - 1, (t - 1) % 2
                            n = b * TPB + u
                            dve.wait_ge(m_ready, n + 3)
                            dve.wait_ge(x_in[u % NB], 16 * (b * (TPB // NB) + u // NB) + 16)
                            nc.vector.scalar_tensor_tensor(out=part[:, q, :], in0=mp[:, q, 0:D],
                                                           scalar=rz[:, u:u + 1], in1=x[:, u % NB, :], op0=ALU.mult,
                                                           op1=ALU.add).then_inc(part_ready, 1)
                            dve.wait_ge(part_ready, n + 1)
                            dve.wait_ge(out[q], 16 * (b * H2 + u // 2) + 16)
                            nc.vector.tensor_tensor(o[:, q, :], part[:, q, :], mp[:, q, D:2 * D],
                                                    ALU.add).then_inc(o_ready, 1)

            @block.gpsimd
            def _(pool):
                nc.gpsimd.tensor_copy(woh[:], w["woT"][:]).then_inc(wo_high, 1)
                pool.wait_ge(wo_high, 1)
                nc.gpsimd.tensor_tensor(wol[:], w["woT"][:], woh[:].bitcast(F32), ALU.subtract).then_inc(wo_split, 1)
                for b in range(B):
                    pool.wait_ge(eo_in[b], 16)
                    nc.gpsimd.tensor_copy(eoh[:, b], eo[:, b]).then_inc(eo_high, 1)
                    pool.wait_ge(eo_high, b + 1)
                    nc.gpsimd.tensor_tensor(eol[:, b], eo[:, b], eoh[:, b].bitcast(F32),
                                            ALU.subtract).then_inc(eo_split, 1)

            @block.tensor
            def _(pe):
                pe.wait_ge(wo_split, 1)
                with pe.Fori(0, B) as b:
                    for t in range(TPB + 1):
                        if t < TPB:
                            q = t % 2
                            n = b * TPB + t
                            pe.wait_ge(in_[t % NB], 32 * (b * (TPB // NB) + t // NB) + 32)
                            pe.wait_ge(e1l_kept, n + 1)
                            pe.wait_ge(cl_kept, n + 1)
                            for s in range(SB):
                                nc.tensor.transpose(tp[:, q, s // 4, (s % 4) * P:(s % 4 + 1) * P],
                                                    e1[:, t % NB, s * P:(s + 1) * P], w["ident"][:])
                            for k in range(DK):
                                last = nc.tensor.transpose(tp[:, q, 2, k * P:(k + 1) * P], c[:, t % NB, k * P:(k + 1) * P],
                                                           w["ident"][:])
                            last.then_inc(turned, 1)
                        if t > 0:
                            u, q = t - 1, (t - 1) % 2
                            n = b * TPB + u
                            if u == 0:
                                pe.wait_ge(eo_split, b + 1)
                            pe.wait_ge(o_ready, n - 1 + NB)
                            pe.wait_ge(cl_kept, n + 3)
                            for k in range(DK):
                                for lhs, rhs in ((ch, woh), (ch, wol), (cl, woh)):
                                    nc.tensor.matmul(mp[:, q, D:2 * D], lhs[:, q, k, :], rhs[:, k, :],
                                                     start=(k == 0 and rhs is woh and lhs is ch),
                                                     stop=(k == DK - 1 and lhs is cl))
                            pe.wait_ge(e1l_kept, n + 3)
                            for s in range(SB):
                                for lhs, rhs in ((e1h, eoh), (e1h, eol), (e1l, eoh)):
                                    last = nc.tensor.matmul(mp[:, q, 0:D], lhs[:, q, s, :], rhs[:, b, s, :],
                                                            start=(s == 0 and rhs is eoh and lhs is e1h),
                                                            stop=(s == SB - 1 and lhs is e1l))
                            last.then_inc(m_ready, 1)


def block_kernel(nc, x, wq, wk, wv, wo, norm_g, norm_b, slot_g, slot_b, scale, slot_embeds,
                 Wg, bg, Wu, bu, Wd, bd, out):
    def dram(name, shape, dt=F32):
        return nc.dram_tensor(name, shape, dt, kind="Internal").ap()

    q_d = dram("q_parts", [3, NCH, D, CH], BF16)
    k_d = dram("k_parts", [3, NKV * HD, TOK], BF16)
    v_d = dram("v_rows", [NCH, P, NKV, TPC * VW])
    y_d = dram("y_rows", [NCH, P, TPC, D])
    yT_d = dram("y_cols", [NCH, P, DK, CH])
    c_d = dram("context", [B, S, D])
    e_d = dram("slot_exps", [B, TPB, P, NS])
    z_d = dram("slot_sums", [B, P, TPB])
    s_d = dram("slots", [E, P, DK, B * SL])
    o_d = dram("expert_out", [B, NS, D])
    io = {
        "x": x.rearrange("b (c t p) d -> (b c) p t d", p=P, t=TPC),
        "x_tile": x.rearrange("b (n p) d -> b n p d", p=P),
        "out_tile": out.rearrange("b (n p) d -> b n p d", p=P),
        "wq": wq, "wk": wk, "wv": wv, "wo": wo, "norm_g": norm_g, "norm_b": norm_b, "slot_g": slot_g,
        "slot_b": slot_b, "scale": scale, "slot_embeds": slot_embeds, "bg": bg, "bu": bu, "bd": bd,
        "Wg": Wg.rearrange("e (k p) f -> e p k f", p=P), "Wu": Wu.rearrange("e (k p) f -> e p k f", p=P),
        "Wd": Wd.rearrange("e (k p) o -> e p k o", p=P),
    }
    scr = {
        "q_out": q_d.rearrange("a i (m p) t -> i m p a t", p=P),
        "q_in": q_d.rearrange("a (b c) (g d h) t -> b a g d c (h t)", g=NKV, h=GS, b=B),
        "k_out": k_d.rearrange("a p (i t) -> i p a t", t=CH),
        "k_in": k_d.rearrange("a (g d) (b s) -> b a g d s", g=NKV, b=B),
        "v_out": v_d.rearrange("i p g x -> i p (g x)"),
        "v_in": v_d.rearrange("(b c) p g x -> b p g c x", b=B),
        "y": y_d, "y_in": y_d.rearrange("(b c) p t d -> b c p t d", b=B),
        "yT_out": yT_d, "yT_in": yT_d.rearrange("(b c) p k t -> b c p k t", b=B),
        "ctx_out": c_d.rearrange("b (c t p) d -> b c p t d", p=P, t=TPC),
        "ctx_in": c_d.rearrange("b (n p) d -> b n p d", p=P),
        "e1": e_d, "zr": z_d,
        "slot_out": s_d.rearrange("(s e) p k (b j) -> b s k p e j", e=2, b=B),
        "slot_in": s_d,
        "eo_out": o_d.rearrange("b (e j) d -> e b j d", e=E),
        "eo_in": o_d.rearrange("b (s p) d -> b p s d", p=P),
    }
    with ExitStack() as ctx:
        a = Alloc(nc, ctx, "w")
        w = {
            "ident": a.sb("ident", [P, P]), "identb": a.sb("identb", [P, P], BF16), "causal": a.sb("causal", [P, CH]),
            "wqT": a.sb("wqT", [P, DK, D]), "wkvT": a.sb("wkvT", [P, DK, P]), "woT": a.sb("woT", [P, DK, D]),
            "seTh": a.sb("seTh", [P, DK, NS], F32R), "seTl": a.sb("seTl", [P, DK, NS], F32R),
            "bgT": a.sb("bgT", [P, F // P, E]), "buT": a.sb("buT", [P, F // P, E]),
            "power": a.sb("power", [P, SB]), "gbT": a.sb("gbT", [P, 2 * DK]),
        }
        prepare(nc, w, io)
        project(nc, w, io, scr)
        attend(nc, w, scr)
        dispatch(nc, w, scr)
        experts(nc, w, io, scr)
        combine(nc, w, io, scr)


_INS = ['L0_attn_x', 'L0_attn_wq', 'L0_attn_wk', 'L0_attn_wv', 'L0_attn_wo', 'L0_ffn_norm_g', 'L0_ffn_norm_b',
        'L0_ffn_slot_g', 'L0_ffn_slot_b', 'L0_ffn_scale', 'L0_ffn_slot_embeds', 'L0_ffn_Wg', 'L0_ffn_bg',
        'L0_ffn_Wu', 'L0_ffn_bu', 'L0_ffn_Wd', 'L0_ffn_bd']
_OUTS = [((B, S, D), 'float32')]


def kernel(**inputs):
    import numpy as _np
    import concourse.bacc as _bacc
    from concourse import mybir as _mybir
    from concourse.bass_utils import run_bass_kernel_spmd as _run

    nc = _bacc.Bacc("TRN2", target_bir_lowering=False, num_devices=1)
    arrays, args = {}, []
    for name in _INS:
        a = _np.ascontiguousarray(inputs[name])
        arrays[f"in_{name}_dram"] = a
        args.append(nc.dram_tensor(f"in_{name}_dram", a.shape, _mybir.dt.from_np(a.dtype), kind="ExternalInput").ap())
    for i, (shape, dtype) in enumerate(_OUTS):
        dt = _mybir.dt.from_np(_np.dtype(dtype))
        args.append(nc.dram_tensor(f"out_{i}_dram", shape, dt, kind="ExternalOutput").ap())
    block_kernel(nc, *args)
    r = _run(nc, [arrays], core_ids=[0])
    got = tuple(r.results[0][f"out_{i}_dram"] for i in range(len(_OUTS)))
    return got[0]
```

```python
from contextlib import ExitStack

import concourse.bass as bass
from concourse import mybir

ALU = mybir.AluOpType
ACT = mybir.ActivationFunctionType
AX = mybir.AxisListType
F32 = mybir.dt.float32
BF16 = mybir.dt.bfloat16
F32R = mybir.dt.float32r
RMAX = bass.bass_isa.ReduceOp.max

P = 128
B, S, D = 4, 2048, 256
NH, NKV, HD = 16, 4, 16
GS = NH // NKV
E, SL, F = 16, 64, 512
NS = E * SL
DK = D // P
EPS = 1e-5
LOW = -3.0e38
TOK = B * S
CH = 512
TPC = CH // P
CPB = S // CH
NCH = TOK // CH
TPB = S // P
SB = NS // P
Q_PART = (0, 0, 1, 1, 0, 2)
K_PART = (0, 1, 0, 1, 2, 0)
KR = HD * len(Q_PART)
VW = 32


class Alloc:

    def __init__(self, nc, ctx, tag):
        self.nc, self.ctx, self.tag = nc, ctx, tag

    def sb(self, name, shape, dt=F32):
        return self.ctx.enter_context(self.nc.sbuf_tensor(f"{self.tag}_{name}", shape, dt))

    def ps(self, name, shape, dt=F32):
        return self.ctx.enter_context(self.nc.psum_tensor(f"{self.tag}_{name}", shape, dt))

    def sem(self, name):
        return self.ctx.enter_context(self.nc.semaphore(f"{self.tag}_{name}"))


def wait_apart(eng, sem, value, passed):
    eng.wait_ge(sem, value)
    eng.sem_inc(passed, 1)


def prepare(nc, w, io):
    with ExitStack() as ctx:
        a = Alloc(nc, ctx, "prep")
        wq, wo = a.sb("wq", [P, DK, D]), a.sb("wo", [P, DK, D])
        wkv = a.sb("wkv", [P, D])
        se = a.sb("se", [P, SB, D])
        sg, sbb, sc = a.sb("sg", [P, D]), a.sb("sbb", [P, D]), a.sb("sc", [P, 1])
        bgr, bur = a.sb("bgr", [E, F]), a.sb("bur", [E, F])
        gb = a.sb("gb", [2 * DK, P])
        st, mv, rs = a.sb("st", [P, SB, 6]), a.sb("mv", [P, SB, 2]), a.sb("rs", [P, SB])
        bank = a.ps("bank", [P, 8, 512])
        loaded, zeroed, made = a.sem("loaded"), a.sem("zeroed"), a.sem("made")
        rooted, high = a.sem("rooted"), a.sem("high")
        step, scaled, turned, kept = a.sem("step"), a.sem("scaled"), a.sem("turned"), a.sem("kept")
        ident, identb = w["ident"], w["identb"]
        NLOAD = 13

        jobs = []
        jobs.append(([(wq[:, m, k * P:(k + 1) * P], P, (k * DK + m) * P) for k in range(DK) for m in range(DK)],
                     w["wqT"][:, :, :].rearrange("p k n -> p (k n)"), P))
        jobs.append(([(wkv[:, k * P:(k + 1) * P], P, k * P) for k in range(DK)],
                     w["wkvT"][:, :, :].rearrange("p k n -> p (k n)"), P))
        jobs.append(([(wo[:, m, k * P:(k + 1) * P], P, (k * DK + m) * P) for k in range(DK) for m in range(DK)],
                     w["woT"][:, :, :].rearrange("p k n -> p (k n)"), P))
        jobs.append(([(bgr[:, f * P:(f + 1) * P], E, f * E) for f in range(F // P)],
                     w["bgT"][:, :, :].rearrange("p f e -> p (f e)"), P))
        jobs.append(([(bur[:, f * P:(f + 1) * P], E, f * E) for f in range(F // P)],
                     w["buT"][:, :, :].rearrange("p f e -> p (f e)"), P))
        jobs.append(([(gb[:, :], 2 * DK, 0)], w["gbT"][:, :], P))
        for k in range(DK):
            for h in range(SB // 4):
                jobs.append(([(se[:, 4 * h + j, k * P:(k + 1) * P], P, j * P) for j in range(4)],
                             w["seTh"][:, k, h * 512:(h + 1) * 512], P))

        with nc.Block() as block:
            @block.sync
            def _(sp):
                pm = lambda t: t.rearrange("(m p) d -> p m d", p=P)
                sp.dma_start(wq[:], pm(io["wq"])).then_inc(loaded, 16)
                sp.dma_start(wkv[0:64, :], io["wv"]).then_inc(loaded, 16)
                sp.dma_start(wkv[64:128, :], io["wk"]).then_inc(loaded, 16)
                sp.dma_start(wo[:], pm(io["wo"])).then_inc(loaded, 16)
                sp.dma_start(se[:], pm(io["slot_embeds"].rearrange("e s d -> (e s) d"))).then_inc(loaded, 16)
                sp.dma_start(bgr[:], io["bg"]).then_inc(loaded, 16)
                sp.dma_start(bur[:], io["bu"]).then_inc(loaded, 16)
                for t, v in ((sg, "slot_g"), (sbb, "slot_b")):
                    for h in range(2):
                        sp.dma_start(t[:, h * P:(h + 1) * P],
                                     io[v][h * P:(h + 1) * P].partition_broadcast(P)).then_inc(loaded, 16)
                for i, v in enumerate(("norm_g", "norm_b")):
                    sp.dma_start(gb[i * DK:(i + 1) * DK, :],
                                 io[v].rearrange("(k p) -> k p", p=P)).then_inc(loaded, 16)
                sp.dma_start(sc[:], io["scale"].partition_broadcast(P)).then_inc(loaded, 16)

            @block.gpsimd
            def _(pool):
                nc.gpsimd.memset(w["power"][:], -0.5).then_inc(zeroed, 1)
                nc.gpsimd.memset(ident[:], 0.0).then_inc(zeroed, 1)
                pool.wait_ge(zeroed, 2)
                nc.gpsimd.affine_select(out=ident[:], in_=ident[:], compare_op=ALU.not_equal, fill=1.0, base=0,
                                        pattern=[[-1, P]], channel_multiplier=1).then_inc(made, 1)
                nc.gpsimd.memset(w["causal"][:], 0.0).then_inc(zeroed, 1)
                pool.wait_ge(zeroed, 3)
                tri = w["causal"][:, CH - P:CH]
                nc.gpsimd.affine_select(out=tri, in_=tri, compare_op=ALU.is_ge, fill=LOW, base=0,
                                        pattern=[[-1, P]], channel_multiplier=1).then_inc(made, 1)
                pool.wait_ge(made, 1)
                nc.gpsimd.tensor_copy(identb[:], ident[:]).then_inc(made, 1)
                pool.wait_ge(step, 2 * SB)
                nc.gpsimd.tensor_scalar(rs[:], mv[:, :, 1], EPS, None, ALU.add).then_inc(made, 1)
                pool.wait_ge(made, 4)
                nc.gpsimd.tensor_tensor(rs[:], rs[:], w["power"][:], ALU.pow).then_inc(rooted, 1)

            @block.vector
            def _(dve):
                n = 0

                def after(ins):
                    nonlocal n
                    ins.then_inc(step, 1)
                    n += 1

                dve.wait_ge(loaded, 16 * (NLOAD + 1))
                for t in range(SB):
                    after(nc.vector.bn_stats(st[:, t, :], se[:, t, :]))
                dve.wait_ge(step, n)
                for t in range(SB):
                    after(nc.vector.bn_aggr(mv[:, t, :], st[:, t, :]))
                dve.wait_ge(step, n)
                dve.wait_ge(rooted, 1)
                for t in range(SB):
                    after(nc.vector.tensor_scalar(se[:, t, :], se[:, t, :], mv[:, t, 0:1], rs[:, t:t + 1],
                                                  ALU.subtract, ALU.mult))
                dve.wait_ge(step, n)
                for t in range(SB):
                    after(nc.vector.tensor_tensor(se[:, t, :], se[:, t, :], sg[:], ALU.mult))
                dve.wait_ge(step, n)
                for t in range(SB):
                    after(nc.vector.tensor_tensor(se[:, t, :], se[:, t, :], sbb[:], ALU.add))
                dve.wait_ge(step, n)
                for t in range(SB):
                    nc.vector.tensor_scalar(se[:, t, :], se[:, t, :], sc[:, 0:1], None, ALU.mult).then_inc(scaled, 1)
                for i, (parts, dest, _) in enumerate(jobs):
                    dve.wait_ge(turned, i + 1)
                    src = bank[:, i % 8, 0:dest.shape[1]]
                    if i == 0:
                        for k in range(DK):
                            ins = nc.vector.tensor_copy(
                                w["wqT"][:, k, :].rearrange("p (g d h) -> p g h d", g=NKV, h=GS),
                                bank[:, 0, k * D:(k + 1) * D].rearrange("p (g h d) -> p g h d", g=NKV, h=GS))
                        ins.then_inc(kept, 1)
                    elif i >= 6:
                        nc.vector.tensor_copy(dest, src).then_inc(high, 1)
                        dve.wait_ge(high, i - 5)
                        k, h = divmod(i - 6, 2)
                        nc.vector.tensor_tensor(w["seTl"][:, k, h * 512:(h + 1) * 512], src, dest.bitcast(F32),
                                                ALU.subtract).then_inc(kept, 1)
                    else:
                        nc.vector.tensor_copy(dest, src).then_inc(kept, 1)

            @block.tensor
            def _(pe):
                pe.wait_ge(made, 3)
                pe.wait_ge(loaded, 16 * (NLOAD + 1))
                for i, (parts, dest, _) in enumerate(jobs):
                    if i == 6:
                        pe.wait_ge(scaled, SB)
                    if i >= 8:
                        pe.wait_ge(kept, i - 7)
                    for src, rows, col in parts:
                        last = nc.tensor.transpose(bank[:, i % 8, col:col + rows], src, ident[0:rows, 0:rows])
                    last.then_inc(turned, 1)


def project(nc, w, io, scr):
    with ExitStack() as ctx:
        a = Alloc(nc, ctx, "proj")
        passed = a.sem("passed")
        x = a.sb("x", [P, 2, TPC, D])
        xn = a.sb("xn", [P, 2, TPC, D])
        y = a.sb("y", [P, 2, TPC, D])
        st, mv, rs = a.sb("st", [P, 2, TPC, 6]), a.sb("mv", [P, 2, 2, TPC, 2]), a.sb("rs", [P, 2, 2, TPC])
        xT = a.sb("xT", [P, 2, DK, CH])
        yT = a.sb("yT", [P, 2, DK, CH])
        part = a.sb("part", [P, 2, 3, 3, CH], BF16)
        rest = a.sb("rest", [P, 3, CH])
        vT = a.sb("vT", [64, CH])
        v = a.sb("v", [P, 2, NKV, TPC, VW])
        xTp = a.ps("xTp", [P, DK, CH])
        yTp = a.ps("yTp", [P, DK, CH])
        pj = a.ps("pj", [P, 3, CH])
        vp = a.ps("vp", [P, TPC, 2 * 64])
        sem = a.sem
        x_in = [sem(f"x_in{q}") for q in range(2)]
        out = [sem(f"out{q}") for q in range(2)]
        st_done = [sem(f"st_done{r}") for r in range(2)]
        rs_ready = [sem(f"rs_ready{r}") for r in range(2)]
        eps_added = [sem(f"eps_added{r}") for r in range(2)]
        xn_ready, y_ready = sem("xn_ready"), sem("y_ready")
        xT_ready, xT_kept, yT_ready, yT_kept = (sem(n) for n in ("xT_ready", "xT_kept", "yT_ready", "yT_kept"))
        pj_ready, p1_ready, rest_ready, p2_ready, p3_ready = (
            sem(n) for n in ("pj_ready", "p1_ready", "rest_ready", "p2_ready", "p3_ready"))
        vT_ready, vp_ready, v_ready, v_ones, v_init = (sem(n) for n in ("vT_ready", "vp_ready", "v_ready", "v_ones", "v_init"))
        NOUT = 6
        LAST = NCH - 1
        credits = [(xn_ready, 2 * TPC), (xT_kept, DK), (yT_kept, DK), (rest_ready, 3),
                   (p3_ready, 3), (v_ready, 1), (vp_ready, 1), (out[0], 16 * NOUT), (out[1], 16 * NOUT),
                   (yT_ready, 2 * DK)]
        idn = w["ident"]
        rows = lambda s: slice(64, 128) if s == 2 else slice(0, 128)

        def steps(step, eng):
            step(0, 0, 0)
            step(1, 0, 1)
            with eng.Fori(1, NCH // 2 - 2) as j:
                for q in range(2):
                    step(2 * j + q, j, q)
            for i in range(NCH - 4, NCH):
                step(i, i // 2, i % 2)

        known = lambda i: isinstance(i, int)

        with nc.Block() as block:
            @block.sync
            def _(sp):
                for s, n in credits:
                    sp.sem_inc(s, n)
                for i in range(2):
                    sp.dma_start(x[:, i], io["x"][i]).then_inc(x_in[i], 16)

                def chunk(i, j, q):
                    sp.wait_ge(y_ready, i * TPC + TPC)
                    sp.dma_start(scr["y"][i], y[:, q]).then_inc(out[q], 16)
                    wait_apart(sp, p3_ready, 3 * i + 6, passed)
                    for m in range(2):
                        sp.dma_start(scr["q_out"][i, m], part[:, q, m]).then_inc(out[q], 16)
                    sp.dma_start(scr["k_out"][i], part[64:128, q, 2]).then_inc(out[q], 16)
                    sp.wait_ge(yT_kept, DK * i + 2 * DK)
                    sp.dma_start(scr["yT_out"][i], yT[:, q]).then_inc(out[q], 16)
                    sp.wait_ge(v_ready, i + 2)
                    sp.dma_start(scr["v_out"][i], v[:, q].rearrange("p g t c -> p (g t c)")).then_inc(out[q], 16)

                with sp.Fori(0, NCH // 2) as j:
                    for q in range(2):
                        chunk(2 * j + q, j, q)
                for q in range(2):
                    sp.wait_ge(out[q], 16 * NOUT * (NCH // 2 + 1))

            @block.vector
            def _(dve):
                nc.vector.memset(v[:], 0.0).then_inc(v_init, 1)
                dve.wait_ge(v_init, 1)
                nc.vector.memset(v[:, :, :, :, HD:HD + 1], 1.0).then_inc(v_ones, 1)

                def stats(r, i, j, q):
                    src = (x, xn)[r]
                    if r == 0:
                        dve.wait_ge(x_in[q], 16 * j + 16)
                    else:
                        dve.wait_ge(xn_ready, i * TPC + 3 * TPC)
                    if not known(i) or i > 0:
                        dve.wait_ge(st_done[r], i * 2 * TPC)
                    for t in range(TPC):
                        nc.vector.bn_stats(st[:, r, t, :], src[:, q, t]).then_inc(st_done[r], 1)
                    wait_apart(dve, st_done[r], i * 2 * TPC + TPC, passed)
                    for t in range(TPC):
                        nc.vector.bn_aggr(mv[:, r, q, t, :], st[:, r, t, :]).then_inc(st_done[r], 1)

                def norm(r, i, j, q):
                    src, dst, ready = ((x, xn, xn_ready), (xn, y, y_ready))[r]
                    dve.wait_ge(st_done[r], i * 2 * TPC + 2 * TPC)
                    dve.wait_ge(rs_ready[r], i + 1)
                    if r == 1:
                        dve.wait_ge(out[q], 16 * NOUT * j + 16 * NOUT)
                    elif not known(i) or i >= 2:
                        dve.wait_ge(y_ready, TPC * (i - 1))
                        dve.wait_ge(xT_ready, DK * (i - 1))
                    for t in range(TPC):
                        nc.vector.tensor_scalar(dst[:, q, t], src[:, q, t], mv[:, r, q, t, 0:1],
                                                rs[:, r, q, t:t + 1], ALU.subtract, ALU.mult).then_inc(ready, 1)

                def splits(i, q):
                    for s in range(3):
                        dve.wait_ge(p1_ready, 3 * i + s + 1)
                        dve.wait_ge(p3_ready, 3 * i + s + 1)
                        r = rows(s)
                        nc.vector.tensor_tensor(rest[r, s, :], pj[r, s, :], part[r, q, s, 0, :],
                                                ALU.subtract).then_inc(rest_ready, 1)

                def step(i, j, q):
                    if not known(i) or i + 2 <= LAST:
                        stats(0, i + 2, j + 1, q)
                    if not known(i) or i + 1 <= LAST:
                        norm(0, i + 1, j + q, 1 - q)
                        stats(1, i + 1, j + q, 1 - q)
                    splits(i, q)
                    if not known(i) or i + 1 <= LAST:
                        norm(1, i + 1, j + q, 1 - q)

                stats(0, 0, 0, 0)
                stats(0, 1, 0, 1)
                norm(0, 0, 0, 0)
                stats(1, 0, 0, 0)
                norm(1, 0, 0, 0)
                steps(step, dve)

            @block.gpsimd
            def _(pool):
                def roots(r, i, q):
                    wait_apart(pool, st_done[r], i * 2 * TPC + 2 * TPC, passed)
                    nc.gpsimd.tensor_scalar(rs[:, r, q], mv[:, r, q, :, 1], EPS, None, ALU.add).then_inc(eps_added[r], 1)
                    pool.wait_ge(eps_added[r], i + 1)
                    nc.gpsimd.tensor_tensor(rs[:, r, q], rs[:, r, q], w["power"][:, 0:TPC],
                                            ALU.pow).then_inc(rs_ready[r], 1)

                def thirds(i, q):
                    for s in range(3):
                        pool.wait_ge(p2_ready, 3 * i + s + 1)
                        pool.wait_ge(p3_ready, 3 * i + s + 3)
                        r = rows(s)
                        nc.gpsimd.tensor_tensor(part[r, q, s, 2, :], rest[r, s, :], part[r, q, s, 1, :],
                                                ALU.subtract).then_inc(p3_ready, 1)
                    pool.wait_ge(p3_ready, 3 * i + 6)

                def step(i, j, q):
                    if not known(i) or i + 2 <= LAST:
                        roots(0, i + 2, q)
                    if not known(i) or i + 1 <= LAST:
                        roots(1, i + 1, 1 - q)
                    thirds(i, q)

                roots(0, 0, 0)
                roots(0, 1, 1)
                roots(1, 0, 0)
                steps(step, pool)

            @block.scalar
            def _(act):
                act.wait_ge(v_ones, 1)

                def x_turned(i, j, q):
                    if not known(i) or i >= 2:
                        act.wait_ge(pj_ready, 3 * (i - 1))
                    for k in range(DK):
                        act.wait_ge(xT_ready, DK * i + k + 1)
                        nc.scalar.copy(xT[:, q, k, :], xTp[:, k, :]).then_inc(xT_kept, 1)
                    if not known(i) or i + 2 <= LAST:
                        act.wait_ge(xn_ready, i * TPC + 3 * TPC)
                        act.dma_start(x[:, q], io["x"][i + 2]).then_inc(x_in[q], 16)

                def values(i, q):
                    act.wait_ge(vp_ready, i + 2)
                    nc.scalar.copy(v[:, q, :, :, 0:HD],
                                   vp[:, :, 0:64].rearrange("p t (g d) -> p g t d", g=NKV)).then_inc(v_ready, 1)

                def step(i, j, q):
                    if not known(i) or i >= 1:
                        values(i - 1, 1 - q)
                    act.wait_ge(out[q], 16 * NOUT * j + 16 * NOUT)
                    for s in range(3):
                        r = rows(s)
                        act.wait_ge(pj_ready, 3 * i + s + 1)
                        if s == 2:
                            act.wait_ge(vp_ready, i + 1)
                            nc.scalar.copy(vT[:, :], pj[0:64, 2, :]).then_inc(vT_ready, 1)
                        nc.scalar.copy(part[r, q, s, 0, :], pj[r, s, :]).then_inc(p1_ready, 1)
                    if not known(i) or i + 1 <= LAST:
                        x_turned(i + 1, j + q, 1 - q)
                    for s in range(3):
                        r = rows(s)
                        act.wait_ge(rest_ready, 3 * i + 3 + s + 1)
                        nc.scalar.copy(part[r, q, s, 1, :], rest[r, s, :]).then_inc(p2_ready, 1)
                    for k in range(DK):
                        act.wait_ge(yT_ready, DK * (i + 2) + k + 1)
                        nc.scalar.activation(yT[:, q, k, :], yTp[:, k, :], ACT.Identity,
                                             scale=w["gbT"][:, k:k + 1],
                                             bias=w["gbT"][:, DK + k:DK + k + 1]).then_inc(yT_kept, 1)

                x_turned(0, 0, 0)
                steps(step, act)
                values(LAST, LAST % 2)

            @block.tensor
            def _(pe):
                def turn_x(i, q):
                    pe.wait_ge(xn_ready, i * TPC + 3 * TPC)
                    for k in range(DK):
                        pe.wait_ge(xT_kept, DK * i + k + 1)
                        for t in range(TPC):
                            last = nc.tensor.transpose(xTp[:, k, t * P:(t + 1) * P], xn[:, q, t, k * P:(k + 1) * P],
                                                       idn[:])
                        last.then_inc(xT_ready, 1)

                def turn_y(i, q):
                    pe.wait_ge(y_ready, i * TPC + TPC)
                    for k in range(DK):
                        pe.wait_ge(yT_kept, DK * i + k + 1)
                        for t in range(TPC):
                            last = nc.tensor.transpose(yTp[:, k, t * P:(t + 1) * P], y[:, q, t, k * P:(k + 1) * P],
                                                       idn[:])
                        last.then_inc(yT_ready, 1)

                def products(i, q):
                    pe.wait_ge(xT_kept, DK * i + 2 * DK)
                    for s in range(3):
                        pe.wait_ge(rest_ready, 3 * i + s + 1)
                        for k in range(DK):
                            lhsT = w["wqT"][:, k, s * P:(s + 1) * P] if s < 2 else w["wkvT"][:, k, :]
                            last = nc.tensor.matmul(pj[:, s, :], lhsT, xT[:, q, k, :], start=(k == 0),
                                                    stop=(k == DK - 1))
                        last.then_inc(pj_ready, 1)

                def turn_v(i):
                    pe.wait_ge(v_ready, i + 1)
                    wait_apart(pe, vT_ready, i + 1, passed)
                    for t in range(TPC):
                        last = nc.tensor.transpose(vp[:, t, 0:64], vT[:, t * P:(t + 1) * P], idn[0:64, 0:64])
                    last.then_inc(vp_ready, 1)

                def step(i, j, q):
                    if not known(i) or i >= 1:
                        turn_v(i - 1)
                    products(i, q)
                    if not known(i) or i + 1 <= LAST:
                        turn_x(i + 1, 1 - q)
                    turn_y(i, q)

                turn_x(0, 0)
                steps(step, pe)
                turn_v(LAST)


def attend(nc, w, scr):
    UNITS = [(c, kb) for c in range(CPB) for kb in range(TPC * (c + 1))]
    NU = len(UNITS)
    MAXES = [(c, h, t, j) for c in range(CPB) for h in range(GS) for t in range(TPC) for j in range(c + 1)]
    NM = len(MAXES)
    MPS = NM // NU
    NBANK = 3
    LEAD = 20
    STEPS = NU * NKV
    ROWS = GS * TPC
    last_max = {}
    for n, (c, h, t, j) in enumerate(MAXES):
        last_max[c] = n + 1
    diag = [u for u, (c, kb) in enumerate(UNITS) if kb >= TPC * c]
    ends = [u for u, (c, kb) in enumerate(UNITS) if kb == TPC * (c + 1) - 1]

    with ExitStack() as ctx:
        a = Alloc(nc, ctx, "att")
        passed = a.sem("passed")
        qs = a.sb("qs", [KR + 2, NKV, CPB, GS * CH], BF16)
        ks = a.sb("ks", [KR + 2, NKV, S], BF16)
        v = a.sb("v", [P, NKV, TPB, VW])
        pr = a.sb("pr", [P, 4, GS, CH])
        junk = a.sb("junk", [P, 2, CH], BF16)
        mx = a.sb("mx", [P, 2, ROWS, CPB])
        nm = a.sb("nm", [P, ROWS])
        nml = a.sb("nml", [P, 2, ROWS], BF16)
        mrow = a.sb("mrow", [2 * ROWS, CPB, P], BF16)
        cT = a.sb("cT", [P, 2, CH])
        rz = a.sb("rz", [P, TPC, GS])
        cn = a.sb("cn", [P, CPB, TPC, GS * HD])
        sT = a.ps("sT", [P, GS, CH])
        mb = a.ps("mb", [P, NBANK, CH])
        acc = a.ps("acc", [P, CH])
        sem = a.sem
        loaded = [sem(f"loaded{g}") for g in range(NKV)]
        m_rows = [sem(f"m_rows{c}") for c in range(CPB)]
        c_out = [sem(f"c_out{c}") for c in range(CPB)]
        (ones_set, sT_ready, exp_done, mask_done, pv_done, mb_ready, mb_used, m_step, nm_ready,
         cT_ready, rz_ready) = (
            sem(n) for n in ("ones_set", "sT_ready", "exp_done", "mask_done", "pv_done", "mb_ready",
                             "mb_used", "m_step", "nm_ready", "cT_ready",
                             "rz_ready"))
        NLD = 2 * len(Q_PART) + 1
        credits = [(exp_done, 2), (pv_done, 4), (mb_used, NBANK), (cT_ready, 1), (rz_ready, 2)] + \
                  [(s, 32) for s in m_rows] + [(s, 16) for s in c_out]

        def m_events(s, limit):
            lo, hi = MPS * (s + LEAD), MPS * (s + LEAD + 1) if s < STEPS else 0
            return [(g, c) for g in range(limit) for c in range(CPB) if lo < g * NM + last_max[c] <= hi]

        def c_events(s, lag):
            return [((s - lag) // NU, UNITS[(s - lag) % NU][0])] if 0 <= s - lag < STEPS and (s - lag) % NU in ends else []

        C_LAG = 3
        TAIL = STEPS + C_LAG + 1
        NMC = NKV * CPB

        def run(step_fn, eng):
            for s in range(-LEAD, 0):
                step_fn(0, s, False, NKV)
            with eng.Fori(0, B - 1) as b:
                for s in range(TAIL):
                    step_fn(b, s, True, NKV + 1)
            for s in range(TAIL):
                step_fn(B - 1, s, True, NKV)

        def maxes_of(s, limit):
            lo = MPS * (s + LEAD)
            return [k for k in range(lo, lo + MPS) if k < limit * NM] if s < STEPS else []
        def entries(s, main, limit):
            xs = [("x", k) for k in maxes_of(s, limit)]
            ms = [("m", g, c) for g, c in m_events(s - 1, limit)]
            cs = [("c", g, c) for g, c in c_events(s, C_LAG)] if main else []
            return xs[:MPS - 1] + ms + cs + xs[MPS - 1:]

        def numbered(steps, main, limit):
            return {e: n for n, e in enumerate(e for s in steps for e in entries(s, main, limit))}

        ahead_no = numbered(range(-LEAD, 0), False, NKV)
        batch_no = {limit: numbered(range(TAIL), True, limit) for limit in (NKV, NKV + 1)}
        PER_BATCH = len(batch_no[NKV + 1])
        assert PER_BATCH % NBANK == 0

        def place(b, s, limit, e):
            if s < 0:
                return ahead_no[e], ahead_no[e] % NBANK
            n = len(ahead_no) + batch_no[limit][e]
            return b * PER_BATCH + n, n % NBANK

        with nc.Block() as block:
            @block.sync
            def _(sp):
                for s, n in credits:
                    sp.sem_inc(s, n)

                def load(b, g):
                    for j in range(len(Q_PART)):
                        r = slice(HD * j, HD * (j + 1))
                        sp.dma_start(qs[r, g], scr["q_in"][b, Q_PART[j], g]).then_inc(loaded[g], 16)
                        sp.dma_start(ks[r, g], scr["k_in"][b, K_PART[j], g]).then_inc(loaded[g], 16)
                    sp.dma_start(v[:, g].rearrange("p (c t) w -> p c (t w)", c=CPB),
                                 scr["v_in"][b, :, g]).then_inc(loaded[g], 16)

                for g in range(NKV):
                    load(0, g)

                def step(b, s, main, limit):
                    for e in entries(s, main, limit):
                        if e[0] == "x":
                            continue
                        kind, g, c = e
                        sp.wait_ge(mb_used, place(b, s, limit, e)[0] + 1 + NBANK)
                        if kind == "m":
                            for hl in range(2):
                                sp.dma_start(qs[KR + hl:KR + hl + 1, g % NKV, c, :],
                                             mrow[hl * ROWS:(hl + 1) * ROWS, c, :]).then_inc(m_rows[c], 16)
                        else:
                            sp.dma_start(scr["ctx_out"][b, c, :, :, g * GS * HD:(g + 1) * GS * HD],
                                         cn[:, c]).then_inc(c_out[c], 16)
                    if main and limit > NKV and s > 0 and s % NU == 0 and s <= STEPS:
                        g = s // NU - 1
                        sp.wait_ge(pv_done, b * STEPS + s + 4)
                        load(b + 1, g)

                run(step, sp)
                for c in range(CPB):
                    sp.wait_ge(c_out[c], 16 * (B * NKV + 1))

            @block.gpsimd
            def _(pool):
                def step(b, s, main, limit):
                    if main and s < STEPS and s % NU in diag:
                        u = s % NU
                        c, kb = UNITS[u]
                        off = (kb - TPC * c) * P
                        wait_apart(pool, exp_done, 2 * (b * STEPS + s) + 4, passed)
                        blk = pr[:, s % 4, :, off:off + P]
                        nc.gpsimd.affine_select(out=blk, in_=blk, compare_op=ALU.is_ge, fill=0.0, base=0,
                                                pattern=[[0, GS], [1, P]],
                                                channel_multiplier=-1).then_inc(mask_done, 1)

                with pool.Fori(0, B) as b:
                    for s in range(STEPS):
                        step(b, s, True, NKV)

            @block.scalar
            def _(act):
                def step(b, s, main, limit):
                    n = b * STEPS + s
                    if main and s < STEPS:
                        c, kb = UNITS[s % NU]
                        off = max(0, kb - TPC * c) * P
                        act.wait_ge(pv_done, n + 1)
                        for hf in range(2):
                            act.wait_ge(sT_ready, 2 * n + hf + 1)
                            nc.scalar.activation(pr[:, s % 4, 2 * hf:2 * hf + 2, off:CH],
                                                 sT[:, 2 * hf:2 * hf + 2, off:CH], ACT.Exp,
                                                 scale=float(HD) ** -0.5).then_inc(exp_done, 1)
                    if main:
                        for g, c in c_events(s, 1):
                            m = b * NMC + g * CPB + c
                            act.wait_ge(pv_done, b * STEPS + s - 1 + 5)
                            act.wait_ge(rz_ready, m + 1)
                            nc.scalar.copy(cT[:, c % 2, :], acc[:, :]).then_inc(cT_ready, 1)

                with act.Fori(0, B) as b:
                    for s in range(STEPS + 2):
                        step(b, s, True, NKV)

            @block.vector
            def _(dve):
                nc.vector.memset(ks[KR:KR + 2, :, :], 1.0).then_inc(ones_set, 1)

                def take_max(k, n, bank):
                    c, h, t, j = MAXES[k % NM]
                    r = h * TPC + t
                    dst = mx[:, c % 2, r, j:j + 1]
                    if j < c:
                        dve.wait_ge(mb_ready, n + 1)
                        nc.vector.tensor_reduce(dst, mb[:, bank, :], AX.X, ALU.max).then_inc(mb_used, 1)
                    else:
                        wd = (t + 1) * P
                        dve.wait_ge(mb_used, n + NBANK - 1)
                        wait_apart(dve, mb_ready, n + 1, passed)
                        nc.vector.tensor_tensor_reduce(junk[:, t % 2, 0:wd], mb[:, bank, 0:wd],
                                                       w["causal"][:, CH - wd:CH], 1.0, LOW, ALU.add, ALU.max,
                                                       dst).then_inc(mb_used, 1)

                def step(b, s, main, limit):
                    for e in entries(s, main, limit):
                        n, bank = place(b, s, limit, e)
                        if e[0] == "x":
                            take_max(e[1], n, bank)
                            continue
                        kind, g, c = e
                        dve.wait_ge(mb_ready, n + 1)
                        if kind == "m":
                            dve.wait_ge(m_rows[c], 32 * (b * NKV + g) + 32)
                            nc.vector.tensor_copy(mrow[:, c, :],
                                                  mb[0:2 * ROWS, bank, 0:P // 2].bitcast(BF16)).then_inc(mb_used, 1)
                        else:
                            ct = mb[:, bank, :].rearrange("p (t h w) -> p t h w", t=TPC, h=GS)
                            dve.wait_ge(mb_used, n + NBANK)
                            nc.vector.reciprocal(rz[:, :, :], ct[:, :, :, HD]).then_inc(rz_ready, 1)
                            dve.wait_ge(rz_ready, b * NMC + g * CPB + c + 3)
                            dve.wait_ge(c_out[c], 16 * (b * NKV + g) + 16)
                            nc.vector.tensor_tensor(cn[:, c].rearrange("p t (h d) -> p t h d", h=GS),
                                                    ct[:, :, :, 0:HD],
                                                    rz[:, :, :].unsqueeze(3).to_broadcast([P, TPC, GS, HD]),
                                                    ALU.mult).then_inc(mb_used, 1)
                    for g, c in m_events(s, limit):
                        n = b * NMC + g * CPB + c
                        last = entries(s, main, limit)[-1]
                        dve.wait_ge(mb_used, place(b, s, limit, last)[0] + 1 + NBANK)
                        nc.vector.tensor_reduce(nm[:], mx[:, c % 2, :, 0:c + 1], AX.X, ALU.max,
                                                negate=True).then_inc(m_step, 1)
                        dve.wait_ge(m_step, 2 * n + 1)
                        nc.vector.tensor_copy(nml[:, 0, :], nm[:]).then_inc(m_step, 1)
                        dve.wait_ge(m_step, 2 * n + 2)
                        nc.vector.tensor_tensor(nml[:, 1, :], nm[:], nml[:, 0, :], ALU.subtract).then_inc(nm_ready, 1)

                run(step, dve)

            @block.tensor
            def _(pe):
                pe.wait_ge(ones_set, 1)

                def fill(b, s, limit, todo):
                    for e in todo:
                        n, bank = place(b, s, limit, e)
                        pe.wait_ge(mb_used, n + 1)
                        if e[0] == "x":
                            k = e[1]
                            g, (c, h, t, j) = k // NM, MAXES[k % NM]
                            if k % NM == 0:
                                pe.wait_ge(loaded[g % NKV], 16 * NLD * (b + g // NKV) + 16 * NLD)
                            q0 = h * CH + t * P
                            wd = CH if j < c else (t + 1) * P
                            last = nc.tensor.matmul(mb[:, bank, 0:wd], qs[0:KR, g % NKV, c, q0:q0 + P],
                                                    ks[0:KR, g % NKV, j * CH:j * CH + wd], start=True, stop=True)
                        elif e[0] == "m":
                            _, g, c = e
                            pe.wait_ge(nm_ready, b * NMC + g * CPB + c + 1)
                            last = nc.tensor.transpose(mb[0:2 * ROWS, bank, 0:P // 2].bitcast(BF16),
                                                       nml[:, :, :].rearrange("p a r -> p (a r)"), w["identb"][:])
                        else:
                            _, g, c = e
                            pe.wait_ge(cT_ready, b * NMC + g * CPB + c + 2)
                            for t in range(TPC):
                                last = nc.tensor.transpose(mb[:, bank, t * P:(t + 1) * P],
                                                           cT[:, c % 2, t * P:(t + 1) * P], w["ident"][:])
                        last.then_inc(mb_ready, 1)

                def values(b, s):
                    c, kb = UNITS[s % NU]
                    g, n = s // NU, b * STEPS + s
                    off = max(0, kb - TPC * c) * P
                    pe.wait_ge(exp_done, 2 * n + 4)
                    if s % NU in diag:
                        pe.wait_ge(mask_done, b * len(diag) * NKV + g * len(diag) + diag.index(s % NU) + 1)
                    if kb == 0:
                        pe.wait_ge(cT_ready, b * NMC + g * CPB + c + 1)
                    for h in range(GS):
                        last = nc.tensor.matmul(acc[VW * h:VW * (h + 1), off:CH], v[:, g, kb, :],
                                                pr[:, s % 4, h, off:CH], start=(kb == 0),
                                                stop=(kb == TPC * (c + 1) - 1), skip_group_check=True)
                    last.then_inc(pv_done, 1)

                def step(b, s, main, limit):
                    todo = entries(s, main, limit)
                    tail = min(1, sum(e[0] == "x" for e in todo))
                    if main and s < STEPS:
                        c, kb = UNITS[s % NU]
                        g, n = s // NU, b * STEPS + s
                        off = max(0, kb - TPC * c) * P
                        if kb == 0:
                            pe.wait_ge(m_rows[c], 32 * (b * NKV + g) + 64)
                        for hf in range(2):
                            pe.wait_ge(exp_done, 2 * n + hf + 1)
                            for h in (2 * hf, 2 * hf + 1):
                                last = nc.tensor.matmul(sT[:, h, off:CH], ks[:, g, kb * P:(kb + 1) * P],
                                                        qs[:, g, c, h * CH + off:(h + 1) * CH], start=True, stop=True)
                            last.then_inc(sT_ready, 1)
                            fill(b, s, limit, todo[hf:hf + 1])
                        fill(b, s, limit, todo[2:len(todo) - tail])
                    else:
                        fill(b, s, limit, todo[:len(todo) - tail])
                    if main and 1 <= s <= STEPS:
                        values(b, s - 1)
                    fill(b, s, limit, todo[len(todo) - tail:])

                run(step, pe)


def dispatch(nc, w, scr):
    HB = SB // 2
    with ExitStack() as ctx:
        a = Alloc(nc, ctx, "dis")
        passed = a.sem("passed")
        yT = a.sb("yT", [P, 2, DK, CH])
        yTh, yTl = a.sb("yTh", [P, CPB, DK, CH], F32R), a.sb("yTl", [P, CPB, DK, CH], F32R)
        y = a.sb("y", [P, 2, TPC, D])
        yh, yl = a.sb("yh", [P, TPB, D + 2], F32R), a.sb("yl", [P, TPB, D + 2], F32R)
        ND = 3
        dh, dl = a.sb("dh", [P, ND, 512], F32R), a.sb("dl", [P, ND, 512], F32R)
        lg = a.sb("lg", [P, TPB, NS])
        e1 = a.sb("e1", [P, 2, NS])
        nr = a.sb("nr", [P, TPB])
        zr = a.sb("zr", [P, TPB])
        cm = a.sb("cm", [P, NS])
        ca = a.sb("ca", [P, NS])
        rz = a.sb("rz", [P, SB])
        sl = a.sb("sl", [P, HB, D])
        slT = a.sb("slT", [P, HB, DK, P])
        lp = a.ps("lp", [P, 4, 512])
        dp = a.ps("dp", [P, 4, 512])
        sem = a.sem
        yT_in = [sem(f"yT_in{c}") for c in range(CPB)]
        y_in = [sem(f"y_in{c}") for c in range(CPB)]
        e_out0, e_out1, z_out, s_out = (sem(n) for n in ("e_out0", "e_out1", "z_out", "s_out"))
        e_out = [e_out0, e_out1]
        (ones_set, lp_ready, lg_ready, nr_ready, cm_done, ca_ready, e1_ready, d_ready, rz_ready, sl_ready, slT_ready, slT_kept) = (
            sem(n) for n in ("ones_set", "lp_ready", "lg_ready", "nr_ready", "cm_done", "ca_ready", "e1_ready",
                             "d_ready", "rz_ready", "sl_ready", "slT_ready",
                             "slT_kept"))
        sub_v, sub_p = sem("sub_v"), sem("sub_p")
        yT_high, yT_split, y_high, y_split = sem("yT_high"), sem("yT_split"), sem("y_high"), sem("y_split")
        dh_ready, dl_ready, d_free = sem("dh_ready"), sem("dl_ready"), sem("d_free")
        credits = [(dl_ready, TPB), (slT_kept, DK * SB), (ca_ready, 2), (e_out0, 16), (e_out1, 16),
                   (z_out, 16), (s_out, 16 * 2 * SB), (lg_ready, 2), (sub_p, TPB), (sub_v, TPB), (d_free, 2)]
        bank = lambda s: (lp if s < HB else dp)[:, s % HB, :]

        with nc.Block() as block:
            @block.sync
            def _(sp):
                for s, n in credits:
                    sp.sem_inc(s, n)

                def slots_out(b):
                    for s in range(SB):
                        sp.wait_ge(slT_kept, DK * (b * SB + SB + s + 1))
                        for k in range(DK):
                            sp.dma_start(scr["slot_out"][b, s, k],
                                         slT[:, s % HB, k, :].rearrange("p (e j) -> p e j", e=2)).then_inc(s_out, 16)

                def load_y(b, c, first):
                    if not (first and c < 2):
                        sp.wait_ge(y_split, b * CPB + c - 1)
                    sp.dma_start(y[:, c % 2], scr["y_in"][b, c]).then_inc(y_in[c], 16)

                def batch(b, first):
                    for c in range(CPB):
                        if not (first and c < 2):
                            sp.wait_ge(yT_split, b * CPB + c - 1)
                        sp.dma_start(yT[:, c % 2], scr["yT_in"][b, c]).then_inc(yT_in[c], 16)
                    if not first:
                        slots_out(b - 1)
                    load_y(b, 0, first)
                    load_y(b, 1, first)
                    for t in range(TPB):
                        sp.wait_ge(e1_ready, b * TPB + t + 1)
                        sp.dma_start(scr["e1"][b, t], e1[:, t % 2]).then_inc(e_out[t % 2], 16)
                        if t in (3, 6):
                            load_y(b, 2 + t // 6, first)
                    sp.dma_start(scr["zr"][b], zr[:, :]).then_inc(z_out, 16)

                batch(0, True)
                with sp.Fori(1, B) as b:
                    batch(b, False)
                slots_out(B - 1)
                sp.wait_ge(e_out0, 16 * (B * TPB // 2 + 1))
                sp.wait_ge(e_out1, 16 * (B * TPB // 2 + 1))
                sp.wait_ge(z_out, 16 * (B + 1))
                sp.wait_ge(s_out, 16 * 2 * SB * (B + 1))

            @block.scalar
            def _(act):
                with act.Fori(0, B) as b:
                    for t in range(TPB + 1):
                        if t < TPB:
                            act.wait_ge(lp_ready, b * TPB + t + 1)
                            act.wait_ge(dl_ready, 2 * TPB * b + t + 1)
                            nc.scalar.copy(lg[:, t, :], lp[:, 2 * (t % 2):2 * (t % 2) + 2, :]
                                           .rearrange("p a n -> p (a n)")).then_inc(lg_ready, 1)
                        if t > 0:
                            u = t - 1
                            act.wait_ge(nr_ready, b * TPB + u + 1)
                            if u == 0:
                                act.wait_ge(z_out, 16 * b + 16)
                            act.wait_ge(e_out[u % 2], 16 * (b * TPB // 2 + u // 2) + 16)
                            nc.scalar.activation(e1[:, u % 2], lg[:, u, :], ACT.Exp, bias=nr[:, u:u + 1],
                                                 accum_out=zr[:, u:u + 1]).then_inc(e1_ready, 1)
                    for n in range(2 * TPB + 1):
                        if n < 2 * TPB:
                            hf, t = divmod(n, TPB)
                            act.wait_ge(sub_v if t % 2 else sub_p, (b + 1) * TPB + hf * (TPB // 2) + t // 2 + 1)
                            cols = lg[:, t, hf * 512:(hf + 1) * 512]
                            nc.scalar.activation(cols, cols, ACT.Exp).then_inc(d_ready, 1)
                        if n > 0:
                            m = n - 1
                            hf, t = divmod(m, TPB)
                            act.wait_ge(d_ready, 2 * TPB * b + m + 1)
                            act.wait_ge(d_free, 2 * TPB * b + 3 + max(m - ND, -1))
                            nc.scalar.copy(dh[:, m % ND], lg[:, t, hf * 512:(hf + 1) * 512]).then_inc(dh_ready, 1)
                    for s in range(SB):
                        act.wait_ge(slT_ready, b * SB + s + 1)
                        if s == 0:
                            act.wait_ge(s_out, 16 * 2 * SB * b + 16 * 2 * SB)
                        if s == HB:
                            act.wait_ge(s_out, 16 * 2 * SB * b + 16 * 2 * (SB + HB))
                        for k in range(DK):
                            nc.scalar.activation(slT[:, s % HB, k, :], bank(s)[:, k * P:(k + 1) * P], ACT.Identity,
                                                 scale=w["gbT"][:, k:k + 1],
                                                 bias=w["gbT"][:, DK + k:DK + k + 1]).then_inc(slT_kept, 1)

            @block.vector
            def _(dve):
                nc.vector.memset(cm[:, 0:2 * TPB], 0.0).then_inc(ones_set, 1)
                dve.wait_ge(ones_set, 1)
                zeros = cm[:, 0:2 * TPB].rearrange("p (t o) -> p t o", o=2)
                nc.vector.tensor_copy(yl[:, :, D:D + 2], zeros).then_inc(ones_set, 1)
                nc.vector.tensor_copy(yh[:, :, D:D + 2], zeros).then_inc(ones_set, 1)
                dve.wait_ge(ones_set, 3)
                nc.vector.tensor_scalar(yh[:, :, D:D + 1], zeros[:, :, 0:1], 1.0, None, ALU.add).then_inc(ones_set, 1)
                dve.wait_ge(ones_set, 4)

                def less_max(b, hf, t):
                    h = slice(hf * 512, (hf + 1) * 512)
                    dve.wait_ge(ca_ready, 2 * b + hf + 3)
                    dve.wait_ge(e1_ready, b * TPB + t + 1)
                    nc.vector.tensor_tensor(lg[:, t, h], lg[:, t, h], ca[:, h], ALU.subtract).then_inc(sub_v, 1)

                def low(b, m):
                    hf, t = divmod(m, TPB)
                    dve.wait_ge(dh_ready, 2 * TPB * b + m + 1)
                    dve.wait_ge(d_free, 2 * TPB * b + 3 + max(m - ND, -1))
                    nc.vector.tensor_tensor(dl[:, m % ND], lg[:, t, hf * 512:(hf + 1) * 512],
                                            dh[:, m % ND].bitcast(F32), ALU.subtract).then_inc(dl_ready, 1)

                def slots(b, hf):
                    for s in range(hf * HB, (hf + 1) * HB):
                        if s < HB:
                            dve.wait_ge(d_free, 2 * TPB * b + TPB + 2)
                        else:
                            dve.wait_ge(d_free, 2 * TPB * b + 2 * TPB + 2)
                        nc.vector.reciprocal(rz[:, s:s + 1], bank(s)[:, D:D + 1]).then_inc(rz_ready, 1)
                        dve.wait_ge(rz_ready, b * SB + s + 1)
                        if s >= HB:
                            dve.wait_ge(slT_ready, b * SB + s - HB + 1)
                        nc.vector.tensor_scalar(sl[:, s % HB, :], bank(s)[:, 0:D], rz[:, s:s + 1], None,
                                                ALU.mult).then_inc(sl_ready, 1)

                with dve.Fori(0, B) as b:
                    for t in range(TPB):
                        dve.wait_ge(lg_ready, b * TPB + t + 3)
                        if t == 0:
                            dve.wait_ge(ca_ready, 2 * b + 2)
                        nc.vector.tensor_reduce(nr[:, t:t + 1], lg[:, t, :], AX.X, ALU.max,
                                                negate=True).then_inc(nr_ready, 1)
                        if t == 0:
                            nc.vector.tensor_copy(cm[:], lg[:, t, :]).then_inc(cm_done, 1)
                        else:
                            dve.wait_ge(cm_done, b * TPB + t)
                            nc.vector.tensor_tensor(cm[:], cm[:], lg[:, t, :], ALU.max).then_inc(cm_done, 1)
                    less_max(b, 0, 1)
                    less_max(b, 0, 3)
                    for m in range(2 * TPB):
                        low(b, m)
                        if 2 * m + 5 < TPB:
                            less_max(b, 0, 2 * m + 5)
                        if TPB // 2 <= m < TPB:
                            less_max(b, 1, 2 * (m - TPB // 2) + 1)
                        if m == TPB + 1:
                            slots(b, 0)
                    slots(b, 1)

            @block.gpsimd
            def _(pool):
                with pool.Fori(0, B) as b:
                    pool.wait_ge(lg_ready, b * TPB + 2)
                    for c in range(CPB):
                        wait_apart(pool, yT_in[c], 16 * b + 16, passed)
                        nc.gpsimd.tensor_copy(yTh[:, c], yT[:, c % 2]).then_inc(yT_high, 1)
                        pool.wait_ge(yT_high, b * CPB + c + 1)
                        nc.gpsimd.tensor_tensor(yTl[:, c], yT[:, c % 2], yTh[:, c].bitcast(F32),
                                                ALU.subtract).then_inc(yT_split, 1)
                    pool.wait_ge(d_free, 2 * TPB * b + 2)
                    for c in range(CPB):
                        r = slice(c * TPC, (c + 1) * TPC)
                        wait_apart(pool, y_in[c], 16 * b + 16, passed)
                        nc.gpsimd.tensor_copy(yh[:, r, 0:D], y[:, c % 2]).then_inc(y_high, 1)
                        pool.wait_ge(y_high, b * CPB + c + 1)
                        nc.gpsimd.tensor_tensor(yl[:, r, 0:D], y[:, c % 2], yh[:, r, 0:D].bitcast(F32),
                                                ALU.subtract).then_inc(y_split, 1)
                    pool.wait_ge(sub_v, (b + 1) * TPB)
                    for hf in range(2):
                        h = slice(hf * 512, (hf + 1) * 512)
                        pool.wait_ge(sub_p, (b + 1) * TPB + hf * (TPB // 2))
                        wait_apart(pool, cm_done, b * TPB + TPB, passed)
                        nc.gpsimd.partition_all_reduce(ca[:, h], cm[:, h], P, RMAX).then_inc(ca_ready, 1)
                        pool.wait_ge(ca_ready, 2 * b + hf + 3)
                        for t in range(0, TPB, 2):
                            pool.wait_ge(e1_ready, b * TPB + t + 1)
                            nc.gpsimd.tensor_tensor(lg[:, t, h], lg[:, t, h], ca[:, h],
                                                    ALU.subtract).then_inc(sub_p, 1)

            @block.tensor
            def _(pe):
                pe.wait_ge(ones_set, 4)
                with pe.Fori(0, B) as b:
                    pe.wait_ge(slT_kept, DK * (b * SB + HB))
                    for t in range(TPB):
                        if t % TPC == 0:
                            pe.wait_ge(yT_split, b * CPB + t // TPC + 1)
                        pe.wait_ge(lg_ready, b * TPB + t + 1)
                        for h in range(2):
                            for k in range(DK):
                                for lhs, rhs in ((yTh, "seTh"), (yTh, "seTl"), (yTl, "seTh")):
                                    last = nc.tensor.matmul(lp[:, 2 * (t % 2) + h, :],
                                                            lhs[:, t // TPC, k, (t % TPC) * P:(t % TPC + 1) * P],
                                                            w[rhs][:, k, h * 512:(h + 1) * 512],
                                                            start=(k == 0 and lhs is yTh and rhs == "seTh"),
                                                            stop=(k == DK - 1 and lhs is yTl))
                        last.then_inc(lp_ready, 1)
                    pe.wait_ge(lg_ready, b * TPB + TPB + 2)
                    pe.wait_ge(slT_kept, DK * (b * SB + SB))
                    pe.wait_ge(y_split, CPB * b + CPB)

                    def turn(hf):
                        for s in range(hf * HB, (hf + 1) * HB):
                            pe.wait_ge(sl_ready, b * SB + s + 1)
                            for k in range(DK):
                                last = nc.tensor.transpose(bank(s)[:, k * P:(k + 1) * P], sl[:, s % HB, k * P:(k + 1) * P],
                                                           w["ident"][:])
                            last.then_inc(slT_ready, 1)

                    for hf in range(2):
                        for t in range(TPB):
                            if hf and t == 5:
                                turn(0)
                            pe.wait_ge(dl_ready, (2 * b + hf) * TPB + t + 1 + TPB)
                            for s in range(HB):
                                for lhs, rhs in ((dh, yh), (dh, yl), (dl, yh)):
                                    last = nc.tensor.matmul(bank(hf * HB + s)[:, 0:D + 2],
                                                            lhs[:, (hf * TPB + t) % ND, s * P:(s + 1) * P], rhs[:, t, :],
                                                            start=(t == 0 and lhs is dh and rhs is yh),
                                                            stop=(t == TPB - 1 and lhs is dl))
                            last.then_inc(d_free, 1)
                    turn(1)


def experts(nc, w, io, scr):
    FB = F // P
    RB = B * SL // P
    with ExitStack() as ctx:
        a = Alloc(nc, ctx, "exp")
        wg, wu = a.sb("wg", [P, 2, DK, F]), a.sb("wu", [P, 2, DK, F])
        wd = a.sb("wd", [P, 2, FB, D])
        sl = a.sb("sl", [P, 2, DK, B * SL])
        wgh, wgl = a.sb("wgh", [P, 2, DK, F], F32R), a.sb("wgl", [P, 2, DK, F], F32R)
        wuh, wul = a.sb("wuh", [P, 2, DK, F], F32R), a.sb("wul", [P, 2, DK, F], F32R)
        slh, sll = a.sb("slh", [P, 2, DK, B * SL], F32R), a.sb("sll", [P, 2, DK, B * SL], F32R)
        passed = a.sem("passed")
        w_high, up_split, sl_high, gate_split = (a.sem(n) for n in ("w_high", "up_split", "sl_high",
                                                                 "gate_split"))
        bd = a.sb("bd", [P, 2, D])
        bg, bu = a.sb("bg", [P, 2, FB]), a.sb("bu", [P, 2, FB])
        gate = a.sb("gate", [P, 2, FB, B * SL])
        h = a.sb("h", [P, 2, FB, B * SL])
        eo = a.sb("eo", [P, 2, RB, D])
        gp = a.ps("gp", [P, FB, B * SL])
        up = a.ps("up", [P, FB, B * SL])
        op = a.ps("op", [P, 2, RB, D])
        sem = a.sem
        gu_in = [sem(f"gu_in{q}") for q in range(2)]
        down_in = [sem(f"down_in{q}") for q in range(2)]
        out = [sem(f"out{q}") for q in range(2)]
        bias_ready, gu_ready, gate_ready, h_ready, o_ready, eo_ready = (
            sem(n) for n in ("bias_ready", "gu_ready", "gate_ready", "h_ready", "o_ready", "eo_ready"))
        NGU, NDN = 3, 2
        credits = [(gu_ready, 2), (gate_ready, FB), (h_ready, FB), (o_ready, 2), (eo_ready, 2 * RB),
                   (out[0], 16 * B), (out[1], 16 * B)]

        with nc.Block() as block:
            @block.sync
            def _(sp):
                for s, n in credits:
                    sp.sem_inc(s, n)

                def load_gu(e, q):
                    if not isinstance(e, int) or e >= 2:
                        sp.wait_ge(up_split, e - 1)
                        sp.wait_ge(gate_split, 2 * e - 2)
                    for dst, src in ((sl[:, q], scr["slot_in"][e]), (wg[:, q], io["Wg"][e]), (wu[:, q], io["Wu"][e])):
                        sp.dma_start(dst, src).then_inc(gu_in[q], 16)

                def load_down(e, q):
                    sp.wait_ge(o_ready, e + 1)
                    sp.wait_ge(eo_ready, RB * (e + 1))
                    for dst, src in ((wd[:, q], io["Wd"][e]), (bd[:, q], io["bd"][e].partition_broadcast(P))):
                        sp.dma_start(dst, src).then_inc(down_in[q], 16)

                def store(e, q):
                    sp.wait_ge(eo_ready, RB * (e + 3))
                    for b in range(B):
                        r = slice(SL * (b % 2), SL * (b % 2) + SL)
                        sp.dma_start(scr["eo_out"][e, b], eo[r, q, b // 2, :]).then_inc(out[q], 16)

                sp_first = ((sl[:, 0], scr["slot_in"][0]), (wg[:, 0], io["Wg"][0]), (wu[:, 0], io["Wu"][0]))
                for dst, src in sp_first:
                    sp.dma_start(dst, src).then_inc(gu_in[0], 16)
                load_gu(1, 1)
                load_down(0, 0)
                load_gu(2, 0)
                load_down(1, 1)
                with sp.Fori(1, E // 2 - 1) as j:
                    for q in range(2):
                        e = 2 * j + q
                        load_gu(e + 1, 1 - q)
                        store(e - 2, q)
                        load_down(e, q)
                load_gu(E - 1, 1)
                store(E - 4, 0)
                load_down(E - 2, 0)
                store(E - 3, 1)
                load_down(E - 1, 1)
                store(E - 2, 0)
                store(E - 1, 1)
                for q in range(2):
                    sp.wait_ge(out[q], 16 * B * (E // 2 + 1))

            @block.scalar
            def _(act):
                def gates(e, q):
                    act.wait_ge(bias_ready, 2 * e + 1)
                    for f in range(FB):
                        act.wait_ge(gu_ready, 2 * e + f // 2 + 3)
                        nc.scalar.activation(gate[:, q, f, :], gp[:, f, :], ACT.Gelu,
                                             bias=bg[:, q, f:f + 1]).then_inc(gate_ready, 1)

                with act.Fori(0, E // 2) as j:
                    for q in range(2):
                        gates(2 * j + q, q)

            @block.gpsimd
            def _(pool):
                def low(e, j, q):
                    pool.wait_ge(gu_ready, 2 * e) if not isinstance(e, int) or e > 0 else None
                    wait_apart(pool, gu_in[q], 16 * NGU * j + 16 * NGU, passed)
                    nc.gpsimd.tensor_copy(slh[:, q], sl[:, q]).then_inc(sl_high, 1)
                    pool.wait_ge(sl_high, e + 1)
                    nc.gpsimd.tensor_tensor(sll[:, q], sl[:, q], slh[:, q].bitcast(F32),
                                            ALU.subtract).then_inc(gate_split, 1)
                    pool.wait_ge(w_high, 2 * e + 1)
                    nc.gpsimd.tensor_tensor(wgl[:, q], wg[:, q], wgh[:, q].bitcast(F32),
                                            ALU.subtract).then_inc(gate_split, 1)

                with pool.Fori(0, E // 2) as j:
                    for q in range(2):
                        low(2 * j + q, j, q)

            @block.vector
            def _(dve):
                def hidden(e, q):
                    nc.vector.tensor_copy(bg[:, q, :], w["bgT"][:, :, bass.ds(e, 1)].rearrange("p f o -> p (f o)")
                                          ).then_inc(bias_ready, 1)
                    nc.vector.tensor_copy(bu[:, q, :], w["buT"][:, :, bass.ds(e, 1)].rearrange("p f o -> p (f o)")
                                          ).then_inc(bias_ready, 1)
                    dve.wait_ge(bias_ready, 2 * e + 2)
                    dve.wait_ge(o_ready, e + 1)
                    for f in range(FB):
                        dve.wait_ge(gate_ready, FB * e + FB + f + 1)
                        dve.wait_ge(gu_ready, 2 * e + f // 2 + 3)
                        nc.vector.scalar_tensor_tensor(out=h[:, q, f, :], in0=up[:, f, :], scalar=bu[:, q, f:f + 1],
                                                       in1=gate[:, q, f, :], op0=ALU.add,
                                                       op1=ALU.mult).then_inc(h_ready, 1)

                def output(e, j, q):
                    dve.wait_ge(o_ready, e + 3)
                    dve.wait_ge(down_in[q], 16 * NDN * j + 16 * NDN)
                    dve.wait_ge(out[q], 16 * B * j + 16 * B)
                    for r in range(RB):
                        nc.vector.tensor_tensor(eo[:, q, r, :], op[:, q, r, :], bd[:, q, :],
                                                ALU.add).then_inc(eo_ready, 1)

                def parts(e, j, q):
                    dve.wait_ge(gu_in[q], 16 * NGU * j + 16 * NGU)
                    dve.wait_ge(gu_ready, 2 * e) if not isinstance(e, int) or e > 0 else None
                    nc.vector.tensor_copy(wgh[:, q], wg[:, q]).then_inc(w_high, 1)
                    nc.vector.tensor_copy(wuh[:, q], wu[:, q]).then_inc(w_high, 1)
                    dve.wait_ge(w_high, 2 * e + 2)
                    nc.vector.tensor_tensor(wul[:, q], wu[:, q], wuh[:, q].bitcast(F32),
                                            ALU.subtract).then_inc(up_split, 1)

                parts(0, 0, 0)
                parts(1, 0, 1)
                hidden(0, 0)
                with dve.Fori(0, E // 2 - 1) as j:
                    parts(2 * j + 2, j + 1, 0)
                    hidden(2 * j + 1, 1)
                    output(2 * j, j, 0)
                    parts(2 * j + 3, j + 1, 1)
                    hidden(2 * j + 2, 0)
                    output(2 * j + 1, j, 1)
                hidden(E - 1, 1)
                output(E - 2, E // 2 - 1, 0)
                output(E - 1, E // 2 - 1, 1)

            @block.tensor
            def _(pe):
                def gate_up(e, j, q):
                    pe.wait_ge(up_split, e + 1)
                    pe.wait_ge(gate_split, 2 * e + 2)
                    for half in range(FB // 2):
                        pe.wait_ge(gate_ready, FB * e + 2 * half + 2)
                        pe.wait_ge(h_ready, FB * e + 2 * half + 2)
                        for f in (2 * half, 2 * half + 1):
                            for dst, wh, wl in ((gp, wgh, wgl), (up, wuh, wul)):
                                for k in range(DK):
                                    for lhs, rhs in ((wh, slh), (wh, sll), (wl, slh)):
                                        last = nc.tensor.matmul(dst[:, f, :], lhs[:, q, k, f * P:(f + 1) * P],
                                                                rhs[:, q, k, :],
                                                                start=(k == 0 and lhs is wh and rhs is slh),
                                                                stop=(k == DK - 1 and lhs is wl))
                        last.then_inc(gu_ready, 1)

                def down(e, j, q):
                    pe.wait_ge(down_in[q], 16 * NDN * j + 16 * NDN)
                    pe.wait_ge(h_ready, FB * e + 2 * FB)
                    pe.wait_ge(eo_ready, RB * (e + 1))
                    for r in range(RB):
                        for f in range(FB):
                            last = nc.tensor.matmul(op[:, q, r, :], h[:, q, f, r * P:(r + 1) * P], wd[:, q, f, :],
                                                    start=(f == 0), stop=(f == FB - 1))
                    last.then_inc(o_ready, 1)

                gate_up(0, 0, 0)
                with pe.Fori(0, E // 2 - 1) as j:
                    gate_up(2 * j + 1, j, 1)
                    down(2 * j, j, 0)
                    gate_up(2 * j + 2, j + 1, 0)
                    down(2 * j + 1, j, 1)
                gate_up(E - 1, E // 2 - 1, 1)
                down(E - 2, E // 2 - 1, 0)
                down(E - 1, E // 2 - 1, 1)


def combine(nc, w, io, scr):
    NB = 4
    with ExitStack() as ctx:
        a = Alloc(nc, ctx, "com")
        eo = a.sb("eo", [P, B, SB, D])
        eoh, eol = a.sb("eoh", [P, B, SB, D], F32R), a.sb("eol", [P, B, SB, D], F32R)
        woh, wol = a.sb("woh", [P, DK, D], F32R), a.sb("wol", [P, DK, D], F32R)
        e1 = a.sb("e1", [P, NB, NS])
        c = a.sb("c", [P, NB, D])
        x = a.sb("x", [P, NB, D])
        e1h, e1l = a.sb("e1h", [P, 2, SB, P], F32R), a.sb("e1l", [P, 2, SB, P], F32R)
        ch, cl = a.sb("ch", [P, 2, DK, P], F32R), a.sb("cl", [P, 2, DK, P], F32R)
        zr, rz = a.sb("zr", [P, TPB]), a.sb("rz", [P, TPB])
        part = a.sb("part", [P, 2, D])
        o = a.sb("o", [P, 2, D])
        tp = a.ps("tp", [P, 2, 3, 512])
        mp = a.ps("mp", [P, 2, 512])
        sem = a.sem
        in_ = [sem(f"in{q}") for q in range(NB)]
        x_in = [sem(f"x_in{q}") for q in range(NB)]
        out = [sem(f"out{q}") for q in range(2)]
        (z_in, turned, e1h_kept, e1l_kept, ch_kept, cl_kept, m_ready, rz_ready, part_ready, o_ready,
         wo_high, wo_split, eo_high, eo_split) = (
            sem(n) for n in ("z_in", "turned", "e1h_kept", "e1l_kept", "ch_kept", "cl_kept", "m_ready", "rz_ready",
                             "part_ready", "o_ready", "wo_high", "wo_split", "eo_high", "eo_split"))
        eo_in = [sem(f"eo_in{b}") for b in range(B)]
        credits = [(turned, NB), (e1l_kept, 2), (cl_kept, 2), (m_ready, 2), (o_ready, NB), (rz_ready, 1),
                   (out[0], 16), (out[1], 16)]
        H2 = TPB // 2
        with nc.Block() as block:
            @block.sync
            def _(sp):
                for s, n in credits:
                    sp.sem_inc(s, n)
                with sp.Fori(0, B) as b:
                    for t in range(TPB):
                        q = t % NB
                        n = b * TPB + t
                        sp.wait_ge(turned, n + 1)
                        sp.dma_start(e1[:, q], scr["e1"][b, t]).then_inc(in_[q], 16)
                        sp.dma_start(c[:, q], scr["ctx_in"][b, t]).then_inc(in_[q], 16)
                        sp.wait_ge(o_ready, n + 1)
                        sp.dma_start(x[:, q], io["x_tile"][b, t]).then_inc(x_in[q], 16)
                        if t == 0:
                            sp.wait_ge(rz_ready, b + 1)
                            sp.dma_start(zr[:], scr["zr"][b]).then_inc(z_in, 16)

            @block.scalar
            def _(act):
                def store(b, t):
                    act.wait_ge(o_ready, b * TPB + t + 1 + NB)
                    act.dma_start(io["out_tile"][b, t], o[:, t % 2]).then_inc(out[t % 2], 16)

                act.dma_start(eo[:, 0], scr["eo_in"][0]).then_inc(eo_in[0], 16)
                act.wait_ge(turned, NB + 1)
                for b in range(1, B):
                    act.dma_start(eo[:, b], scr["eo_in"][b]).then_inc(eo_in[b], 16)
                with act.Fori(0, B) as b:
                    for t in range(TPB):
                        q = t % 2
                        n = b * TPB + t
                        act.wait_ge(turned, n + 1 + NB)
                        act.wait_ge(m_ready, n + 1)
                        nc.scalar.copy(e1h[:, q].rearrange("p s n -> p (s n)"),
                                       tp[:, q, 0:2, :].rearrange("p a n -> p (a n)")).then_inc(e1h_kept, 1)
                        if t > 1:
                            store(b, t - 2)
                    for t in (TPB - 2, TPB - 1):
                        store(b, t)
                for q in range(2):
                    act.wait_ge(out[q], 16 * (B * H2 + 1))

            @block.vector
            def _(dve):
                with dve.Fori(0, B) as b:
                    for t in range(TPB + 1):
                        n = b * TPB + t
                        if t < TPB:
                            q = t % 2
                            dve.wait_ge(turned, n + 1 + NB)
                            dve.wait_ge(m_ready, n + 1)
                            nc.vector.tensor_copy(ch[:, q].rearrange("p k n -> p (k n)"),
                                                  tp[:, q, 2, 0:D]).then_inc(ch_kept, 1)
                            dve.wait_ge(ch_kept, n + 1)
                            nc.vector.tensor_tensor(cl[:, q].rearrange("p k n -> p (k n)"), tp[:, q, 2, 0:D],
                                                    ch[:, q].rearrange("p k n -> p (k n)").bitcast(F32),
                                                    ALU.subtract).then_inc(cl_kept, 1)
                            dve.wait_ge(e1h_kept, n + 1)
                            nc.vector.tensor_tensor(e1l[:, q].rearrange("p s n -> p (s n)"),
                                                    tp[:, q, 0:2, :].rearrange("p a n -> p (a n)"),
                                                    e1h[:, q].rearrange("p s n -> p (s n)").bitcast(F32),
                                                    ALU.subtract).then_inc(e1l_kept, 1)
                        if t == 0:
                            dve.wait_ge(z_in, 16 * b + 16)
                            nc.vector.reciprocal(rz[:], zr[:]).then_inc(rz_ready, 1)
                            dve.wait_ge(rz_ready, b + 2)
                        if t > 0:
                            u, q = t - 1, (t - 1) % 2
                            n = b * TPB + u
                            dve.wait_ge(m_ready, n + 3)
                            dve.wait_ge(x_in[u % NB], 16 * (b * (TPB // NB) + u // NB) + 16)
                            nc.vector.scalar_tensor_tensor(out=part[:, q, :], in0=mp[:, q, 0:D],
                                                           scalar=rz[:, u:u + 1], in1=x[:, u % NB, :], op0=ALU.mult,
                                                           op1=ALU.add).then_inc(part_ready, 1)
                            dve.wait_ge(part_ready, n + 1)
                            dve.wait_ge(out[q], 16 * (b * H2 + u // 2) + 16)
                            nc.vector.tensor_tensor(o[:, q, :], part[:, q, :], mp[:, q, D:2 * D],
                                                    ALU.add).then_inc(o_ready, 1)

            @block.gpsimd
            def _(pool):
                nc.gpsimd.tensor_copy(woh[:], w["woT"][:]).then_inc(wo_high, 1)
                pool.wait_ge(wo_high, 1)
                nc.gpsimd.tensor_tensor(wol[:], w["woT"][:], woh[:].bitcast(F32), ALU.subtract).then_inc(wo_split, 1)
                for b in range(B):
                    pool.wait_ge(eo_in[b], 16)
                    nc.gpsimd.tensor_copy(eoh[:, b], eo[:, b]).then_inc(eo_high, 1)
                    pool.wait_ge(eo_high, b + 1)
                    nc.gpsimd.tensor_tensor(eol[:, b], eo[:, b], eoh[:, b].bitcast(F32),
                                            ALU.subtract).then_inc(eo_split, 1)

            @block.tensor
            def _(pe):
                pe.wait_ge(wo_split, 1)
                with pe.Fori(0, B) as b:
                    for t in range(TPB + 1):
                        if t < TPB:
                            q = t % 2
                            n = b * TPB + t
                            pe.wait_ge(in_[t % NB], 32 * (b * (TPB // NB) + t // NB) + 32)
                            pe.wait_ge(e1l_kept, n + 1)
                            pe.wait_ge(cl_kept, n + 1)
                            for s in range(SB):
                                nc.tensor.transpose(tp[:, q, s // 4, (s % 4) * P:(s % 4 + 1) * P],
                                                    e1[:, t % NB, s * P:(s + 1) * P], w["ident"][:])
                            for k in range(DK):
                                last = nc.tensor.transpose(tp[:, q, 2, k * P:(k + 1) * P], c[:, t % NB, k * P:(k + 1) * P],
                                                           w["ident"][:])
                            last.then_inc(turned, 1)
                        if t > 0:
                            u, q = t - 1, (t - 1) % 2
                            n = b * TPB + u
                            if u == 0:
                                pe.wait_ge(eo_split, b + 1)
                            pe.wait_ge(o_ready, n - 1 + NB)
                            pe.wait_ge(cl_kept, n + 3)
                            for k in range(DK):
                                for lhs, rhs in ((ch, woh), (ch, wol), (cl, woh)):
                                    nc.tensor.matmul(mp[:, q, D:2 * D], lhs[:, q, k, :], rhs[:, k, :],
                                                     start=(k == 0 and rhs is woh and lhs is ch),
                                                     stop=(k == DK - 1 and lhs is cl))
                            pe.wait_ge(e1l_kept, n + 3)
                            for s in range(SB):
                                for lhs, rhs in ((e1h, eoh), (e1h, eol), (e1l, eoh)):
                                    last = nc.tensor.matmul(mp[:, q, 0:D], lhs[:, q, s, :], rhs[:, b, s, :],
                                                            start=(s == 0 and rhs is eoh and lhs is e1h),
                                                            stop=(s == SB - 1 and lhs is e1l))
                            last.then_inc(m_ready, 1)


def block_kernel(nc, x, wq, wk, wv, wo, norm_g, norm_b, slot_g, slot_b, scale, slot_embeds,
                 Wg, bg, Wu, bu, Wd, bd, out):
    def dram(name, shape, dt=F32):
        return nc.dram_tensor(name, shape, dt, kind="Internal").ap()

    q_d = dram("q_parts", [3, NCH, D, CH], BF16)
    k_d = dram("k_parts", [3, NKV * HD, TOK], BF16)
    v_d = dram("v_rows", [NCH, P, NKV, TPC * VW])
    y_d = dram("y_rows", [NCH, P, TPC, D])
    yT_d = dram("y_cols", [NCH, P, DK, CH])
    c_d = dram("context", [B, S, D])
    e_d = dram("slot_exps", [B, TPB, P, NS])
    z_d = dram("slot_sums", [B, P, TPB])
    s_d = dram("slots", [E, P, DK, B * SL])
    o_d = dram("expert_out", [B, NS, D])
    io = {
        "x": x.rearrange("b (c t p) d -> (b c) p t d", p=P, t=TPC),
        "x_tile": x.rearrange("b (n p) d -> b n p d", p=P),
        "out_tile": out.rearrange("b (n p) d -> b n p d", p=P),
        "wq": wq, "wk": wk, "wv": wv, "wo": wo, "norm_g": norm_g, "norm_b": norm_b, "slot_g": slot_g,
        "slot_b": slot_b, "scale": scale, "slot_embeds": slot_embeds, "bg": bg, "bu": bu, "bd": bd,
        "Wg": Wg.rearrange("e (k p) f -> e p k f", p=P), "Wu": Wu.rearrange("e (k p) f -> e p k f", p=P),
        "Wd": Wd.rearrange("e (k p) o -> e p k o", p=P),
    }
    scr = {
        "q_out": q_d.rearrange("a i (m p) t -> i m p a t", p=P),
        "q_in": q_d.rearrange("a (b c) (g d h) t -> b a g d c (h t)", g=NKV, h=GS, b=B),
        "k_out": k_d.rearrange("a p (i t) -> i p a t", t=CH),
        "k_in": k_d.rearrange("a (g d) (b s) -> b a g d s", g=NKV, b=B),
        "v_out": v_d.rearrange("i p g x -> i p (g x)"),
        "v_in": v_d.rearrange("(b c) p g x -> b p g c x", b=B),
        "y": y_d, "y_in": y_d.rearrange("(b c) p t d -> b c p t d", b=B),
        "yT_out": yT_d, "yT_in": yT_d.rearrange("(b c) p k t -> b c p k t", b=B),
        "ctx_out": c_d.rearrange("b (c t p) d -> b c p t d", p=P, t=TPC),
        "ctx_in": c_d.rearrange("b (n p) d -> b n p d", p=P),
        "e1": e_d, "zr": z_d,
        "slot_out": s_d.rearrange("(s e) p k (b j) -> b s k p e j", e=2, b=B),
        "slot_in": s_d,
        "eo_out": o_d.rearrange("b (e j) d -> e b j d", e=E),
        "eo_in": o_d.rearrange("b (s p) d -> b p s d", p=P),
    }
    with ExitStack() as ctx:
        a = Alloc(nc, ctx, "w")
        w = {
            "ident": a.sb("ident", [P, P]), "identb": a.sb("identb", [P, P], BF16), "causal": a.sb("causal", [P, CH]),
            "wqT": a.sb("wqT", [P, DK, D]), "wkvT": a.sb("wkvT", [P, DK, P]), "woT": a.sb("woT", [P, DK, D]),
            "seTh": a.sb("seTh", [P, DK, NS], F32R), "seTl": a.sb("seTl", [P, DK, NS], F32R),
            "bgT": a.sb("bgT", [P, F // P, E]), "buT": a.sb("buT", [P, F // P, E]),
            "power": a.sb("power", [P, SB]), "gbT": a.sb("gbT", [P, 2 * DK]),
        }
        prepare(nc, w, io)
        project(nc, w, io, scr)
        attend(nc, w, scr)
        dispatch(nc, w, scr)
        experts(nc, w, io, scr)
        combine(nc, w, io, scr)


_INS = ['L0_attn_x', 'L0_attn_wq', 'L0_attn_wk', 'L0_attn_wv', 'L0_attn_wo', 'L0_ffn_norm_g', 'L0_ffn_norm_b',
        'L0_ffn_slot_g', 'L0_ffn_slot_b', 'L0_ffn_scale', 'L0_ffn_slot_embeds', 'L0_ffn_Wg', 'L0_ffn_bg',
        'L0_ffn_Wu', 'L0_ffn_bu', 'L0_ffn_Wd', 'L0_ffn_bd']
_OUTS = [((B, S, D), 'float32')]


def kernel(**inputs):
    import numpy as _np
    import concourse.bacc as _bacc
    from concourse import mybir as _mybir
    from concourse.bass_utils import run_bass_kernel_spmd as _run

    nc = _bacc.Bacc("TRN2", target_bir_lowering=False, num_devices=1)
    arrays, args = {}, []
    for name in _INS:
        a = _np.ascontiguousarray(inputs[name])
        arrays[f"in_{name}_dram"] = a
        args.append(nc.dram_tensor(f"in_{name}_dram", a.shape, _mybir.dt.from_np(a.dtype), kind="ExternalInput").ap())
    for i, (shape, dtype) in enumerate(_OUTS):
        dt = _mybir.dt.from_np(_np.dtype(dtype))
        args.append(nc.dram_tensor(f"out_{i}_dram", shape, dt, kind="ExternalOutput").ap())
    block_kernel(nc, *args)
    r = _run(nc, [arrays], core_ids=[0])
    got = tuple(r.results[0][f"out_{i}_dram"] for i in range(len(_OUTS)))
    return got[0]
```
